# Optimizing a Trainium2 kernel written in Bass

```python
import numpy as np
import jax
import jax.numpy as jnp

def _softmax(x, axis=-1):
    return jax.nn.softmax(x, axis=axis)

def _gelu(x):
    return jax.nn.gelu(x, approximate=True)

def _silu(x):
    return jax.nn.silu(x)

def _sigmoid(x):
    return jax.nn.sigmoid(x)

def _layernorm(x, axis=-1, eps=1e-05):
    m = jnp.mean(x, axis=axis, keepdims=True)
    v = jnp.var(x, axis=axis, keepdims=True)
    return (x - m) / jnp.sqrt(v + eps)

def _scatter_add(tgt, idx, src, axis=0):
    return tgt.at[idx].add(src)

def _segment_sum(src, seg, n):
    return jax.ops.segment_sum(src, seg, n)
kernel_name = 'mk_adj_seq_d2_adj_r2_020cd6'

def setup_inputs(seed: int=0):
    np.random.seed(seed)
    _w = jnp.asarray

    def _rec_inputs():
        import jax
        import jax.numpy as jnp
        _gk = jax.random.key(seed)
        x = -0.0005207 + 1.001 * jax.random.normal(jax.random.fold_in(_gk, 1), (64, 128, 256), jnp.float32)
        _a = jax.random.bernoulli(jax.random.fold_in(_gk, 2), 0.125, (64, 128, 128))
        _a = jnp.logical_or(_a, jnp.eye(128, dtype=bool))
        adj = _a.astype(jnp.int32)
        return (x, adj)
    x, adj = _rec_inputs()

    def _L0_gnn_setup():
        import jax, jax.numpy as jnp
        import numpy as np
        B, S, D, H = (2, 1024, 256, 8)
        HD = D // H
        EPS = 1e-05

        def _ln(x, g, b):
            mu = jnp.mean(x, axis=-1, keepdims=True)
            var = jnp.mean((x - mu) ** 2, axis=-1, keepdims=True)
            return (x - mu) * jax.lax.rsqrt(var + EPS) * g + b
        key = jax.random.key(seed)
        ks = jax.random.split(key, 16)
        x = jax.random.normal(ks[0], (B, S, D), dtype=jnp.float32)
        adj = jax.random.randint(ks[1], (B, S, S), 0, 2, dtype=jnp.int32)
        adj = adj.at[:, jnp.arange(S), jnp.arange(S)].set(1)
        edge_attr = jax.random.normal(ks[2], (B, S, S), dtype=jnp.float32)
        sc = 1.0 / np.sqrt(D)
        p = lambda k, shp: jax.random.normal(k, shp, dtype=jnp.float32) * sc
        return {'x': x, 'adj_matrix': adj, 'edge_attr_matrix': edge_attr, 'ln1_g': jnp.ones((D,)), 'ln1_b': jnp.zeros((D,)), 'ln2_g': jnp.ones((D,)), 'ln2_b': jnp.zeros((D,)), 'wq': p(ks[3], (D, D)), 'bq': jnp.zeros((D,)), 'wk': p(ks[4], (D, D)), 'bk': jnp.zeros((D,)), 'wv': p(ks[5], (D, D)), 'bv': jnp.zeros((D,)), 'wo': p(ks[6], (D, D)), 'bo': jnp.zeros((D,)), 'w1': p(ks[7], (D, 4 * D)), 'b1': jnp.zeros((4 * D,)), 'w2': p(ks[8], (4 * D, D)), 'b2': jnp.zeros((D,))}
    _L0_gnn_all = _L0_gnn_setup()
    _L0_gnn_in = {k: v for k, v in _L0_gnn_all.items() if k in ('ln1_g', 'ln1_b', 'ln2_g', 'ln2_b', 'wq', 'bq', 'wk', 'bk', 'wv', 'bv', 'wo', 'bo', 'w1', 'b1', 'w2', 'b2')}
    del _L0_gnn_all

    def _L1_gnn_setup():
        import jax, jax.numpy as jnp
        import numpy as np
        HIDDEN = 256
        NHEADS = 8
        ALPHA = 0.1
        NUM_HOP = 4
        MASK_VAL = -16384.0
        LN_EPS = 1e-05
        key = jax.random.key(seed)
        ks = jax.random.split(key, 10)
        B, N, H = (8, 512, HIDDEN)
        s = 1.0 / np.sqrt(H)
        x = jax.random.normal(ks[0], (B, N, H), dtype=jnp.float32)
        adj = jax.random.randint(ks[1], (B, N, N), 0, 2, dtype=jnp.int32)
        Wq = jax.random.uniform(ks[2], (H, H), jnp.float32, -s, s)
        bq = jax.random.uniform(ks[3], (H,), jnp.float32, -s, s)
        Wk = jax.random.uniform(ks[4], (H, H), jnp.float32, -s, s)
        bk = jax.random.uniform(ks[5], (H,), jnp.float32, -s, s)
        Wv = jax.random.uniform(ks[6], (H, H), jnp.float32, -s, s)
        bv = jax.random.uniform(ks[7], (H,), jnp.float32, -s, s)
        gamma = jnp.ones((H,), jnp.float32)
        beta = jnp.zeros((H,), jnp.float32)
        return {'x': x, 'adj': adj, 'Wq': Wq, 'bq': bq, 'Wk': Wk, 'bk': bk, 'Wv': Wv, 'bv': bv, 'gamma': gamma, 'beta': beta}
    _L1_gnn_all = _L1_gnn_setup()
    _L1_gnn_in = {k: v for k, v in _L1_gnn_all.items() if k in ('Wq', 'bq', 'Wk', 'bk', 'Wv', 'bv', 'gamma', 'beta')}
    del _L1_gnn_all
    return {'x': x, 'adj': adj, 'L0_gnn_ln1_g': _L0_gnn_in['ln1_g'], 'L0_gnn_ln1_b': _L0_gnn_in['ln1_b'], 'L0_gnn_ln2_g': _L0_gnn_in['ln2_g'], 'L0_gnn_ln2_b': _L0_gnn_in['ln2_b'], 'L0_gnn_wq': _L0_gnn_in['wq'], 'L0_gnn_bq': _L0_gnn_in['bq'], 'L0_gnn_wk': _L0_gnn_in['wk'], 'L0_gnn_bk': _L0_gnn_in['bk'], 'L0_gnn_wv': _L0_gnn_in['wv'], 'L0_gnn_bv': _L0_gnn_in['bv'], 'L0_gnn_wo': _L0_gnn_in['wo'], 'L0_gnn_bo': _L0_gnn_in['bo'], 'L0_gnn_w1': _L0_gnn_in['w1'], 'L0_gnn_b1': _L0_gnn_in['b1'], 'L0_gnn_w2': _L0_gnn_in['w2'], 'L0_gnn_b2': _L0_gnn_in['b2'], 'L1_gnn_Wq': _L1_gnn_in['Wq'], 'L1_gnn_bq': _L1_gnn_in['bq'], 'L1_gnn_Wk': _L1_gnn_in['Wk'], 'L1_gnn_bk': _L1_gnn_in['bk'], 'L1_gnn_Wv': _L1_gnn_in['Wv'], 'L1_gnn_bv': _L1_gnn_in['bv'], 'L1_gnn_gamma': _L1_gnn_in['gamma'], 'L1_gnn_beta': _L1_gnn_in['beta']}

def reference(x, adj, L0_gnn_ln1_g, L0_gnn_ln1_b, L0_gnn_ln2_g, L0_gnn_ln2_b, L0_gnn_wq, L0_gnn_bq, L0_gnn_wk, L0_gnn_bk, L0_gnn_wv, L0_gnn_bv, L0_gnn_wo, L0_gnn_bo, L0_gnn_w1, L0_gnn_b1, L0_gnn_w2, L0_gnn_b2, L1_gnn_Wq, L1_gnn_bq, L1_gnn_Wk, L1_gnn_bk, L1_gnn_Wv, L1_gnn_bv, L1_gnn_gamma, L1_gnn_beta):
    import jax
    import jax.numpy as jnp

    def _L0_gnn_ref(x, adj_matrix, edge_attr_matrix, ln1_g, ln1_b, ln2_g, ln2_b, wq, bq, wk, bk, wv, bv, wo, bo, w1, b1, w2, b2):
        import jax, jax.numpy as jnp
        import numpy as np
        B, S, D, H = (2, 1024, 256, 8)
        HD = D // H
        EPS = 1e-05

        def _ln(x, g, b):
            mu = jnp.mean(x, axis=-1, keepdims=True)
            var = jnp.mean((x - mu) ** 2, axis=-1, keepdims=True)
            return (x - mu) * jax.lax.rsqrt(var + EPS) * g + b
        b, s, d = x.shape
        residual = x
        nx = _ln(x, ln1_g, ln1_b)
        q = (nx @ wq + bq).reshape(b, s, H, HD).transpose(0, 2, 1, 3)
        k = (nx @ wk + bk).reshape(b, s, H, HD).transpose(0, 2, 1, 3)
        v = (nx @ wv + bv).reshape(b, s, H, HD).transpose(0, 2, 1, 3)
        adjf = adj_matrix.astype(jnp.float32)
        bias = jnp.where(adj_matrix > 0, 0.1 * edge_attr_matrix * adjf, -jnp.inf)[:, None]
        scores = jnp.einsum('bhqd,bhkd->bhqk', q, k) / np.sqrt(HD) + bias
        attn = jax.nn.softmax(scores, axis=-1)
        out = jnp.einsum('bhqk,bhkd->bhqd', attn, v)
        out = out.transpose(0, 2, 1, 3).reshape(b, s, d)
        x1 = residual + (out @ wo + bo)
        n2 = _ln(x1, ln2_g, ln2_b)
        mlp = jax.nn.gelu(n2 @ w1 + b1, approximate=False) @ w2 + b2
        return x1 + mlp

    def _L1_gnn_ref(x, adj, Wq, bq, Wk, bk, Wv, bv, gamma, beta):
        import jax, jax.numpy as jnp
        import numpy as np
        HIDDEN = 256
        NHEADS = 8
        ALPHA = 0.1
        NUM_HOP = 4
        MASK_VAL = -16384.0
        LN_EPS = 1e-05
        B, N, H = x.shape
        u = H // NHEADS
        q = x @ Wq.T + bq
        k = x @ Wk.T + bk
        v = x @ Wv.T + bv
        qh = q.reshape(B, N, NHEADS, u).transpose(0, 2, 1, 3)
        kh = k.reshape(B, N, NHEADS, u).transpose(0, 2, 1, 3)
        vh = v.reshape(B, N, NHEADS, u).transpose(0, 2, 1, 3)
        scores = jnp.einsum('bhnd,bhmd->bhnm', qh, kh)
        mask = (adj == 0)[:, None, :, :]
        scores = jnp.where(mask, MASK_VAL, scores)
        pros = jax.nn.softmax(scores, axis=-1)
        z_init = vh
        z = z_init
        for _ in range(NUM_HOP):
            z = (1.0 - ALPHA) * jnp.einsum('bhnm,bhmd->bhnd', pros, z) + ALPHA * z_init
        h_prime = z.transpose(0, 2, 1, 3).reshape(B, N, H)
        y = x + h_prime
        mu = jnp.mean(y, axis=-1, keepdims=True)
        var = jnp.mean((y - mu) ** 2, axis=-1, keepdims=True)
        return (y - mu) / jnp.sqrt(var + LN_EPS) * gamma + beta
    x = _L0_gnn_ref(x, adj, adj, L0_gnn_ln1_g, L0_gnn_ln1_b, L0_gnn_ln2_g, L0_gnn_ln2_b, L0_gnn_wq, L0_gnn_bq, L0_gnn_wk, L0_gnn_bk, L0_gnn_wv, L0_gnn_bv, L0_gnn_wo, L0_gnn_bo, L0_gnn_w1, L0_gnn_b1, L0_gnn_w2, L0_gnn_b2)
    x = _L1_gnn_ref(x, adj, L1_gnn_Wq, L1_gnn_bq, L1_gnn_Wk, L1_gnn_bk, L1_gnn_Wv, L1_gnn_bv, L1_gnn_gamma, L1_gnn_beta)
    return x

_drawn_inputs = setup_inputs


def setup_inputs(seed=0):
    import zlib

    import numpy as np

    out = dict(_drawn_inputs(seed))
    spreads = {'L0_gnn_ln1_g': (1.0, 0.2),
     'L0_gnn_ln1_b': (0.0, 0.1),
     'L0_gnn_ln2_g': (1.0, 0.2),
     'L0_gnn_ln2_b': (0.0, 0.1),
     'L0_gnn_bq': (0.0, 0.1),
     'L0_gnn_bk': (0.0, 0.8),
     'L0_gnn_bv': (0.0, 0.1),
     'L0_gnn_bo': (0.0, 0.1),
     'L0_gnn_b1': (0.0, 0.1),
     'L0_gnn_b2': (0.0, 0.1),
     'L1_gnn_gamma': (1.0, 0.2),
     'L1_gnn_beta': (0.0, 0.1)}
    factors = {'L1_gnn_bq': 2.744, 'L1_gnn_bk': 8.0, 'L1_gnn_bv': 2.88}
    for name, (base, spread) in spreads.items():
        noise = np.random.default_rng([zlib.crc32(name.encode()), seed]).standard_normal(out[name].shape)
        drawn = base * np.exp(spread * noise) if base else spread * noise
        out[name] = jnp.asarray(drawn.astype(out[name].dtype))
    for name, factor in factors.items():
        out[name] = (out[name] * factor).astype(out[name].dtype)
    return out
```

```python
import concourse.bass as bass
from concourse import mybir
from contextlib import ExitStack

F32 = mybir.dt.float32
F32R = mybir.dt.float32r
I32 = mybir.dt.int32
ALU = mybir.AluOpType
ACT = mybir.ActivationFunctionType

B, N, F = 64, 128, 256
H = 8
D = F // H
FF = 4 * F
G = 4
GROUPS = B // G
KH = F // 128
MC = FF // 128
GN = G * N
GF = G * F
PAIR = 2
ROUNDS = 4
SLOTS = 2 * ROUNDS
HOPS = 4
ALPHA = 0.1
EPS = 1e-5
HOP_MASK = 16384.0
FAR = 1e30
LEAST_START = 3e38
QSCALE = 1.0 / float(D) ** 0.5

COLS = {}
for _name, _n in (("ln1_g", KH), ("ln1_b", KH), ("ln2_g", KH), ("ln2_b", KH), ("bq", KH), ("bk", KH),
                  ("bv", KH), ("b1", MC), ("hop_bq", KH), ("hop_bk", KH)):
    COLS[_name] = slice(sum(s.stop - s.start for s in COLS.values()),
                        sum(s.stop - s.start for s in COLS.values()) + _n)
NCOLS = sum(s.stop - s.start for s in COLS.values())
ROWS = ["bo", "b2", "hop_bv", "gamma", "beta"]


def graph_transformer(nc, x, adj, vec_cols, vec_rows, wq, wk, wv, wo, w1, w2, hwq, hwk, hwv, out):
    outer = ExitStack()
    mlp_stack = ExitStack()
    att_stack = ExitStack()

    def sb(stack, name, shape, dt=F32):
        return stack.enter_context(nc.sbuf_tensor(name, shape, dt))

    def sem(name):
        return outer.enter_context(nc.semaphore(name))

    def f32(ap):
        return ap.bitcast(F32)

    def wait_apart(engine, semaphore, value, passed):
        engine.wait_ge(semaphore, value)
        engine.sem_inc(passed, 1)

    with outer:
        bank = [outer.enter_context(nc.psum_tensor(f"bank{i}", [128, 512], F32)) for i in range(8)]
        acts = sb(outer, "acts", [128, GROUPS * GF])
        cols = sb(outer, "cols", [128, NCOLS])
        rows = sb(outer, "rows", [128, len(ROWS), F])
        ident = sb(outer, "ident", [128, 128])
        ones = sb(outer, "ones", [128, D])
        neg_half = sb(outer, "neg_half", [128, G])
        bo_folded = sb(outer, "bo_folded", [128, F])
        b1_folded = sb(outer, "b1_folded", [128, MC])
        q_bias = sb(outer, "q_bias", [128, KH])
        k_bias = sb(outer, "k_bias", [128, KH])
        hop_q_bias = sb(outer, "hop_q_bias", [128, KH])

        def split_weight(stack, name, shape):
            return tuple(sb(stack, f"{name}_{part}", shape, F32R) for part in ("hi", "lo"))

        wq_s = split_weight(outer, "wq", [128, KH, F])
        wk_s = split_weight(outer, "wk", [128, KH, F])
        wv_s = split_weight(outer, "wv", [128, KH, F])
        w1_s = split_weight(mlp_stack, "w1", [128, KH, FF])
        w2_s = split_weight(mlp_stack, "w2", [128, MC, F])
        wo_s = split_weight(att_stack, "wo", [128, KH, F])

        def products(weight, act):
            return ((weight[0], act[0]), (weight[1], act[0]), (weight[0], act[1]))

        def row(name):
            return rows[:, ROWS.index(name), :]

        def setup():
            s = ExitStack()
            with s:
                vecs_loaded = sem("vecs_loaded")
                w_loaded = {n: sem(f"{n}_loaded") for n in
                            ("wq", "wk", "wv", "wo", "w1", "w2")}
                consts_ready = sem("consts_ready")
                ident_zeroed = sem("ident_zeroed")
                hi_ready = sem("hi_ready")
                lo_ready = sem("lo_ready")
                folds_ready = sem("folds_ready")
                col_biases_ready = sem("col_biases_ready")
                cv_ready = sem("cv_ready")
                cv_spread = sem("cv_spread")
                bo_product_ready = sem("bo_product_ready")
                bo_ready = sem("bo_ready")
                cv = sb(s, "cv", [128, KH])
                cv_wide = sb(s, "cv_wide", [128, KH, 128])
                at = [GROUPS * GF]

                def raw(k, n):
                    at[0] -= k * n
                    return acts[:, at[0]:at[0] + k * n].rearrange("p (k n) -> p k n", k=k)

                raws = {"wq": raw(KH, F), "wk": raw(KH, F), "wv": raw(KH, F), "wo": raw(KH, F),
                        "w1": raw(KH, FF), "w2": raw(MC, F)}
                drams = {"wq": wq, "wk": wk, "wv": wv, "wo": wo, "w1": w1, "w2": w2}
                scaled_by = {"wq": "ln1_g", "wk": "ln1_g", "wv": "ln1_g", "w1": "ln2_g"}
                splits = {"wq": wq_s, "wk": wk_s, "wv": wv_s, "wo": wo_s, "w1": w1_s, "w2": w2_s}
                fold_bank, bo_bank = bank[0], bank[1]
                fold_at = {"wq": 0, "wk": KH, "wv": 2 * KH, "w1": 3 * KH}

                block = s.enter_context(nc.Block())

                @block.sync
                def _(sp):
                    sp.dma_start(cols[:, :], vec_cols).then_inc(vecs_loaded, 16)
                    sp.dma_start(rows[:, :, :].rearrange("p r n -> p (r n)"),
                                 vec_rows.broadcast_to([128, len(ROWS) * F])).then_inc(vecs_loaded, 16)
                    for name in drams:
                        sp.dma_start(raws[name], drams[name].rearrange("(k p) n -> p k n", p=128))\
                            .then_inc(w_loaded[name], 16)

                @block.gpsimd
                def _(pool):
                    nc.gpsimd.memset(ident[:, :], 0.0).then_inc(ident_zeroed, 1)
                    pool.wait_ge(ident_zeroed, 1)
                    nc.gpsimd.affine_select(out=ident[:, :], in_=ident[:, :], compare_op=ALU.not_equal,
                                            fill=1.0, base=0, pattern=[[-1, 128]], channel_multiplier=1)\
                        .then_inc(consts_ready, 1)
                    nc.gpsimd.memset(ones[:, :], 1.0).then_inc(consts_ready, 1)
                    nc.gpsimd.memset(neg_half[:, :], -0.5).then_inc(consts_ready, 1)

                @block.tensor
                def _(pe):
                    pe.wait_ge(vecs_loaded, 32)
                    for name, shift in (("wq", "ln1_b"), ("wk", "ln1_b"), ("wv", "ln1_b"), ("w1", "ln2_b")):
                        pe.wait_ge(w_loaded[name], 16)
                        for m in range(drams[name].shape[1] // 128):
                            c = fold_at[name] + m
                            for k in range(KH):
                                b = COLS[shift].start + k
                                last = nc.tensor.matmul(
                                    fold_bank[:, c:c + 1], raws[name][:, k, m * 128:(m + 1) * 128],
                                    cols[:, b:b + 1], start=(k == 0), stop=(k == KH - 1))
                    last.then_inc(folds_ready, 1)
                    pe.wait_ge(cv_spread, 1)
                    pe.wait_ge(w_loaded["wo"], 16)
                    for k in range(KH):
                        last = nc.tensor.matmul(bo_bank[:, 0:F], cv_wide[:, k, :], raws["wo"][:, k, :],
                                                start=(k == 0), stop=(k == KH - 1))
                    last.then_inc(bo_product_ready, 1)

                @block.vector
                def _(dve):
                    dve.wait_ge(vecs_loaded, 32)
                    done = 0
                    for name in drams:
                        dve.wait_ge(w_loaded[name], 16)
                        hi, lo = splits[name]
                        for k in range(raws[name].shape[1]):
                            if name in scaled_by:
                                c = COLS[scaled_by[name]].start + k
                                gain = cols[:, c:c + 1]
                            else:
                                gain = 1.0
                            nc.vector.tensor_scalar(hi[:, k, :], raws[name][:, k, :], gain, None, ALU.mult)\
                                .then_inc(hi_ready, 1)
                            done += 1
                            dve.wait_ge(hi_ready, done)
                            nc.vector.scalar_tensor_tensor(
                                out=lo[:, k, :], in0=raws[name][:, k, :], scalar=gain,
                                in1=f32(hi[:, k, :]), op0=ALU.mult, op1=ALU.subtract).then_inc(lo_ready, 1)
                    dve.wait_ge(folds_ready, 1)
                    nc.vector.tensor_tensor(cv[:, :], fold_bank[:, fold_at["wv"]:fold_at["wv"] + KH],
                                            cols[:, COLS["bv"]], ALU.add).then_inc(cv_ready, 1)
                    dve.wait_ge(cv_ready, 1)
                    nc.vector.tensor_copy(cv_wide[:, :, :], cv[:, :].unsqueeze(2).broadcast_to([128, KH, 128]))\
                        .then_inc(cv_spread, 1)
                    nc.vector.tensor_tensor(q_bias[:, :], fold_bank[:, fold_at["wq"]:fold_at["wq"] + KH],
                                            cols[:, COLS["bq"]], ALU.add).then_inc(col_biases_ready, 1)
                    nc.vector.tensor_tensor(k_bias[:, :], fold_bank[:, fold_at["wk"]:fold_at["wk"] + KH],
                                            cols[:, COLS["bk"]], ALU.add)
                    nc.vector.tensor_tensor(b1_folded[:, :], fold_bank[:, fold_at["w1"]:fold_at["w1"] + MC],
                                            cols[:, COLS["b1"]], ALU.add)
                    nc.vector.tensor_scalar(hop_q_bias[:, :], cols[:, COLS["hop_bq"]], -1.0, None, ALU.mult)
                    dve.wait_ge(col_biases_ready, 1)
                    nc.vector.tensor_scalar(q_bias[:, :], q_bias[:, :], -QSCALE, None, ALU.mult)
                    dve.wait_ge(bo_product_ready, 1)
                    nc.vector.tensor_tensor(bo_folded[:, :], bo_bank[:, 0:F], row("bo"), ALU.add)\
                        .then_inc(bo_ready, 1)
                    dve.wait_ge(bo_ready, 1)

        def pe_project(pe, lin, xn, act_s, weights, proj_ready):
            def transpose(half):
                for j in range(G):
                    last = nc.tensor.transpose(lin[half][:, j * N:(j + 1) * N],
                                               xn[:, j, half * 128:(half + 1) * 128], ident[:, :])
                last.then_inc(proj_ready, 1)

            def feature_major(which, half):
                todo = [(k, w, a) for k in range(KH) for w, a in products(weights[which], act_s)]
                for n, (k, w, a) in enumerate(todo):
                    last = nc.tensor.matmul(lin[half][:, :], w[:, k, half * 128:(half + 1) * 128],
                                            a[:, k, :], start=(n == 0), stop=(n == len(todo) - 1))
                last.then_inc(proj_ready, 1)

            def node_major(which, pair):
                for j in range(PAIR):
                    g = PAIR * pair + j
                    todo = [(k, w, a) for k in range(KH) for w, a in products(weights[which], act_s)]
                    for n, (k, w, a) in enumerate(todo):
                        last = nc.tensor.matmul(lin[pair][:, j * F:(j + 1) * F],
                                                a[:, k, g * N:(g + 1) * N], w[:, k, :],
                                                start=(n == 0), stop=(n == len(todo) - 1))
                last.then_inc(proj_ready, 1)

            return transpose, feature_major, node_major

        def score_round(score_bank, qT, kT, pair, r):
            for j in range(PAIR):
                cols_ = slice((PAIR * pair + j) * N, (PAIR * pair + j + 1) * N)
                for half in range(KH):
                    last = nc.tensor.matmul(
                        score_bank[:, (2 * j + half) * N:(2 * j + half + 1) * N],
                        qT[D * r:D * (r + 1), half, cols_], kT[D * r:D * (r + 1), half, cols_],
                        start=True, stop=True)
            return last

        def attention_phase():
            s = ExitStack()
            with s:
                xin = [sb(s, f"xin{i}", [128, G, F]) for i in range(2)]
                adj_sb = [sb(s, f"adj_sb{i}", [128, G, N], I32) for i in range(2)]
                bias = [sb(s, f"bias{i}", [128, G, N]) for i in range(2)]
                edge = sb(s, "edge", [128, G, N])
                stats = sb(s, "stats", [128, G, 6])
                moments = sb(s, "moments", [128, G, 2])
                var_eps = sb(s, "var_eps", [128, G])
                rstd = sb(s, "rstd", [128, G])
                xn = sb(s, "xn", [128, G, F])
                xnT = tuple(sb(s, f"xnT_{p}", [128, KH, GN], F32R) for p in ("hi", "lo"))
                qT = [sb(s, f"qT{i}", [128, KH, GN]) for i in range(2)]
                kT = [sb(s, f"kT{i}", [128, KH, GN]) for i in range(2)]
                v = [sb(s, f"v{i}", [128, G, F]) for i in range(2)]
                probs = [sb(s, f"probs{i}", [128, PAIR, H, N]) for i in range(2)]
                least = [sb(s, f"least{i}", [128, PAIR, H]) for i in range(2)]
                probsT = [sb(s, f"probsT{i}", [128, 4 * N]) for i in range(2)]
                rinv = sb(s, "rinv", [128, KH * N])
                att = sb(s, "att", [128, KH * N])
                attT = tuple([sb(s, f"attT{i}_{p}", [128, PAIR, KH * N], F32R) for i in range(2)]
                             for p in ("hi", "lo"))
                score_bank, pt_bank, lin = bank[0:2], bank[2:4], bank[4:6]
                pv_bank, wo_bank = bank[6], bank[7]

                x_loaded = [sem(f"x_loaded{i}") for i in range(2)]
                dve_waits = sem("dve_waits")
                pool_waits = sem("pool_waits")
                adj_loaded = [sem(f"adj_loaded{i}") for i in range(2)]
                bias_parts = sem("bias_parts")
                bias_ready = sem("bias_ready")
                resid_ready = sem("resid_ready")
                stats_ready = sem("stats_ready")
                moments_ready = sem("moments_ready")
                var_ready = sem("var_ready")
                rstd_ready = sem("rstd_ready")
                normed = sem("normed")
                proj_ready = sem("proj_ready")
                hi_ready = sem("xnT_hi_ready")
                lo_ready = sem("xnT_lo_ready")
                proj_copied = sem("proj_copied")
                scores_ready = sem("scores_ready")
                round_masked = sem("round_masked")
                exp_done = sem("exp_done")
                pt_ready = sem("pt_ready")
                pt_copied = sem("pt_copied")
                pv_ready = sem("pv_ready")
                rinv_ready = sem("rinv_ready")
                att_taken = sem("att_taken")
                att_hi_ready = sem("att_hi_ready")
                att_split = sem("att_split")
                wo_ready = sem("wo_ready")
                x1_added = sem("x1_added")

                def loaded(g, par):
                    return g * 8 + (8 if par else 16)

                def run(engine, group):
                    group(0, 0, cur=True, prev=False, nxt=True)
                    group(1, 1, cur=True, prev=True, nxt=True)
                    with engine.Fori(1, GROUPS // 2 - 1) as i:
                        group(i * 2, 0, cur=True, prev=True, nxt=True)
                        group(i * 2 + 1, 1, cur=True, prev=True, nxt=True)
                    group(GROUPS - 2, 0, cur=True, prev=True, nxt=True)
                    group(GROUPS - 1, 1, cur=True, prev=True, nxt=False)
                    group(GROUPS, 0, cur=False, prev=True, nxt=False)

                block = s.enter_context(nc.Block())

                @block.sync
                def _(sp):
                    def load(g, par):
                        sp.dma_start(xin[par][:, :, :], x[g, :, :, :]).then_inc(x_loaded[par], 16)
                        sp.dma_start(adj_sb[par][:, :, :], adj[g, :, :, :]).then_inc(adj_loaded[par], 16)

                    load(0, 0)
                    load(1, 1)
                    with sp.Fori(0, GROUPS // 2 - 1) as i:
                        for par in range(2):
                            g = i * 2 + par
                            sp.wait_ge(bias_ready, g + 1)
                            sp.wait_ge(resid_ready, g + 1)
                            sp.wait_ge(normed, g + 1)
                            load(g + 2, par)

                @block.gpsimd
                def _(pool):
                    def root(g):
                        wait_apart(pool, moments_ready, g + 1, pool_waits)
                        nc.gpsimd.tensor_scalar(var_eps[:, :], moments[:, :, 1], EPS, None, ALU.add)\
                            .then_inc(var_ready, 1)
                        pool.wait_ge(var_ready, g + 1)
                        nc.gpsimd.tensor_tensor(rstd[:, :], var_eps[:, :], neg_half[:, :], ALU.pow)\
                            .then_inc(rstd_ready, 1)

                    def mask(g, par, early):
                        if not early:
                            pool.wait_ge(round_masked, (g - 1) * SLOTS)
                        wait_apart(pool, adj_loaded[par], loaded(g, par), pool_waits)
                        nc.gpsimd.tensor_scalar(edge[:, :, :], adj_sb[par][:, :, :], 0.0, -ALPHA,
                                                ALU.max, ALU.mult).then_inc(bias_parts, 1)
                        nc.gpsimd.tensor_scalar(bias[par][:, :, :], adj_sb[par][:, :, :], 0.0, None,
                                                ALU.max).then_inc(bias_parts, 1)
                        pool.wait_ge(bias_parts, g * 4 + 2)
                        nc.gpsimd.tensor_tensor(edge[:, :, :], edge[:, :, :], bias[par][:, :, :], ALU.mult)\
                            .then_inc(bias_parts, 1)
                        wait_apart(pool, bias_parts, g * 4 + 3, pool_waits)
                        nc.gpsimd.tensor_scalar(bias[par][:, :, :], adj_sb[par][:, :, :], 0.0, FAR,
                                                ALU.is_le, ALU.mult).then_inc(bias_parts, 1)
                        pool.wait_ge(bias_parts, g * 4 + 4)
                        nc.gpsimd.tensor_tensor(bias[par][:, :, :], bias[par][:, :, :], edge[:, :, :], ALU.add)\
                            .then_inc(bias_ready, 1)
                        pool.wait_ge(bias_ready, g + 1)

                    def residual(g, par):
                        pool.wait_ge(x_loaded[par], loaded(g, par))
                        nc.gpsimd.tensor_tensor(
                            acts[:, bass.ds(g * GF, GF)].rearrange("p (j f) -> p j f", j=G),
                            xin[par][:, :, :], bo_folded[:, :].unsqueeze(1).broadcast_to([128, G, F]),
                            ALU.add).then_inc(resid_ready, 1)

                    root(0)
                    mask(0, 0, early=True)

                    def group(g, par, cur, prev, nxt):
                        if nxt:
                            root(g + 1)
                            mask(g + 1, 1 - par, early=not prev)
                        if cur:
                            residual(g, par)

                    run(pool, group)

                @block.tensor
                def _(pe):
                    transpose, feature_major, node_major = pe_project(
                        pe, lin, xn, xnT, {"q": wq_s, "k": wk_s, "v": wv_s}, proj_ready)

                    def project(g, chunk, first=False):
                        if chunk == 0:
                            pe.wait_ge(normed, g + 1)
                            if not first:
                                pe.wait_ge(proj_copied, g * 6 - 1)
                            transpose(0)
                        elif chunk == 1:
                            if not first:
                                pe.wait_ge(proj_copied, g * 6)
                            transpose(1)
                        elif chunk in (2, 3):
                            pe.wait_ge(lo_ready, g * 2 + 2)
                            feature_major("q", chunk - 2)
                        elif chunk in (4, 5):
                            pe.wait_ge(proj_copied, g * 6 + chunk - 3)
                            feature_major("k", chunk - 4)
                        else:
                            pe.wait_ge(proj_copied, g * 6 + chunk - 3)
                            node_major("v", chunk - 6)

                    def scores(g, par, slot, early):
                        if slot == 0:
                            pe.wait_ge(proj_copied, g * 6 + 4)
                        if not early:
                            pe.wait_ge(round_masked, g * SLOTS + slot - 1)
                        score_round(score_bank[slot % 2], qT[par], kT[par], slot // ROUNDS, slot % ROUNDS)\
                            .then_inc(scores_ready, 1)

                    def transpose_probs(g, unit, early):
                        graph, half = unit // 2, unit % 2
                        pair = graph // PAIR
                        if unit % 4 == 0:
                            pe.wait_ge(exp_done, g * SLOTS + ROUNDS * pair + ROUNDS)
                        if not early:
                            pe.wait_ge(pt_copied, g * SLOTS + unit - 1)
                        for c in range(4):
                            last = nc.tensor.transpose(pt_bank[unit % 2][:, c * N:(c + 1) * N],
                                                       probs[pair][:, graph % PAIR, 4 * half + c, :], ident[:, :])
                        last.then_inc(pt_ready, 1)

                    def weigh(g, par, unit, early):
                        graph, half = unit // 2, unit % 2
                        if unit == 0:
                            pe.wait_ge(proj_copied, g * 6 + 6)
                        pe.wait_ge(pt_copied, g * SLOTS + unit + 1)
                        if half == 0 and not early:
                            pe.wait_ge(att_taken, g * G + graph)
                        for lhs, at in ((None, 0), (ones, KH * N)):
                            for c in range(4):
                                h = 4 * half + c
                                l = v[par][:, graph, h * D:(h + 1) * D] if lhs is None else ones[:, :]
                                last = nc.tensor.matmul(
                                    pv_bank[D * c:D * (c + 1), at + half * N:at + (half + 1) * N], l,
                                    probsT[unit % 2][:, c * N:(c + 1) * N], start=True, stop=True,
                                    tile_position=(0, D * c))
                        last.then_inc(pv_ready, 1)

                    def output(g, pair, early):
                        pe.wait_ge(att_split, g * G + PAIR * (pair + 1))
                        if not early:
                            pe.wait_ge(x1_added, g * 2 + pair)
                        for j in range(PAIR):
                            todo = [(k, w, a) for k in range(KH)
                                    for w, a in products(wo_s, (attT[0][pair], attT[1][pair]))]
                            for n, (k, w, a) in enumerate(todo):
                                last = nc.tensor.matmul(wo_bank[:, j * F:(j + 1) * F],
                                                        a[:, j, k * N:(k + 1) * N], w[:, k, :],
                                                        start=(n == 0), stop=(n == len(todo) - 1))
                        last.then_inc(wo_ready, 1)

                    for chunk in range(6):
                        project(0, chunk, first=True)

                    def group(g, par, cur, prev, nxt):
                        for slot in range(SLOTS):
                            if cur:
                                scores(g, par, slot, early=not prev and slot < 2)
                                if slot < 2:
                                    project(g, 6 + slot)
                            if nxt and slot >= 3:
                                for chunk in {3: (0, 1), 4: (2, 3), 5: (4,), 6: (5,), 7: ()}[slot]:
                                    project(g + 1, chunk)
                            if prev and slot < 4:
                                transpose_probs(g - 1, slot + 4, early=False)
                            if cur and slot >= 4:
                                transpose_probs(g, slot - 4, early=not prev and slot < 6)
                            if prev and slot < 5:
                                weigh(g - 1, 1 - par, slot + 3, early=False)
                            if cur and slot >= 5:
                                weigh(g, par, slot - 5, early=not prev and slot == 5)
                            if prev and slot == 2:
                                output(g - 1, 0, early=False if not isinstance(g, int) else g == 1)
                            if prev and slot == 7:
                                output(g - 1, 1, early=False)

                    run(pe, group)

                @block.scalar
                def _(act):
                    def project(g, par, chunk, early):
                        act.wait_ge(proj_ready, g * 8 + chunk + 1)
                        if chunk < 2:
                            nc.scalar.activation(xnT[0][:, chunk, :], lin[chunk][:, :], ACT.Copy)\
                                .then_inc(hi_ready, 1)
                        elif chunk < 4:
                            if not early:
                                act.wait_ge(scores_ready, (g - 1) * SLOTS)
                            h = chunk - 2
                            nc.scalar.activation(qT[par][:, h, :], lin[h][:, :], ACT.Identity,
                                                 scale=-QSCALE, bias=q_bias[:, h:h + 1])\
                                .then_inc(proj_copied, 1)
                        elif chunk < 6:
                            h = chunk - 4
                            nc.scalar.activation(kT[par][:, h, :], lin[h][:, :], ACT.Identity,
                                                 bias=k_bias[:, h:h + 1]).then_inc(proj_copied, 1)
                        else:
                            if not early:
                                act.wait_ge(pv_ready, (g - 1) * SLOTS)
                            p = chunk - 6
                            nc.scalar.activation(
                                v[par][:, PAIR * p:PAIR * (p + 1), :].rearrange("p j f -> p (j f)"),
                                lin[p][:, :], ACT.Copy).then_inc(proj_copied, 1)

                    def exponentials(g, slot):
                        pair, r = slot // ROUNDS, slot % ROUNDS
                        act.wait_ge(round_masked, g * SLOTS + slot + 1)
                        for j in range(PAIR):
                            for h in (r, r + 4):
                                last = nc.scalar.activation(probs[pair][:, j, h, :], probs[pair][:, j, h, :],
                                                            ACT.Exp, scale=-1.0,
                                                            bias=least[pair][:, j, h:h + 1])
                        last.then_inc(exp_done, 1)

                    def copy_probs(g, unit, early):
                        act.wait_ge(pt_ready, g * SLOTS + unit + 1)
                        if not early:
                            act.wait_ge(pv_ready, g * SLOTS + unit - 1)
                        nc.scalar.activation(probsT[unit % 2][:, :], pt_bank[unit % 2][:, :], ACT.Copy)\
                            .then_inc(pt_copied, 1)

                    for chunk in range(6):
                        project(0, 0, chunk, early=True)

                    def group(g, par, cur, prev, nxt):
                        for slot in range(SLOTS):
                            if cur:
                                exponentials(g, slot)
                                if slot < 2:
                                    project(g, par, 6 + slot, early=isinstance(g, int) and g < 2)
                            if nxt and slot >= 3:
                                for chunk in {3: (0, 1), 4: (2, 3), 5: (4,), 6: (5,), 7: ()}[slot]:
                                    project(g + 1, 1 - par, chunk, early=not prev)
                            if prev and slot < 4:
                                copy_probs(g - 1, slot + 4, early=False)
                            if cur and slot >= 4:
                                copy_probs(g, slot - 4, early=not prev and slot < 6)

                    run(act, group)

                @block.vector
                def _(dve):
                    def norm_stats(g, par):
                        dve.wait_ge(x_loaded[par], loaded(g, par))
                        for j in range(G):
                            last = nc.vector.bn_stats(stats[:, j, :], xin[par][:, j, :])
                        last.then_inc(stats_ready, 1)
                        wait_apart(dve, stats_ready, g + 1, dve_waits)
                        for j in range(G):
                            last = nc.vector.bn_aggr(moments[:, j, :], stats[:, j, :])
                        last.then_inc(moments_ready, 1)

                    def normalise(g, par, early):
                        dve.wait_ge(rstd_ready, g + 1)
                        if not early:
                            dve.wait_ge(proj_ready, g * 8 - 6)
                        for j in range(G):
                            last = nc.vector.tensor_scalar(xn[:, j, :], xin[par][:, j, :],
                                                           moments[:, j, 0:1], rstd[:, j:j + 1],
                                                           ALU.subtract, ALU.mult)
                        last.then_inc(normed, 1)

                    def split(g):
                        for half in range(KH):
                            dve.wait_ge(hi_ready, g * 2 + half + 1)
                            nc.vector.tensor_tensor(xnT[1][:, half, :], lin[half][:, :],
                                                    f32(xnT[0][:, half, :]), ALU.subtract)\
                                .then_inc(lo_ready, 1)

                    def mask_round(g, par, slot, early):
                        pair, r = slot // ROUNDS, slot % ROUNDS
                        if slot == 0:
                            dve.wait_ge(bias_ready, g + 1)
                        if r == 0 and not early:
                            dve.wait_ge(pt_ready, (g - 1) * SLOTS + 4 * pair + 4)
                        wait_apart(dve, scores_ready, g * SLOTS + slot + 1, dve_waits)
                        for j in range(PAIR):
                            for half in range(KH):
                                h = r + 4 * half
                                last = nc.vector.tensor_tensor_reduce(
                                    out=probs[pair][:, j, h, :],
                                    in0=score_bank[slot % 2][:, (2 * j + half) * N:(2 * j + half + 1) * N],
                                    in1=bias[par][:, PAIR * pair + j, :], scale=1.0, scalar=LEAST_START,
                                    op0=ALU.add, op1=ALU.min, accum_out=least[pair][:, j, h:h + 1])
                        last.then_inc(round_masked, 1)

                    def take_attention(g, graph, early):
                        pair, j = graph // PAIR, graph % PAIR
                        n = g * G + graph
                        dve.wait_ge(pv_ready, n * 2 + 2)
                        nc.vector.reciprocal(rinv[:, :], pv_bank[:, KH * N:2 * KH * N]).then_inc(rinv_ready, 1)
                        dve.wait_ge(rinv_ready, n + 1)
                        nc.vector.tensor_tensor(att[:, :], pv_bank[:, 0:KH * N], rinv[:, :], ALU.mult)\
                            .then_inc(att_taken, 1)
                        dve.wait_ge(att_taken, n + 1)
                        if j == 0 and not early:
                            dve.wait_ge(wo_ready, g * 2 + pair - 1)
                        nc.vector.tensor_copy(attT[0][pair][:, j, :], att[:, :]).then_inc(att_hi_ready, 1)
                        dve.wait_ge(att_hi_ready, n + 1)
                        nc.vector.tensor_tensor(attT[1][pair][:, j, :], att[:, :], f32(attT[0][pair][:, j, :]),
                                                ALU.subtract).then_inc(att_split, 1)

                    def add_output(g, pair):
                        dve.wait_ge(wo_ready, g * 2 + pair + 1)
                        if pair == 0:
                            dve.wait_ge(resid_ready, g + 1)
                        where = acts[:, bass.ds(g * GF + pair * PAIR * F, PAIR * F)]
                        nc.vector.tensor_tensor(where, wo_bank[:, :], where, ALU.add).then_inc(x1_added, 1)

                    norm_stats(0, 0)
                    normalise(0, 0, early=True)
                    split(0)

                    def group(g, par, cur, prev, nxt):
                        for slot in range(SLOTS):
                            if prev and slot in (1, 3, 5):
                                take_attention(g - 1, {1: 1, 3: 2, 5: 3}[slot],
                                               early=isinstance(g, int) and g == 1)
                            if cur and slot == 7:
                                take_attention(g, 0, early=not prev)
                            if cur:
                                mask_round(g, par, slot, early=not prev)
                            if nxt and slot == 0:
                                norm_stats(g + 1, 1 - par)
                            if nxt and slot == 2:
                                normalise(g + 1, 1 - par, early=False)
                            if nxt and slot == 3:
                                split(g + 1)
                            if prev and slot == 3:
                                add_output(g - 1, 0)
                            if prev and slot == 7:
                                add_output(g - 1, 1)

                    run(dve, group)

        def mlp_phase():
            s = ExitStack()
            with s:
                RING = 4
                stats = sb(s, "m_stats", [128, G, 6])
                moments = sb(s, "m_moments", [128, G, 2])
                var_eps = sb(s, "m_var_eps", [128, G])
                rstd = sb(s, "m_rstd", [128, G])
                xn = sb(s, "m_xn", [128, G, F])
                xnT = tuple(sb(s, f"m_xnT_{p}", [128, KH, GN], F32R) for p in ("hi", "lo"))
                hid = [sb(s, f"hid{i}", [128, GN]) for i in range(RING)]
                hid_hi = [sb(s, f"hid_hi{i}", [128, GN], F32R) for i in range(RING)]
                hid_lo = [sb(s, f"hid_lo{i}", [128, GN], F32R) for i in range(RING)]
                raw = [sb(s, f"raw{i}", [128, KH, F]) for i in range(3)]
                up, tr, acc = bank[0:4], bank[4:6], bank[6:8]

                raw_loaded = [sem(f"raw_loaded{i}") for i in range(3)]
                raw_hi_ready = sem("raw_hi_ready")
                raw_split = sem("raw_split")

                dve_waits = sem("m_dve_waits")
                pool_waits = sem("m_pool_waits")
                stats_ready = sem("m_stats_ready")
                moments_ready = sem("m_moments_ready")
                var_ready = sem("m_var_ready")
                rstd_ready = sem("m_rstd_ready")
                normed = sem("m_normed")
                t_ready = sem("m_t_ready")
                hi_ready = sem("m_hi_ready")
                lo_ready = sem("m_lo_ready")
                up_ready = sem("up_ready")
                gelu_done = sem("gelu_done")
                hid_hi_ready = sem("hid_hi_ready")
                hid_split = sem("hid_split")
                down_done = sem("down_done")
                b2_added = sem("b2_added")
                x2_added = sem("x2_added")

                def run(engine, group):
                    group(0, prev=False, nxt=True)
                    with engine.Fori(1, GROUPS - 1) as g:
                        group(g, prev=True, nxt=True)
                    group(GROUPS - 1, prev=True, nxt=False)

                def group_acts(g):
                    return acts[:, bass.ds(g * GF, GF)]

                block = s.enter_context(nc.Block())

                @block.sync
                def _(sp):
                    for i, w in enumerate((hwq, hwk, hwv)):
                        sp.dma_start(raw[i][:, :, :], w.rearrange("(k p) n -> p k n", p=128))\
                            .then_inc(raw_loaded[i], 16)

                @block.gpsimd
                def _(pool):
                    def root(g):
                        wait_apart(pool, moments_ready, g + 1, pool_waits)
                        nc.gpsimd.tensor_scalar(var_eps[:, :], moments[:, :, 1], EPS, None, ALU.add)\
                            .then_inc(var_ready, 1)
                        pool.wait_ge(var_ready, g + 1)
                        nc.gpsimd.tensor_tensor(rstd[:, :], var_eps[:, :], neg_half[:, :], ALU.pow)\
                            .then_inc(rstd_ready, 1)

                    root(0)

                    def group(g, prev, nxt):
                        pool.wait_ge(normed, g + 1)
                        where = group_acts(g).rearrange("p (j f) -> p j f", j=G)
                        nc.gpsimd.tensor_tensor(where, where, row("b2").unsqueeze(1).broadcast_to([128, G, F]),
                                                ALU.add).then_inc(b2_added, 1)
                        if nxt:
                            root(g + 1)

                    run(pool, group)

                @block.tensor
                def _(pe):
                    def transpose(g):
                        pe.wait_ge(normed, g + 1)
                        for half in range(KH):
                            for j in range(G):
                                last = nc.tensor.transpose(tr[half][:, j * N:(j + 1) * N],
                                                           xn[:, j, half * 128:(half + 1) * 128], ident[:, :])
                            last.then_inc(t_ready, 1)

                    def up_chunk(g, m, early):
                        if m == 0:
                            pe.wait_ge(lo_ready, g * 2 + 2)
                        if not early:
                            pe.wait_ge(gelu_done, g * MC + m - RING + 1)
                        todo = [(k, w, a) for k in range(KH) for w, a in products(w1_s, xnT)]
                        for n, (k, w, a) in enumerate(todo):
                            last = nc.tensor.matmul(up[m % RING][:, :], w[:, k, m * 128:(m + 1) * 128],
                                                    a[:, k, :], start=(n == 0), stop=(n == len(todo) - 1))
                        last.then_inc(up_ready, 1)

                    def down_chunk(g, m, early):
                        pe.wait_ge(hid_split, g * MC + m + 1)
                        if m == 0 and not early:
                            pe.wait_ge(x2_added, g * 2)
                        r = m % RING
                        for j in range(G):
                            for n, (w, a) in enumerate(products(w2_s, (hid_hi[r], hid_lo[r]))):
                                last = nc.tensor.matmul(
                                    acc[j // 2][:, (j % 2) * F:(j % 2 + 1) * F], a[:, j * N:(j + 1) * N],
                                    w[:, m, :], start=(m == 0 and n == 0 and j % 2 == 0),
                                    stop=(m == MC - 1 and n == 2), skip_group_check=True)
                        last.then_inc(down_done, 1)

                    transpose(0)

                    def group(g, prev, nxt):
                        for m in range(MC):
                            up_chunk(g, m, early=not prev and m < RING)
                            if m >= 2:
                                down_chunk(g, m - 2, early=not prev)
                        if nxt:
                            transpose(g + 1)
                        for m in (MC - 2, MC - 1):
                            down_chunk(g, m, early=False)

                    run(pe, group)

                @block.scalar
                def _(act):
                    def split(g):
                        for half in range(KH):
                            act.wait_ge(t_ready, g * 2 + half + 1)
                            nc.scalar.activation(xnT[0][:, half, :], tr[half][:, :], ACT.Copy)\
                                .then_inc(hi_ready, 1)

                    split(0)

                    def group(g, prev, nxt):
                        for m in range(MC):
                            act.wait_ge(up_ready, g * MC + m + 1)
                            if prev or m >= RING:
                                act.wait_ge(hid_split, g * MC + m - RING + 1)
                            nc.scalar.activation(hid[m % RING][:, :], up[m % RING][:, :], ACT.Gelu,
                                                 bias=b1_folded[:, m:m + 1]).then_inc(gelu_done, 1)
                        if nxt:
                            split(g + 1)

                    run(act, group)

                @block.vector
                def _(dve):
                    def norm_stats(g):
                        for j in range(G):
                            last = nc.vector.bn_stats(stats[:, j, :], acts[:, bass.ds(g * GF + j * F, F)])
                        last.then_inc(stats_ready, 1)
                        wait_apart(dve, stats_ready, g + 1, dve_waits)
                        for j in range(G):
                            last = nc.vector.bn_aggr(moments[:, j, :], stats[:, j, :])
                        last.then_inc(moments_ready, 1)

                    def normalise(g, early):
                        dve.wait_ge(rstd_ready, g + 1)
                        if not early:
                            dve.wait_ge(t_ready, g * 2)
                        for j in range(G):
                            last = nc.vector.tensor_scalar(xn[:, j, :], acts[:, bass.ds(g * GF + j * F, F)],
                                                           moments[:, j, 0:1], rstd[:, j:j + 1],
                                                           ALU.subtract, ALU.mult)
                        last.then_inc(normed, 1)

                    def split(g):
                        for half in range(KH):
                            dve.wait_ge(hi_ready, g * 2 + half + 1)
                            nc.vector.tensor_tensor(xnT[1][:, half, :], tr[half][:, :],
                                                    f32(xnT[0][:, half, :]), ALU.subtract)\
                                .then_inc(lo_ready, 1)

                    def split_hidden(g, m, early):
                        r = m % RING
                        dve.wait_ge(gelu_done, g * MC + m + 1)
                        if not early:
                            dve.wait_ge(down_done, g * MC + m - RING + 1)
                        nc.vector.tensor_copy(hid_hi[r][:, :], hid[r][:, :]).then_inc(hid_hi_ready, 1)
                        dve.wait_ge(hid_hi_ready, g * MC + m + 1)
                        nc.vector.tensor_tensor(hid_lo[r][:, :], hid[r][:, :], f32(hid_hi[r][:, :]),
                                                ALU.subtract).then_inc(hid_split, 1)

                    def add_down(g):
                        dve.wait_ge(b2_added, g + 1)
                        dve.wait_ge(down_done, g * MC + MC)
                        for i in range(2):
                            where = acts[:, bass.ds(g * GF + i * PAIR * F, PAIR * F)]
                            nc.vector.tensor_tensor(where, acc[i][:, :], where, ALU.add).then_inc(x2_added, 1)

                    norm_stats(0)
                    normalise(0, early=True)
                    split(0)

                    def group(g, prev, nxt):
                        for m in range(MC):
                            split_hidden(g, m, early=not prev and m < RING)
                            if prev and m == 0:
                                add_down(g - 1)
                            if nxt and m == 2:
                                norm_stats(g + 1)
                            if nxt and m == 4:
                                normalise(g + 1, early=False)
                        if nxt:
                            split(g + 1)

                    def refill_weights():
                        for i, (hi, lo) in enumerate((wq_s, wk_s, wv_s)):
                            dve.wait_ge(raw_loaded[i], 16)
                            nc.vector.tensor_copy(hi[:, :, :], raw[i][:, :, :]).then_inc(raw_hi_ready, 1)
                            dve.wait_ge(raw_hi_ready, i + 1)
                            nc.vector.tensor_tensor(lo[:, :, :], raw[i][:, :, :], f32(hi[:, :, :]),
                                                    ALU.subtract).then_inc(raw_split, 1)

                    run(dve, group)
                    add_down(GROUPS - 1)
                    refill_weights()

        def hop_phase():
            s = ExitStack()
            with s:
                adj_sb = [sb(s, f"h_adj_sb{i}", [128, G, N], I32) for i in range(2)]
                keep = [sb(s, f"keep{i}", [128, G, N]) for i in range(2)]
                fill = [sb(s, f"fill{i}", [128, G, N]) for i in range(2)]
                xs = [sb(s, f"xs{i}", [128, G, F]) for i in range(2)]
                xsT = tuple(sb(s, f"xsT_{p}", [128, KH, GN], F32R) for p in ("hi", "lo"))
                qT = [sb(s, f"h_qT{i}", [128, KH, GN]) for i in range(2)]
                kT = [sb(s, f"h_kT{i}", [128, KH, GN]) for i in range(2)]
                z0 = [sb(s, f"z0{i}", [128, G, F]) for i in range(2)]
                z0_part = [sb(s, f"z0_part{i}", [128, G, F]) for i in range(2)]
                resid = [sb(s, f"resid{i}", [128, G, F]) for i in range(2)]
                probs = [sb(s, f"h_probs{i}", [128, PAIR, H, N]) for i in range(2)]
                least = [sb(s, f"h_least{i}", [128, PAIR * H]) for i in range(2)]
                sums = [sb(s, f"sums{i}", [128, PAIR * H]) for i in range(2)]
                shares = [sb(s, f"shares{i}", [128, PAIR * H]) for i in range(2)]
                probsT = [sb(s, f"h_probsT{i}", [128, 4, 4 * N]) for i in range(2)]
                zT = sb(s, "zT", [128, PAIR, KH * N])
                z = sb(s, "z", [128, PAIR, F])
                y = [sb(s, f"y{i}", [128, PAIR, F]) for i in range(2)]
                stats = sb(s, "h_stats", [128, PAIR, 6])
                moments = sb(s, "h_moments", [128, PAIR, 2])
                var_eps = sb(s, "h_var_eps", [128, PAIR])
                rstd = sb(s, "h_rstd", [128, PAIR])
                score_bank, pt_bank, lin = bank[0:2], bank[2:4], bank[4:6]
                fwd_bank, back_bank = bank[6], bank[7]

                dve_waits = sem("h_dve_waits")
                pool_waits = sem("h_pool_waits")
                adj_loaded = [sem(f"h_adj_loaded{i}") for i in range(2)]
                fill_ready = sem("fill_ready")
                mask_ready = sem("mask_ready")
                xs_ready = sem("xs_ready")
                z0_part_ready = sem("z0_part_ready")
                resid_ready = sem("h_resid_ready")
                proj_ready = sem("h_proj_ready")
                hi_ready = sem("xsT_hi_ready")
                lo_ready = sem("xsT_lo_ready")
                proj_copied = sem("h_proj_copied")
                z0_ready = sem("z0_ready")
                scores_ready = sem("h_scores_ready")
                round_kept = sem("round_kept")
                round_masked = sem("h_round_masked")
                exp_done = sem("h_exp_done")
                pt_ready = sem("h_pt_ready")
                pt_copied = sem("h_pt_copied")
                sums_inverted = sem("sums_inverted")
                shares_ready = sem("shares_ready")
                fwd_ready = sem("fwd_ready")
                zT_copied = sem("zT_copied")
                back_ready = sem("back_ready")
                back_taken = sem("back_taken")
                z_ready = sem("z_ready")
                stats_ready = sem("h_stats_ready")
                moments_ready = sem("h_moments_ready")
                var_ready = sem("h_var_ready")
                rstd_ready = sem("h_rstd_ready")
                centred = sem("centred")
                y_ready = sem("y_ready")
                y_stored = [sem(f"y_stored{i}") for i in range(2)]

                def loaded(g, par):
                    return g * 8 + (8 if par else 16)

                def run(engine, group):
                    group(0, 0, cur=True, prev=False, nxt=True)
                    group(1, 1, cur=True, prev=True, nxt=True)
                    with engine.Fori(1, GROUPS // 2 - 1) as i:
                        group(i * 2, 0, cur=True, prev=True, nxt=True)
                        group(i * 2 + 1, 1, cur=True, prev=True, nxt=True)
                    group(GROUPS - 2, 0, cur=True, prev=True, nxt=True)
                    group(GROUPS - 1, 1, cur=True, prev=True, nxt=False)
                    group(GROUPS, 0, cur=False, prev=True, nxt=False)

                block = s.enter_context(nc.Block())

                @block.sync
                def _(sp):
                    def load(g, par):
                        sp.dma_start(adj_sb[par][:, :, :], adj[g, :, :, :]).then_inc(adj_loaded[par], 16)

                    def store(g, pair):
                        sp.wait_ge(y_ready, g * 2 + pair + 1)
                        sp.dma_start(out[g, :, PAIR * pair:PAIR * (pair + 1), :], y[pair][:, :, :])\
                            .then_inc(y_stored[pair], 16)

                    load(0, 0)
                    load(1, 1)

                    def group(g, par, more):
                        if more:
                            sp.wait_ge(mask_ready, g + 1)
                            load(g + 2, par)
                        for pair in range(2):
                            store(g, pair)

                    with sp.Fori(0, GROUPS // 2 - 1) as i:
                        group(i * 2, 0, True)
                        group(i * 2 + 1, 1, True)
                    group(GROUPS - 2, 0, False)
                    group(GROUPS - 1, 1, False)
                    for pair in range(2):
                        sp.wait_ge(y_stored[pair], 16 * GROUPS)

                @block.gpsimd
                def _(pool):
                    def mask(g, par, early):
                        if not early:
                            pool.wait_ge(round_masked, (g - 1) * SLOTS)
                        wait_apart(pool, adj_loaded[par], loaded(g, par), pool_waits)
                        nc.gpsimd.tensor_scalar(fill[par][:, :, :], adj_sb[par][:, :, :], 0.0, HOP_MASK,
                                                ALU.is_equal, ALU.mult).then_inc(fill_ready, 1)
                        wait_apart(pool, fill_ready, g + 1, pool_waits)
                        nc.gpsimd.tensor_scalar(keep[par][:, :, :], fill[par][:, :, :], -1.0 / HOP_MASK, 1.0,
                                                ALU.mult, ALU.add).then_inc(mask_ready, 1)

                    def z_parts(g, par, early):
                        if not early:
                            pool.wait_ge(z_ready, (g - 1) * 2 * HOPS)
                        wait_apart(pool, z0_ready, g * 2 + 2, pool_waits)
                        nc.gpsimd.tensor_scalar(z0_part[par][:, :, :], z0[par][:, :, :], ALPHA, None, ALU.mult)\
                            .then_inc(z0_part_ready, 1)
                        pool.wait_ge(z0_part_ready, g + 1)
                        pool.wait_ge(xs_ready, g + 1)
                        nc.gpsimd.tensor_tensor(resid[par][:, :, :], xs[par][:, :, :], z0_part[par][:, :, :],
                                                ALU.add).then_inc(resid_ready, 1)

                    def root(n):
                        wait_apart(pool, moments_ready, n + 1, pool_waits)
                        nc.gpsimd.tensor_scalar(var_eps[:, :], moments[:, :, 1], EPS, None, ALU.add)\
                            .then_inc(var_ready, 1)
                        pool.wait_ge(var_ready, n + 1)
                        nc.gpsimd.tensor_tensor(rstd[:, :], var_eps[:, :], neg_half[:, 0:PAIR], ALU.pow)\
                            .then_inc(rstd_ready, 1)

                    mask(0, 0, early=True)

                    def group(g, par, cur, prev, nxt):
                        if nxt:
                            mask(g + 1, 1 - par, early=not prev)
                        if cur:
                            z_parts(g, par, early=isinstance(g, int) and g < 2)
                        if prev:
                            root((g - 1) * 2)
                            root((g - 1) * 2 + 1)

                    run(pool, group)

                @block.tensor
                def _(pe):
                    def project(g, par, chunk, first=False):
                        transpose, feature_major, node_major = pe_project(
                            pe, lin, xs[par], xsT, {"q": wq_s, "k": wk_s, "v": wv_s}, proj_ready)
                        if chunk == 0:
                            pe.wait_ge(xs_ready, g + 1)
                            if not first:
                                pe.wait_ge(z0_ready, g * 2 - 1)
                            transpose(0)
                        elif chunk == 1:
                            if not first:
                                pe.wait_ge(z0_ready, g * 2)
                            transpose(1)
                        elif chunk in (2, 3):
                            pe.wait_ge(lo_ready, g * 2 + 2)
                            feature_major("q", chunk - 2)
                        elif chunk in (4, 5):
                            pe.wait_ge(proj_copied, g * 4 + chunk - 3)
                            feature_major("k", chunk - 4)
                        else:
                            pe.wait_ge(proj_copied, g * 4 + chunk - 3)
                            node_major("v", chunk - 6)

                    def scores(g, par, slot, early):
                        if slot == 0:
                            pe.wait_ge(proj_copied, g * 4 + 4)
                        if not early:
                            pe.wait_ge(round_kept, g * SLOTS + slot - 1)
                        score_round(score_bank[slot % 2], qT[par], kT[par], slot // ROUNDS, slot % ROUNDS)\
                            .then_inc(scores_ready, 1)

                    def transpose_probs(g, unit, early):
                        graph, half = unit // 2, unit % 2
                        pair = graph // PAIR
                        if unit % 4 == 0:
                            pe.wait_ge(exp_done, g * SLOTS + ROUNDS * pair + ROUNDS)
                        if not early:
                            pe.wait_ge(pt_copied, g * SLOTS + unit - 1)
                        for c in range(4):
                            last = nc.tensor.transpose(pt_bank[unit % 2][:, c * N:(c + 1) * N],
                                                       probs[pair][:, graph % PAIR, 4 * half + c, :], ident[:, :])
                        last.then_inc(pt_ready, 1)

                    def forward(g, par, pair, hop, early):
                        n = g * 2 * HOPS + pair * HOPS + hop
                        if hop == 0:
                            pe.wait_ge(pt_copied, g * SLOTS + 4 * pair + 4)
                            pe.wait_ge(z0_ready, g * 2 + 2)
                        if not early:
                            pe.wait_ge(z_ready, n)
                            pe.wait_ge(zT_copied, n)
                        for j in range(PAIR):
                            for half in range(KH):
                                for c in range(4):
                                    h = 4 * half + c
                                    l = (z0[par][:, PAIR * pair + j, h * D:(h + 1) * D] if hop == 0
                                         else z[:, j, h * D:(h + 1) * D])
                                    last = nc.tensor.matmul(
                                        fwd_bank[D * c:D * (c + 1), (2 * j + half) * N:(2 * j + half + 1) * N],
                                        l, probsT[pair][:, 2 * j + half, c * N:(c + 1) * N],
                                        start=True, stop=True, tile_position=(0, D * c))
                        last.then_inc(fwd_ready, 1)

                    def back(g, pair, hop):
                        n = g * 2 * HOPS + pair * HOPS + hop
                        pe.wait_ge(zT_copied, n + 1)
                        for j in range(PAIR):
                            for half in range(KH):
                                last = nc.tensor.transpose(
                                    back_bank[:, j * F + half * 128:j * F + (half + 1) * 128],
                                    zT[:, j, half * N:(half + 1) * N], ident[:, :])
                        last.then_inc(back_ready, 1)

                    for chunk in range(6):
                        project(0, 0, chunk, first=True)

                    def group(g, par, cur, prev, nxt):
                        for slot in range(SLOTS):
                            pair, hop = slot // HOPS, slot % HOPS
                            if cur:
                                scores(g, par, slot, early=not prev and slot < 2)
                            if prev and slot > 0:
                                back(g - 1, (slot - 1) // HOPS, (slot - 1) % HOPS)
                            if cur and slot < 2:
                                project(g, par, 6 + slot)
                            if nxt and slot >= 3:
                                for chunk in {3: (0, 1), 4: (2, 3), 5: (4,), 6: (5,), 7: ()}[slot]:
                                    project(g + 1, 1 - par, chunk)
                            if prev and slot < 4:
                                transpose_probs(g - 1, slot + 4, early=False)
                            if cur and slot >= 4:
                                transpose_probs(g, slot - 4, early=not prev and slot < 6)
                            if prev:
                                forward(g - 1, 1 - par, pair, hop,
                                        early=isinstance(g, int) and g == 1 and slot == 0)
                        if prev:
                            back(g - 1, 1, HOPS - 1)

                    run(pe, group)

                @block.scalar
                def _(act):
                    def project(g, par, chunk, early):
                        act.wait_ge(proj_ready, g * 8 + chunk + 1)
                        if chunk < 2:
                            nc.scalar.activation(xsT[0][:, chunk, :], lin[chunk][:, :], ACT.Copy)\
                                .then_inc(hi_ready, 1)
                        elif chunk < 4:
                            if not early:
                                act.wait_ge(scores_ready, (g - 1) * SLOTS)
                            h = chunk - 2
                            nc.scalar.activation(qT[par][:, h, :], lin[h][:, :], ACT.Identity, scale=-1.0,
                                                 bias=hop_q_bias[:, h:h + 1]).then_inc(proj_copied, 1)
                        else:
                            h = chunk - 4
                            c = COLS["hop_bk"].start + h
                            nc.scalar.activation(kT[par][:, h, :], lin[h][:, :], ACT.Identity,
                                                 bias=cols[:, c:c + 1]).then_inc(proj_copied, 1)

                    def exponentials(g, slot, early):
                        pair, r = slot // ROUNDS, slot % ROUNDS
                        act.wait_ge(round_masked, g * SLOTS + slot + 1)
                        if r == 0 and not early:
                            act.wait_ge(sums_inverted, (g - 1) * 2 + pair + 1)
                        for j in range(PAIR):
                            for h in (r, r + 4):
                                last = nc.scalar.activation(
                                    probs[pair][:, j, h, :], probs[pair][:, j, h, :], ACT.Exp, scale=-1.0,
                                    bias=least[pair][:, j * H + h:j * H + h + 1],
                                    accum_out=sums[pair][:, j * H + h:j * H + h + 1])
                        last.then_inc(exp_done, 1)

                    def copy_probs(g, unit, early):
                        pair = unit // 4
                        act.wait_ge(pt_ready, g * SLOTS + unit + 1)
                        if unit % 4 == 0 and not early:
                            act.wait_ge(fwd_ready, (g - 1) * 2 * HOPS + (pair + 1) * HOPS)
                        nc.scalar.activation(probsT[pair][:, unit % 4, :], pt_bank[unit % 2][:, :], ACT.Copy)\
                            .then_inc(pt_copied, 1)

                    def copy_hop(g, pair, hop, early):
                        n = g * 2 * HOPS + pair * HOPS + hop
                        act.wait_ge(fwd_ready, n + 1)
                        if not early:
                            act.wait_ge(back_ready, n)
                        nc.scalar.activation(zT[:, :, :].rearrange("p j n -> p (j n)"), fwd_bank[:, :], ACT.Copy)\
                            .then_inc(zT_copied, 1)

                    for chunk in range(6):
                        project(0, 0, chunk, early=True)

                    def group(g, par, cur, prev, nxt):
                        for slot in range(SLOTS):
                            if cur:
                                exponentials(g, slot, early=not prev)
                            if nxt and slot >= 3:
                                for chunk in {3: (0, 1), 4: (2, 3), 5: (4,), 6: (5,), 7: ()}[slot]:
                                    project(g + 1, 1 - par, chunk, early=not prev)
                            if prev and slot < 4:
                                copy_probs(g - 1, slot + 4, early=isinstance(g, int) and g == 1)
                            if cur and slot >= 4:
                                copy_probs(g, slot - 4, early=not prev)
                            if prev:
                                copy_hop(g - 1, slot // HOPS, slot % HOPS,
                                         early=isinstance(g, int) and g == 1 and slot == 0)

                    run(act, group)

                @block.vector
                def _(dve):
                    def split(g):
                        for half in range(KH):
                            dve.wait_ge(hi_ready, g * 2 + half + 1)
                            nc.vector.tensor_tensor(xsT[1][:, half, :], lin[half][:, :],
                                                    f32(xsT[0][:, half, :]), ALU.subtract)\
                                .then_inc(lo_ready, 1)

                    def values(g, par, p, early):
                        dve.wait_ge(proj_ready, g * 8 + 7 + p)
                        if p == 0 and not early:
                            dve.wait_ge(z0_part_ready, g - 1)
                        nc.vector.tensor_tensor(
                            z0[par][:, PAIR * p:PAIR * (p + 1), :],
                            lin[p][:, :].rearrange("p (j f) -> p j f", j=PAIR),
                            row("hop_bv").unsqueeze(1).broadcast_to([128, PAIR, F]), ALU.add)\
                            .then_inc(z0_ready, 1)

                    def keep_round(g, par, slot, early):
                        pair, r = slot // ROUNDS, slot % ROUNDS
                        if slot == 0:
                            dve.wait_ge(mask_ready, g + 1)
                        if r == 0 and not early:
                            dve.wait_ge(pt_ready, (g - 1) * SLOTS + 4 * pair + 4)
                        dve.wait_ge(scores_ready, g * SLOTS + slot + 1)
                        nc.vector.tensor_tensor(
                            probs[pair][:, :, r:H:4, :],
                            score_bank[slot % 2][:, :].rearrange("p (j h n) -> p j h n", j=PAIR, h=KH),
                            keep[par][:, PAIR * pair:PAIR * (pair + 1), :].unsqueeze(2)
                            .broadcast_to([128, PAIR, KH, N]), ALU.mult).then_inc(round_kept, 1)

                    def mask_round(g, par, slot):
                        pair, r = slot // ROUNDS, slot % ROUNDS
                        wait_apart(dve, round_kept, g * SLOTS + slot + 1, dve_waits)
                        for j in range(PAIR):
                            for h in (r, r + 4):
                                last = nc.vector.tensor_tensor_reduce(
                                    out=probs[pair][:, j, h, :], in0=probs[pair][:, j, h, :],
                                    in1=fill[par][:, PAIR * pair + j, :], scale=1.0, scalar=LEAST_START,
                                    op0=ALU.add, op1=ALU.min,
                                    accum_out=least[pair][:, j * H + h:j * H + h + 1])
                        last.then_inc(round_masked, 1)

                    def invert_sums(g, pair):
                        n = g * 2 + pair
                        dve.wait_ge(exp_done, (n + 1) * ROUNDS)
                        nc.vector.reciprocal(shares[pair][:, :], sums[pair][:, :]).then_inc(sums_inverted, 1)
                        dve.wait_ge(sums_inverted, n + 1)
                        nc.vector.tensor_scalar(shares[pair][:, :], shares[pair][:, :], 1.0 - ALPHA, None,
                                                ALU.mult).then_inc(shares_ready, 1)

                    def take_hop(g, par, pair, hop):
                        n = g * 2 * HOPS + pair * HOPS + hop
                        if hop == 0:
                            dve.wait_ge(shares_ready, g * 2 + pair + 1)
                            dve.wait_ge(z0_part_ready, g + 1)
                        dve.wait_ge(back_ready, n + 1)
                        to = z if hop < HOPS - 1 else y[pair]
                        nc.vector.tensor_tensor(
                            to[:, :, :].rearrange("p j (h d) -> p (j h) d", d=D),
                            back_bank[:, :].rearrange("p (h d) -> p h d", d=D),
                            shares[pair][:, :].unsqueeze(2).broadcast_to([128, PAIR * H, D]), ALU.mult)\
                            .then_inc(back_taken, 1)

                    def add_part(g, par, pair, hop):
                        n = g * 2 * HOPS + pair * HOPS + hop
                        to = z if hop < HOPS - 1 else y[pair]
                        part = z0_part[par] if hop < HOPS - 1 else resid[par]
                        if hop == HOPS - 1:
                            dve.wait_ge(resid_ready, g + 1)
                        dve.wait_ge(back_taken, n + 1)
                        nc.vector.tensor_tensor(to[:, :, :], to[:, :, :],
                                                part[:, PAIR * pair:PAIR * (pair + 1), :], ALU.add)\
                            .then_inc(z_ready, 1)

                    def final_stats(g, pair):
                        n = g * 2 + pair
                        dve.wait_ge(z_ready, (n + 1) * HOPS)
                        for j in range(PAIR):
                            last = nc.vector.bn_stats(stats[:, j, :], y[pair][:, j, :])
                        last.then_inc(stats_ready, 1)
                        wait_apart(dve, stats_ready, n + 1, dve_waits)
                        for j in range(PAIR):
                            last = nc.vector.bn_aggr(moments[:, j, :], stats[:, j, :])
                        last.then_inc(moments_ready, 1)

                    def final_norm(g, pair):
                        n = g * 2 + pair
                        dve.wait_ge(rstd_ready, n + 1)
                        for j in range(PAIR):
                            last = nc.vector.scalar_tensor_tensor(
                                out=y[pair][:, j, :], in0=y[pair][:, j, :], scalar=moments[:, j, 0:1],
                                in1=row("gamma"), op0=ALU.subtract, op1=ALU.mult)
                        last.then_inc(centred, 1)
                        dve.wait_ge(centred, n + 1)
                        for j in range(PAIR):
                            last = nc.vector.scalar_tensor_tensor(
                                out=y[pair][:, j, :], in0=y[pair][:, j, :], scalar=rstd[:, j:j + 1],
                                in1=row("beta"), op0=ALU.mult, op1=ALU.add)
                        last.then_inc(y_ready, 1)

                    def copy_x(g, par, early):
                        if not early:
                            dve.wait_ge(resid_ready, g - 1)
                            dve.wait_ge(proj_ready, g * 8 - 14)
                        nc.vector.tensor_copy(xs[par][:, :, :].rearrange("p j f -> p (j f)"),
                                              acts[:, bass.ds(g * GF, GF)]).then_inc(xs_ready, 1)

                    copy_x(0, 0, early=True)
                    split(0)

                    def hop_step(g, par, pair, hop, first):
                        if hop == HOPS - 1 and not first:
                            dve.wait_ge(y_stored[pair], g * 16)
                        take_hop(g, par, pair, hop)

                    def group(g, par, cur, prev, nxt):
                        first = isinstance(g, int) and g == 1
                        for slot in range(SLOTS):
                            if cur:
                                keep_round(g, par, slot, early=not prev)
                            if prev and slot > 0:
                                hop_step(g - 1, 1 - par, (slot - 1) // HOPS, (slot - 1) % HOPS, first)
                                add_part(g - 1, 1 - par, (slot - 1) // HOPS, (slot - 1) % HOPS)
                            if cur:
                                mask_round(g, par, slot)
                            if prev and slot % HOPS == 0:
                                invert_sums(g - 1, slot // HOPS)
                            if prev and slot == 4:
                                final_stats(g - 1, 0)
                            if prev and slot == 5:
                                final_norm(g - 1, 0)
                            if cur and slot < 2:
                                values(g, par, slot, early=isinstance(g, int) and g < 2)
                            if nxt and slot == 1:
                                copy_x(g + 1, 1 - par, early=not prev)
                            if nxt and slot == 3:
                                split(g + 1)
                        if prev:
                            hop_step(g - 1, 1 - par, 1, HOPS - 1, first)
                            add_part(g - 1, 1 - par, 1, HOPS - 1)
                            final_stats(g - 1, 1)
                            final_norm(g - 1, 1)

                    run(dve, group)

        with mlp_stack:
            with att_stack:
                setup()
                attention_phase()
            mlp_phase()
        hop_phase()


def kernel(x, adj, L0_gnn_ln1_g, L0_gnn_ln1_b, L0_gnn_ln2_g, L0_gnn_ln2_b, L0_gnn_wq, L0_gnn_bq, L0_gnn_wk,
           L0_gnn_bk, L0_gnn_wv, L0_gnn_bv, L0_gnn_wo, L0_gnn_bo, L0_gnn_w1, L0_gnn_b1, L0_gnn_w2, L0_gnn_b2,
           L1_gnn_Wq, L1_gnn_bq, L1_gnn_Wk, L1_gnn_bk, L1_gnn_Wv, L1_gnn_bv, L1_gnn_gamma, L1_gnn_beta):
    import numpy as np
    import concourse.bacc as bacc
    from concourse.bass_utils import run_bass_kernel_spmd

    def by_group(a):
        a = np.asarray(a)
        return np.ascontiguousarray(a.reshape(GROUPS, G, N, a.shape[2]).transpose(0, 2, 1, 3))

    def columns(*vectors):
        return np.ascontiguousarray(np.concatenate([np.asarray(a).reshape(-1, 128) for a in vectors]).T)

    arrays = {
        "x_in": by_group(x),
        "adj_in": by_group(adj),
        "vec_cols": columns(L0_gnn_ln1_g, L0_gnn_ln1_b, L0_gnn_ln2_g, L0_gnn_ln2_b, L0_gnn_bq, L0_gnn_bk,
                            L0_gnn_bv, L0_gnn_b1, L1_gnn_bq, L1_gnn_bk),
        "vec_rows": np.concatenate([np.asarray(a).reshape(1, -1) for a in
                                    (L0_gnn_bo, L0_gnn_b2, L1_gnn_bv, L1_gnn_gamma, L1_gnn_beta)], axis=1),
        "wq": np.asarray(L0_gnn_wq), "wk": np.asarray(L0_gnn_wk), "wv": np.asarray(L0_gnn_wv),
        "wo": np.asarray(L0_gnn_wo), "w1": np.asarray(L0_gnn_w1), "w2": np.asarray(L0_gnn_w2),
        "hwq": np.ascontiguousarray(np.asarray(L1_gnn_Wq).T),
        "hwk": np.ascontiguousarray(np.asarray(L1_gnn_Wk).T),
        "hwv": np.ascontiguousarray(np.asarray(L1_gnn_Wv).T),
    }
    nc = bacc.Bacc("TRN2", target_bir_lowering=False, num_devices=1)
    aps = [nc.dram_tensor(n, a.shape, mybir.dt.from_np(a.dtype), kind="ExternalInput").ap()
           for n, a in arrays.items()]
    out = nc.dram_tensor("out", (GROUPS, N, G, F), F32, kind="ExternalOutput").ap()
    graph_transformer(nc, *aps, out)
    r = run_bass_kernel_spmd(nc, [arrays], core_ids=[0])
    got = r.results[0]["out"]
    return np.ascontiguousarray(got.transpose(0, 2, 1, 3)).reshape(B, N, F)
```

```python
import concourse.bass as bass
from concourse import mybir
from contextlib import ExitStack

F32 = mybir.dt.float32
F32R = mybir.dt.float32r
I32 = mybir.dt.int32
ALU = mybir.AluOpType
ACT = mybir.ActivationFunctionType

B, N, F = 64, 128, 256
H = 8
D = F // H
FF = 4 * F
G = 4
GROUPS = B // G
KH = F // 128
MC = FF // 128
GN = G * N
GF = G * F
PAIR = 2
ROUNDS = 4
SLOTS = 2 * ROUNDS
HOPS = 4
ALPHA = 0.1
EPS = 1e-5
HOP_MASK = 16384.0
FAR = 1e30
LEAST_START = 3e38
QSCALE = 1.0 / float(D) ** 0.5

COLS = {}
for _name, _n in (("ln1_g", KH), ("ln1_b", KH), ("ln2_g", KH), ("ln2_b", KH), ("bq", KH), ("bk", KH),
                  ("bv", KH), ("b1", MC), ("hop_bq", KH), ("hop_bk", KH)):
    COLS[_name] = slice(sum(s.stop - s.start for s in COLS.values()),
                        sum(s.stop - s.start for s in COLS.values()) + _n)
NCOLS = sum(s.stop - s.start for s in COLS.values())
ROWS = ["bo", "b2", "hop_bv", "gamma", "beta"]


def graph_transformer(nc, x, adj, vec_cols, vec_rows, wq, wk, wv, wo, w1, w2, hwq, hwk, hwv, out):
    outer = ExitStack()
    mlp_stack = ExitStack()
    att_stack = ExitStack()

    def sb(stack, name, shape, dt=F32):
        return stack.enter_context(nc.sbuf_tensor(name, shape, dt))

    def sem(name):
        return outer.enter_context(nc.semaphore(name))

    def f32(ap):
        return ap.bitcast(F32)

    def wait_apart(engine, semaphore, value, passed):
        engine.wait_ge(semaphore, value)
        engine.sem_inc(passed, 1)

    with outer:
        bank = [outer.enter_context(nc.psum_tensor(f"bank{i}", [128, 512], F32)) for i in range(8)]
        acts = sb(outer, "acts", [128, GROUPS * GF])
        cols = sb(outer, "cols", [128, NCOLS])
        rows = sb(outer, "rows", [128, len(ROWS), F])
        ident = sb(outer, "ident", [128, 128])
        ones = sb(outer, "ones", [128, D])
        neg_half = sb(outer, "neg_half", [128, G])
        bo_folded = sb(outer, "bo_folded", [128, F])
        b1_folded = sb(outer, "b1_folded", [128, MC])
        q_bias = sb(outer, "q_bias", [128, KH])
        k_bias = sb(outer, "k_bias", [128, KH])
        hop_q_bias = sb(outer, "hop_q_bias", [128, KH])

        def split_weight(stack, name, shape):
            return tuple(sb(stack, f"{name}_{part}", shape, F32R) for part in ("hi", "lo"))

        wq_s = split_weight(outer, "wq", [128, KH, F])
        wk_s = split_weight(outer, "wk", [128, KH, F])
        wv_s = split_weight(outer, "wv", [128, KH, F])
        w1_s = split_weight(mlp_stack, "w1", [128, KH, FF])
        w2_s = split_weight(mlp_stack, "w2", [128, MC, F])
        wo_s = split_weight(att_stack, "wo", [128, KH, F])

        def products(weight, act):
            return ((weight[0], act[0]), (weight[1], act[0]), (weight[0], act[1]))

        raw_at = [GROUPS * GF]

        def raw_weight(k, n):
            raw_at[0] -= k * n
            return acts[:, raw_at[0]:raw_at[0] + k * n].rearrange("p (k n) -> p k n", k=k)

        w1_raw, w2_raw = raw_weight(KH, FF), raw_weight(MC, F)
        mlp_loaded = [sem("w1_loaded"), sem("w2_loaded")]

        def row(name):
            return rows[:, ROWS.index(name), :]

        def setup():
            s = ExitStack()
            with s:
                vecs_loaded = sem("vecs_loaded")
                w_loaded = {n: sem(f"{n}_loaded") for n in
                            ("wq", "wk", "wv", "wo")}
                consts_ready = sem("consts_ready")
                ident_zeroed = sem("ident_zeroed")
                hi_ready = sem("hi_ready")
                lo_ready = sem("lo_ready")
                folds_ready = sem("folds_ready")
                col_biases_ready = sem("col_biases_ready")
                cv_ready = sem("cv_ready")
                cv_spread = sem("cv_spread")
                bo_product_ready = sem("bo_product_ready")
                bo_ready = sem("bo_ready")
                cv = sb(s, "cv", [128, KH])
                cv_wide = sb(s, "cv_wide", [128, KH, 128])
                drams = {"wq": wq, "wk": wk, "wv": wv, "wo": wo}
                raws = {name: raw_weight(KH, F) for name in drams}
                scaled = ("wq", "wk", "wv")
                splits = {"wq": wq_s, "wk": wk_s, "wv": wv_s, "wo": wo_s}
                fold_bank, bo_bank = bank[0], bank[1]
                fold_at = {"wq": 0, "wk": KH, "wv": 2 * KH}

                block = s.enter_context(nc.Block())

                @block.sync
                def _(sp):
                    sp.dma_start(cols[:, :], vec_cols).then_inc(vecs_loaded, 16)
                    sp.dma_start(rows[:, :, :].rearrange("p r n -> p (r n)"),
                                 vec_rows.broadcast_to([128, len(ROWS) * F])).then_inc(vecs_loaded, 16)
                    for name in drams:
                        sp.dma_start(raws[name], drams[name].rearrange("(k p) n -> p k n", p=128))\
                            .then_inc(w_loaded[name], 16)

                @block.scalar
                def _(act):
                    for raw, w, loaded in zip((w1_raw, w2_raw), (w1, w2), mlp_loaded):
                        act.dma_start(raw, w.rearrange("(k p) n -> p k n", p=128)).then_inc(loaded, 16)

                @block.gpsimd
                def _(pool):
                    nc.gpsimd.memset(ident[:, :], 0.0).then_inc(ident_zeroed, 1)
                    pool.wait_ge(ident_zeroed, 1)
                    nc.gpsimd.affine_select(out=ident[:, :], in_=ident[:, :], compare_op=ALU.not_equal,
                                            fill=1.0, base=0, pattern=[[-1, 128]], channel_multiplier=1)\
                        .then_inc(consts_ready, 1)
                    nc.gpsimd.memset(ones[:, :], 1.0).then_inc(consts_ready, 1)
                    nc.gpsimd.memset(neg_half[:, :], -0.5).then_inc(consts_ready, 1)

                @block.tensor
                def _(pe):
                    pe.wait_ge(vecs_loaded, 32)
                    for name in fold_at:
                        pe.wait_ge(w_loaded[name], 16)
                        for m in range(KH):
                            c = fold_at[name] + m
                            for k in range(KH):
                                b = COLS["ln1_b"].start + k
                                last = nc.tensor.matmul(
                                    fold_bank[:, c:c + 1], raws[name][:, k, m * 128:(m + 1) * 128],
                                    cols[:, b:b + 1], start=(k == 0), stop=(k == KH - 1))
                    last.then_inc(folds_ready, 1)
                    pe.wait_ge(cv_spread, 1)
                    pe.wait_ge(w_loaded["wo"], 16)
                    for k in range(KH):
                        last = nc.tensor.matmul(bo_bank[:, 0:F], cv_wide[:, k, :], raws["wo"][:, k, :],
                                                start=(k == 0), stop=(k == KH - 1))
                    last.then_inc(bo_product_ready, 1)

                @block.vector
                def _(dve):
                    dve.wait_ge(vecs_loaded, 32)
                    done = 0
                    for name in drams:
                        dve.wait_ge(w_loaded[name], 16)
                        hi, lo = splits[name]
                        for k in range(KH):
                            if name in scaled:
                                c = COLS["ln1_g"].start + k
                                gain = cols[:, c:c + 1]
                            else:
                                gain = 1.0
                            nc.vector.tensor_scalar(hi[:, k, :], raws[name][:, k, :], gain, None, ALU.mult)\
                                .then_inc(hi_ready, 1)
                            done += 1
                            dve.wait_ge(hi_ready, done)
                            nc.vector.scalar_tensor_tensor(
                                out=lo[:, k, :], in0=raws[name][:, k, :], scalar=gain,
                                in1=f32(hi[:, k, :]), op0=ALU.mult, op1=ALU.subtract).then_inc(lo_ready, 1)
                    dve.wait_ge(folds_ready, 1)
                    nc.vector.tensor_tensor(cv[:, :], fold_bank[:, fold_at["wv"]:fold_at["wv"] + KH],
                                            cols[:, COLS["bv"]], ALU.add).then_inc(cv_ready, 1)
                    dve.wait_ge(cv_ready, 1)
                    nc.vector.tensor_copy(cv_wide[:, :, :], cv[:, :].unsqueeze(2).broadcast_to([128, KH, 128]))\
                        .then_inc(cv_spread, 1)
                    nc.vector.tensor_tensor(q_bias[:, :], fold_bank[:, fold_at["wq"]:fold_at["wq"] + KH],
                                            cols[:, COLS["bq"]], ALU.add).then_inc(col_biases_ready, 1)
                    nc.vector.tensor_tensor(k_bias[:, :], fold_bank[:, fold_at["wk"]:fold_at["wk"] + KH],
                                            cols[:, COLS["bk"]], ALU.add)
                    nc.vector.tensor_scalar(hop_q_bias[:, :], cols[:, COLS["hop_bq"]], -1.0, None, ALU.mult)
                    dve.wait_ge(col_biases_ready, 1)
                    nc.vector.tensor_scalar(q_bias[:, :], q_bias[:, :], -QSCALE, None, ALU.mult)
                    dve.wait_ge(bo_product_ready, 1)
                    nc.vector.tensor_tensor(bo_folded[:, :], bo_bank[:, 0:F], row("bo"), ALU.add)\
                        .then_inc(bo_ready, 1)
                    dve.wait_ge(bo_ready, 1)

        def pe_project(pe, lin, xn, act_s, weights, proj_ready):
            def transpose(half):
                for j in range(G):
                    last = nc.tensor.transpose(lin[half][:, j * N:(j + 1) * N],
                                               xn[:, j, half * 128:(half + 1) * 128], ident[:, :])
                last.then_inc(proj_ready, 1)

            def feature_major(which, half):
                todo = [(k, w, a) for k in range(KH) for w, a in products(weights[which], act_s)]
                for n, (k, w, a) in enumerate(todo):
                    last = nc.tensor.matmul(lin[half][:, :], w[:, k, half * 128:(half + 1) * 128],
                                            a[:, k, :], start=(n == 0), stop=(n == len(todo) - 1))
                last.then_inc(proj_ready, 1)

            def node_major(which, pair):
                for j in range(PAIR):
                    g = PAIR * pair + j
                    todo = [(k, w, a) for k in range(KH) for w, a in products(weights[which], act_s)]
                    for n, (k, w, a) in enumerate(todo):
                        last = nc.tensor.matmul(lin[pair][:, j * F:(j + 1) * F],
                                                a[:, k, g * N:(g + 1) * N], w[:, k, :],
                                                start=(n == 0), stop=(n == len(todo) - 1))
                last.then_inc(proj_ready, 1)

            return transpose, feature_major, node_major

        def score_round(score_bank, qT, kT, pair, r):
            for j in range(PAIR):
                cols_ = slice((PAIR * pair + j) * N, (PAIR * pair + j + 1) * N)
                for half in range(KH):
                    last = nc.tensor.matmul(
                        score_bank[:, (2 * j + half) * N:(2 * j + half + 1) * N],
                        qT[D * r:D * (r + 1), half, cols_], kT[D * r:D * (r + 1), half, cols_],
                        start=True, stop=True)
            return last

        def attention_phase():
            s = ExitStack()
            with s:
                xin = [sb(s, f"xin{i}", [128, G, F]) for i in range(2)]
                adj_sb = [sb(s, f"adj_sb{i}", [128, G, N], I32) for i in range(2)]
                bias = [sb(s, f"bias{i}", [128, G, N]) for i in range(2)]
                edge = sb(s, "edge", [128, G, N])
                stats = sb(s, "stats", [128, G, 6])
                moments = sb(s, "moments", [128, G, 2])
                var_eps = sb(s, "var_eps", [128, G])
                rstd = sb(s, "rstd", [128, G])
                xn = sb(s, "xn", [128, G, F])
                xnT = tuple(sb(s, f"xnT_{p}", [128, KH, GN], F32R) for p in ("hi", "lo"))
                qT = [sb(s, f"qT{i}", [128, KH, GN]) for i in range(2)]
                kT = [sb(s, f"kT{i}", [128, KH, GN]) for i in range(2)]
                v = [sb(s, f"v{i}", [128, G, F]) for i in range(2)]
                probs = [sb(s, f"probs{i}", [128, PAIR, H, N]) for i in range(2)]
                least = [sb(s, f"least{i}", [128, PAIR, H]) for i in range(2)]
                probsT = [sb(s, f"probsT{i}", [128, 4 * N]) for i in range(2)]
                sums = [sb(s, f"sums{i}", [128, PAIR * H]) for i in range(2)]
                inverse = sb(s, "inverse", [128, PAIR * H])
                inverse_wide = sb(s, "inverse_wide", [128, PAIR, F])
                inverseT = sb(s, "inverseT", [128, PAIR, KH * N])
                att = sb(s, "att", [128, KH * N])
                attT = tuple([sb(s, f"attT{i}_{p}", [128, PAIR, KH * N], F32R) for i in range(2)]
                             for p in ("hi", "lo"))
                score_bank, pt_bank, lin = bank[0:2], bank[2:4], bank[4:6]
                pv_bank, wo_bank = bank[6], bank[7]

                x_loaded = [sem(f"x_loaded{i}") for i in range(2)]
                mlp_hi_ready = sem("mlp_hi_ready")
                mlp_split = sem("mlp_split")
                fold_ready = sem("b1_fold_ready")
                b1_ready = sem("b1_ready")
                dve_waits = sem("dve_waits")
                pool_waits = sem("pool_waits")
                adj_loaded = [sem(f"adj_loaded{i}") for i in range(2)]
                bias_parts = sem("bias_parts")
                bias_ready = sem("bias_ready")
                resid_ready = sem("resid_ready")
                stats_ready = sem("stats_ready")
                moments_ready = sem("moments_ready")
                var_ready = sem("var_ready")
                rstd_ready = sem("rstd_ready")
                normed = sem("normed")
                proj_ready = sem("proj_ready")
                hi_ready = sem("xnT_hi_ready")
                lo_ready = sem("xnT_lo_ready")
                proj_copied = sem("proj_copied")
                v_copied = sem("v_copied")
                scores_ready = sem("scores_ready")
                round_masked = sem("round_masked")
                exp_done = sem("exp_done")
                pt_ready = sem("pt_ready")
                pt_copied = sem("pt_copied")
                pv_ready = sem("pv_ready")
                sums_inverted = sem("a_sums_inverted")
                inverse_widened = sem("inverse_widened")
                spread_ready = sem("spread_ready")
                spread_copied = sem("spread_copied")
                att_taken = sem("att_taken")
                att_hi_ready = sem("att_hi_ready")
                att_split = sem("att_split")
                wo_ready = sem("wo_ready")
                x1_added = sem("x1_added")

                def loaded(g, par):
                    return g * 8 + (8 if par else 16)

                def run(engine, group):
                    group(0, 0, cur=True, prev=False, nxt=True)
                    group(1, 1, cur=True, prev=True, nxt=True)
                    with engine.Fori(1, GROUPS // 2 - 1) as i:
                        group(i * 2, 0, cur=True, prev=True, nxt=True)
                        group(i * 2 + 1, 1, cur=True, prev=True, nxt=True)
                    group(GROUPS - 2, 0, cur=True, prev=True, nxt=True)
                    group(GROUPS - 1, 1, cur=True, prev=True, nxt=False)
                    group(GROUPS, 0, cur=False, prev=True, nxt=False)

                block = s.enter_context(nc.Block())

                @block.sync
                def _(sp):
                    def load(g, par):
                        sp.dma_start(xin[par][:, :, :], x[g, :, :, :]).then_inc(x_loaded[par], 16)
                        sp.dma_start(adj_sb[par][:, :, :], adj[g, :, :, :]).then_inc(adj_loaded[par], 16)

                    load(0, 0)
                    load(1, 1)
                    with sp.Fori(0, GROUPS // 2 - 1) as i:
                        for par in range(2):
                            g = i * 2 + par
                            sp.wait_ge(bias_ready, g + 1)
                            sp.wait_ge(resid_ready, g + 1)
                            sp.wait_ge(normed, g + 1)
                            load(g + 2, par)

                @block.gpsimd
                def _(pool):
                    def root(g):
                        wait_apart(pool, moments_ready, g + 1, pool_waits)
                        nc.gpsimd.tensor_scalar(var_eps[:, :], moments[:, :, 1], EPS, None, ALU.add)\
                            .then_inc(var_ready, 1)
                        pool.wait_ge(var_ready, g + 1)
                        nc.gpsimd.tensor_tensor(rstd[:, :], var_eps[:, :], neg_half[:, :], ALU.pow)\
                            .then_inc(rstd_ready, 1)

                    def mask(g, par, early):
                        if not early:
                            pool.wait_ge(round_masked, (g - 1) * SLOTS)
                        wait_apart(pool, adj_loaded[par], loaded(g, par), pool_waits)
                        nc.gpsimd.tensor_scalar(edge[:, :, :], adj_sb[par][:, :, :], 0.0, -ALPHA,
                                                ALU.max, ALU.mult).then_inc(bias_parts, 1)
                        nc.gpsimd.tensor_scalar(bias[par][:, :, :], adj_sb[par][:, :, :], 0.0, None,
                                                ALU.max).then_inc(bias_parts, 1)
                        pool.wait_ge(bias_parts, g * 4 + 2)
                        nc.gpsimd.tensor_tensor(edge[:, :, :], edge[:, :, :], bias[par][:, :, :], ALU.mult)\
                            .then_inc(bias_parts, 1)
                        wait_apart(pool, bias_parts, g * 4 + 3, pool_waits)
                        nc.gpsimd.tensor_scalar(bias[par][:, :, :], adj_sb[par][:, :, :], 0.0, FAR,
                                                ALU.is_le, ALU.mult).then_inc(bias_parts, 1)
                        pool.wait_ge(bias_parts, g * 4 + 4)
                        nc.gpsimd.tensor_tensor(bias[par][:, :, :], bias[par][:, :, :], edge[:, :, :], ALU.add)\
                            .then_inc(bias_ready, 1)
                        pool.wait_ge(bias_ready, g + 1)

                    def residual(g, par):
                        pool.wait_ge(x_loaded[par], loaded(g, par))
                        nc.gpsimd.tensor_tensor(
                            acts[:, bass.ds(g * GF, GF)].rearrange("p (j f) -> p j f", j=G),
                            xin[par][:, :, :], bo_folded[:, :].unsqueeze(1).broadcast_to([128, G, F]),
                            ALU.add).then_inc(resid_ready, 1)

                    root(0)
                    mask(0, 0, early=True)

                    def group(g, par, cur, prev, nxt):
                        if nxt:
                            root(g + 1)
                            mask(g + 1, 1 - par, early=not prev)
                        if cur:
                            residual(g, par)

                    run(pool, group)

                @block.tensor
                def _(pe):
                    transpose, feature_major, node_major = pe_project(
                        pe, lin, xn, xnT, {"q": wq_s, "k": wk_s, "v": wv_s}, proj_ready)

                    def project(g, chunk, first=False):
                        if chunk == 0:
                            pe.wait_ge(normed, g + 1)
                            if not first:
                                pe.wait_ge(v_copied, g * 2 - 1)
                            transpose(0)
                        elif chunk == 1:
                            if not first:
                                pe.wait_ge(v_copied, g * 2)
                            transpose(1)
                        elif chunk in (2, 3):
                            pe.wait_ge(lo_ready, g * 2 + 2)
                            feature_major("q", chunk - 2)
                        elif chunk in (4, 5):
                            pe.wait_ge(proj_copied, g * 4 + chunk - 3)
                            feature_major("k", chunk - 4)
                        else:
                            pe.wait_ge(proj_copied, g * 4 + chunk - 3)
                            node_major("v", chunk - 6)

                    def scores(g, par, slot, early):
                        if slot == 0:
                            pe.wait_ge(proj_copied, g * 4 + 4)
                        if not early:
                            pe.wait_ge(round_masked, g * SLOTS + slot - 1)
                        score_round(score_bank[slot % 2], qT[par], kT[par], slot // ROUNDS, slot % ROUNDS)\
                            .then_inc(scores_ready, 1)

                    def transpose_probs(g, unit, early):
                        graph, half = unit // 2, unit % 2
                        pair = graph // PAIR
                        if unit % 4 == 0:
                            pe.wait_ge(exp_done, g * SLOTS + ROUNDS * pair + ROUNDS)
                        if not early:
                            pe.wait_ge(pt_copied, g * SLOTS + unit - 1)
                        for c in range(4):
                            last = nc.tensor.transpose(pt_bank[unit % 2][:, c * N:(c + 1) * N],
                                                       probs[pair][:, graph % PAIR, 4 * half + c, :], ident[:, :])
                        last.then_inc(pt_ready, 1)

                    def weigh(g, par, unit, early):
                        graph, half = unit // 2, unit % 2
                        if unit == 0:
                            pe.wait_ge(v_copied, g * 2 + 2)
                        pe.wait_ge(pt_copied, g * SLOTS + unit + 1)
                        if half == 0 and not early:
                            pe.wait_ge(att_taken, g * G + graph)
                        for c in range(4):
                            h = 4 * half + c
                            last = nc.tensor.matmul(
                                pv_bank[D * c:D * (c + 1), half * N:(half + 1) * N],
                                v[par][:, graph, h * D:(h + 1) * D], probsT[unit % 2][:, c * N:(c + 1) * N],
                                start=True, stop=True, tile_position=(0, D * c))
                        last.then_inc(pv_ready, 1)

                    def fold_mlp_shift():
                        pe.wait_ge(mlp_loaded[0], 16)
                        for m in range(MC):
                            for k in range(KH):
                                b = COLS["ln2_b"].start + k
                                last = nc.tensor.matmul(wo_bank[:, m:m + 1], w1_raw[:, k, m * 128:(m + 1) * 128],
                                                        cols[:, b:b + 1], start=(k == 0), stop=(k == KH - 1))
                        last.then_inc(fold_ready, 1)

                    def spread(g, pair, early):
                        pe.wait_ge(inverse_widened, g * 2 + pair + 1)
                        if not early:
                            pe.wait_ge(x1_added, g * 2 - 1 + pair)
                        elif pair == 0:
                            pe.wait_ge(b1_ready, 1)
                        for j in range(PAIR):
                            for half in range(KH):
                                last = nc.tensor.transpose(
                                    wo_bank[:, (2 * j + half) * N:(2 * j + half + 1) * N],
                                    inverse_wide[:, j, half * 128:(half + 1) * 128], ident[:, :])
                        last.then_inc(spread_ready, 1)

                    def output(g, pair, more):
                        pe.wait_ge(att_split, g * G + PAIR * (pair + 1))
                        if pair == 0 or more:
                            pe.wait_ge(spread_copied, g * 2 + 2 + pair)
                        else:
                            pe.wait_ge(x1_added, g * 2 + 1)
                        for j in range(PAIR):
                            todo = [(k, w, a) for k in range(KH)
                                    for w, a in products(wo_s, (attT[0][pair], attT[1][pair]))]
                            for n, (k, w, a) in enumerate(todo):
                                last = nc.tensor.matmul(wo_bank[:, j * F:(j + 1) * F],
                                                        a[:, j, k * N:(k + 1) * N], w[:, k, :],
                                                        start=(n == 0), stop=(n == len(todo) - 1))
                        last.then_inc(wo_ready, 1)

                    for chunk in range(6):
                        project(0, chunk, first=True)

                    def group(g, par, cur, prev, nxt):
                        for slot in range(SLOTS):
                            if cur:
                                scores(g, par, slot, early=not prev and slot < 2)
                                if slot < 2:
                                    project(g, 6 + slot)
                            if nxt and slot >= 3:
                                for chunk in {3: (0, 1), 4: (2, 3), 5: (4,), 6: (5,), 7: ()}[slot]:
                                    project(g + 1, chunk)
                            if prev and slot < 4:
                                transpose_probs(g - 1, slot + 4, early=False)
                            if cur and slot >= 4:
                                transpose_probs(g, slot - 4, early=not prev and slot < 6)
                            if prev and slot < 5:
                                weigh(g - 1, 1 - par, slot + 3, early=False)
                            if cur and slot >= 5:
                                weigh(g, par, slot - 5, early=not prev and slot == 5)
                            if cur and not prev and slot == 2:
                                fold_mlp_shift()
                            if prev and slot == 1:
                                spread(g - 1, 1, early=isinstance(g, int) and g == 1)
                            if cur and slot == 5:
                                spread(g, 0, early=not prev)
                            if prev and slot == 2:
                                output(g - 1, 0, more=cur)
                            if prev and slot == 6:
                                output(g - 1, 1, more=cur)

                    run(pe, group)

                @block.scalar
                def _(act):
                    def project(g, par, chunk, early):
                        act.wait_ge(proj_ready, g * 8 + chunk + 1)
                        if chunk < 2:
                            nc.scalar.activation(xnT[0][:, chunk, :], lin[chunk][:, :], ACT.Copy)\
                                .then_inc(hi_ready, 1)
                        elif chunk < 4:
                            if not early:
                                act.wait_ge(scores_ready, (g - 1) * SLOTS)
                            h = chunk - 2
                            nc.scalar.activation(qT[par][:, h, :], lin[h][:, :], ACT.Identity,
                                                 scale=-QSCALE, bias=q_bias[:, h:h + 1])\
                                .then_inc(proj_copied, 1)
                        else:
                            h = chunk - 4
                            nc.scalar.activation(kT[par][:, h, :], lin[h][:, :], ACT.Identity,
                                                 bias=k_bias[:, h:h + 1]).then_inc(proj_copied, 1)

                    def exponentials(g, slot, early):
                        pair, r = slot // ROUNDS, slot % ROUNDS
                        act.wait_ge(round_masked, g * SLOTS + slot + 1)
                        if r == 0 and not early:
                            act.wait_ge(sums_inverted, (g - 1) * 2 + pair + 1)
                        for j in range(PAIR):
                            for h in (r, r + 4):
                                last = nc.scalar.activation(probs[pair][:, j, h, :], probs[pair][:, j, h, :],
                                                            ACT.Exp, scale=-1.0,
                                                            bias=least[pair][:, j, h:h + 1],
                                                            accum_out=sums[pair][:, j * H + h:j * H + h + 1])
                        last.then_inc(exp_done, 1)

                    def copy_spread(g, pair, early):
                        if not early:
                            act.wait_ge(att_taken, g * G + PAIR * pair)
                        act.wait_ge(spread_ready, g * 2 + pair + 1)
                        nc.scalar.activation(inverseT[:, :, :].rearrange("p j n -> p (j n)"),
                                             wo_bank[:, :], ACT.Copy).then_inc(spread_copied, 1)

                    def copy_probs(g, unit, early):
                        act.wait_ge(pt_ready, g * SLOTS + unit + 1)
                        if not early:
                            act.wait_ge(pv_ready, g * SLOTS + unit - 1)
                        nc.scalar.activation(probsT[unit % 2][:, :], pt_bank[unit % 2][:, :], ACT.Copy)\
                            .then_inc(pt_copied, 1)

                    for chunk in range(6):
                        project(0, 0, chunk, early=True)

                    def group(g, par, cur, prev, nxt):
                        for slot in range(SLOTS):
                            if cur and slot > 0:
                                exponentials(g, slot - 1, early=not prev)
                            if prev and slot == 0:
                                exponentials(g - 1, SLOTS - 1, early=False)
                            if nxt and slot >= 3:
                                for chunk in {3: (0, 1), 4: (2, 3), 5: (4,), 6: (5,), 7: ()}[slot]:
                                    project(g + 1, 1 - par, chunk, early=not prev)
                            if prev and slot < 4:
                                copy_probs(g - 1, slot + 4, early=False)
                            if cur and slot >= 4:
                                copy_probs(g, slot - 4, early=not prev and slot < 6)
                            if prev and slot == 1:
                                copy_spread(g - 1, 1, early=False)
                            if cur and slot == 5:
                                copy_spread(g, 0, early=not prev)

                    run(act, group)

                @block.vector
                def _(dve):
                    def norm_stats(g, par):
                        dve.wait_ge(x_loaded[par], loaded(g, par))
                        for j in range(G):
                            last = nc.vector.bn_stats(stats[:, j, :], xin[par][:, j, :])
                        last.then_inc(stats_ready, 1)
                        wait_apart(dve, stats_ready, g + 1, dve_waits)
                        for j in range(G):
                            last = nc.vector.bn_aggr(moments[:, j, :], stats[:, j, :])
                        last.then_inc(moments_ready, 1)

                    def normalise(g, par, early):
                        dve.wait_ge(rstd_ready, g + 1)
                        if not early:
                            dve.wait_ge(proj_ready, g * 8 - 6)
                        for j in range(G):
                            last = nc.vector.tensor_scalar(xn[:, j, :], xin[par][:, j, :],
                                                           moments[:, j, 0:1], rstd[:, j:j + 1],
                                                           ALU.subtract, ALU.mult)
                        last.then_inc(normed, 1)

                    def split(g):
                        for half in range(KH):
                            dve.wait_ge(hi_ready, g * 2 + half + 1)
                            nc.vector.tensor_tensor(xnT[1][:, half, :], lin[half][:, :],
                                                    f32(xnT[0][:, half, :]), ALU.subtract)\
                                .then_inc(lo_ready, 1)

                    def mask_round(g, par, slot, early):
                        pair, r = slot // ROUNDS, slot % ROUNDS
                        if slot == 0:
                            dve.wait_ge(bias_ready, g + 1)
                        if r == 0 and not early:
                            dve.wait_ge(pt_ready, (g - 1) * SLOTS + 4 * pair + 4)
                        wait_apart(dve, scores_ready, g * SLOTS + slot + 1, dve_waits)
                        for j in range(PAIR):
                            for half in range(KH):
                                h = r + 4 * half
                                last = nc.vector.tensor_tensor_reduce(
                                    out=probs[pair][:, j, h, :],
                                    in0=score_bank[slot % 2][:, (2 * j + half) * N:(2 * j + half + 1) * N],
                                    in1=bias[par][:, PAIR * pair + j, :], scale=1.0, scalar=LEAST_START,
                                    op0=ALU.add, op1=ALU.min, accum_out=least[pair][:, j, h:h + 1])
                        last.then_inc(round_masked, 1)

                    def values(g, par, p, early):
                        dve.wait_ge(proj_ready, g * 8 + 7 + p)
                        if p == 0 and not early:
                            dve.wait_ge(pv_ready, (g - 1) * SLOTS)
                        nc.vector.tensor_copy(
                            v[par][:, PAIR * p:PAIR * (p + 1), :].rearrange("p j f -> p (j f)"),
                            lin[p][:, :]).then_inc(v_copied, 1)

                    def invert_sums(g, pair, early):
                        dve.wait_ge(exp_done, g * SLOTS + ROUNDS * (pair + 1))
                        nc.vector.reciprocal(inverse[:, :], sums[pair][:, :]).then_inc(sums_inverted, 1)
                        if not early:
                            dve.wait_ge(spread_ready, g * 2 + pair)
                        dve.wait_ge(sums_inverted, g * 2 + pair + 1)
                        nc.vector.tensor_copy(
                            inverse_wide[:, :, :].rearrange("p j (h d) -> p (j h) d", d=D),
                            inverse[:, :].unsqueeze(2).broadcast_to([128, PAIR * H, D]))\
                            .then_inc(inverse_widened, 1)

                    def split_mlp_weights(parts):
                        for n in parts:
                            raw, (hi, lo), k = (w1_raw, w1_s, n) if n < KH else (w2_raw, w2_s, n - KH)
                            dve.wait_ge(mlp_loaded[0 if n < KH else 1], 16)
                            c = COLS["ln2_g"].start + k
                            gain = cols[:, c:c + 1] if n < KH else 1.0
                            nc.vector.tensor_scalar(hi[:, k, :], raw[:, k, :], gain, None, ALU.mult)\
                                .then_inc(mlp_hi_ready, 1)
                            dve.wait_ge(mlp_hi_ready, n + 1)
                            nc.vector.scalar_tensor_tensor(
                                out=lo[:, k, :], in0=raw[:, k, :], scalar=gain, in1=f32(hi[:, k, :]),
                                op0=ALU.mult, op1=ALU.subtract).then_inc(mlp_split, 1)

                    def take_attention(g, graph, early):
                        pair, j = graph // PAIR, graph % PAIR
                        n = g * G + graph
                        dve.wait_ge(spread_copied, g * 2 + pair + 1)
                        if not (isinstance(n, int) and n == 0):
                            dve.wait_ge(att_split, n)
                        dve.wait_ge(pv_ready, n * 2 + 2)
                        nc.vector.tensor_tensor(att[:, :], pv_bank[:, 0:KH * N], inverseT[:, j, :],
                                                ALU.mult).then_inc(att_taken, 1)
                        dve.wait_ge(att_taken, n + 1)
                        if j == 0 and not early:
                            dve.wait_ge(wo_ready, g * 2 + pair - 1)
                        nc.vector.tensor_copy(attT[0][pair][:, j, :], att[:, :]).then_inc(att_hi_ready, 1)
                        dve.wait_ge(att_hi_ready, n + 1)
                        nc.vector.tensor_tensor(attT[1][pair][:, j, :], att[:, :], f32(attT[0][pair][:, j, :]),
                                                ALU.subtract).then_inc(att_split, 1)

                    def add_output(g, pair):
                        dve.wait_ge(wo_ready, g * 2 + pair + 1)
                        if pair == 0:
                            dve.wait_ge(resid_ready, g + 1)
                        where = acts[:, bass.ds(g * GF + pair * PAIR * F, PAIR * F)]
                        nc.vector.tensor_tensor(where, wo_bank[:, :], where, ALU.add).then_inc(x1_added, 1)

                    norm_stats(0, 0)
                    normalise(0, 0, early=True)
                    split(0)

                    def group(g, par, cur, prev, nxt):
                        for slot in range(SLOTS):
                            if prev and slot in (1, 3, 5):
                                take_attention(g - 1, {1: 1, 3: 2, 5: 3}[slot],
                                               early=isinstance(g, int) and g == 1)
                            if cur and slot == 7:
                                take_attention(g, 0, early=not prev)
                            if cur:
                                mask_round(g, par, slot, early=not prev)
                            if nxt and slot == 0:
                                norm_stats(g + 1, 1 - par)
                            if nxt and slot == 2:
                                normalise(g + 1, 1 - par, early=False)
                            if prev and slot == 0:
                                invert_sums(g - 1, 1, early=False)
                            if cur and slot == 4:
                                invert_sums(g, 0, early=not prev)
                            if cur and slot < 2:
                                values(g, par, slot, early=isinstance(g, int) and g < 2)
                            if nxt and slot == 3:
                                split(g + 1)
                            if cur and not prev and slot in (1, 2, 4, 5, 6):
                                split_mlp_weights({1: (0,), 2: (1,), 4: (2, 3, 4), 5: (5, 6), 6: (7, 8, 9)}[slot])
                            if cur and not prev and slot == 3:
                                dve.wait_ge(fold_ready, 1)
                                nc.vector.tensor_tensor(b1_folded[:, :], wo_bank[:, 0:MC], cols[:, COLS["b1"]],
                                                        ALU.add).then_inc(b1_ready, 1)
                            if prev and slot == 3:
                                add_output(g - 1, 0)
                            if prev and slot == 7:
                                add_output(g - 1, 1)

                    run(dve, group)

        def mlp_phase():
            s = ExitStack()
            with s:
                RING = 4
                stats = sb(s, "m_stats", [128, G, 6])
                moments = sb(s, "m_moments", [128, G, 2])
                var_eps = sb(s, "m_var_eps", [128, G])
                rstd = sb(s, "m_rstd", [128, G])
                xn = sb(s, "m_xn", [128, G, F])
                xnT = tuple(sb(s, f"m_xnT_{p}", [128, KH, GN], F32R) for p in ("hi", "lo"))
                hid = [sb(s, f"hid{i}", [128, GN]) for i in range(RING)]
                hid_hi = [sb(s, f"hid_hi{i}", [128, GN], F32R) for i in range(RING)]
                hid_lo = [sb(s, f"hid_lo{i}", [128, GN], F32R) for i in range(RING)]
                raw = [sb(s, f"raw{i}", [128, KH, F]) for i in range(3)]
                up, tr, acc = bank[0:4], bank[4:6], bank[6:8]

                raw_loaded = [sem(f"raw_loaded{i}") for i in range(3)]
                raw_hi_ready = sem("raw_hi_ready")
                raw_split = sem("raw_split")

                dve_waits = sem("m_dve_waits")
                pool_waits = sem("m_pool_waits")
                stats_ready = sem("m_stats_ready")
                moments_ready = sem("m_moments_ready")
                var_ready = sem("m_var_ready")
                rstd_ready = sem("m_rstd_ready")
                normed = sem("m_normed")
                t_ready = sem("m_t_ready")
                hi_ready = sem("m_hi_ready")
                lo_ready = sem("m_lo_ready")
                up_ready = sem("up_ready")
                gelu_done = sem("gelu_done")
                hid_hi_ready = sem("hid_hi_ready")
                hid_split = sem("hid_split")
                down_done = sem("down_done")
                b2_added = sem("b2_added")
                x2_added = sem("x2_added")

                def run(engine, group):
                    group(0, prev=False, nxt=True)
                    with engine.Fori(1, GROUPS - 1) as g:
                        group(g, prev=True, nxt=True)
                    group(GROUPS - 1, prev=True, nxt=False)

                def group_acts(g):
                    return acts[:, bass.ds(g * GF, GF)]

                block = s.enter_context(nc.Block())

                @block.sync
                def _(sp):
                    for i, w in enumerate((hwq, hwk, hwv)):
                        sp.dma_start(raw[i][:, :, :], w.rearrange("(k p) n -> p k n", p=128))\
                            .then_inc(raw_loaded[i], 16)

                @block.gpsimd
                def _(pool):
                    def root(g):
                        wait_apart(pool, moments_ready, g + 1, pool_waits)
                        nc.gpsimd.tensor_scalar(var_eps[:, :], moments[:, :, 1], EPS, None, ALU.add)\
                            .then_inc(var_ready, 1)
                        pool.wait_ge(var_ready, g + 1)
                        nc.gpsimd.tensor_tensor(rstd[:, :], var_eps[:, :], neg_half[:, :], ALU.pow)\
                            .then_inc(rstd_ready, 1)

                    root(0)

                    def group(g, prev, nxt):
                        pool.wait_ge(normed, g + 1)
                        where = group_acts(g).rearrange("p (j f) -> p j f", j=G)
                        nc.gpsimd.tensor_tensor(where, where, row("b2").unsqueeze(1).broadcast_to([128, G, F]),
                                                ALU.add).then_inc(b2_added, 1)
                        if nxt:
                            root(g + 1)

                    run(pool, group)

                @block.tensor
                def _(pe):
                    def transpose(g):
                        pe.wait_ge(normed, g + 1)
                        for half in range(KH):
                            for j in range(G):
                                last = nc.tensor.transpose(tr[half][:, j * N:(j + 1) * N],
                                                           xn[:, j, half * 128:(half + 1) * 128], ident[:, :])
                            last.then_inc(t_ready, 1)

                    def up_chunk(g, m, early):
                        if m == 0:
                            pe.wait_ge(lo_ready, g * 2 + 2)
                        if not early:
                            pe.wait_ge(gelu_done, g * MC + m - RING + 1)
                        todo = [(k, w, a) for k in range(KH) for w, a in products(w1_s, xnT)]
                        for n, (k, w, a) in enumerate(todo):
                            last = nc.tensor.matmul(up[m % RING][:, :], w[:, k, m * 128:(m + 1) * 128],
                                                    a[:, k, :], start=(n == 0), stop=(n == len(todo) - 1))
                        last.then_inc(up_ready, 1)

                    def down_chunk(g, m, early):
                        pe.wait_ge(hid_split, g * MC + m + 1)
                        if m == 0 and not early:
                            pe.wait_ge(x2_added, g * 2)
                        r = m % RING
                        for j in range(G):
                            for n, (w, a) in enumerate(products(w2_s, (hid_hi[r], hid_lo[r]))):
                                last = nc.tensor.matmul(
                                    acc[j // 2][:, (j % 2) * F:(j % 2 + 1) * F], a[:, j * N:(j + 1) * N],
                                    w[:, m, :], start=(m == 0 and n == 0 and j % 2 == 0),
                                    stop=(m == MC - 1 and n == 2), skip_group_check=True)
                        last.then_inc(down_done, 1)

                    transpose(0)

                    def group(g, prev, nxt):
                        for m in range(MC):
                            up_chunk(g, m, early=not prev and m < RING)
                            if m >= 2:
                                down_chunk(g, m - 2, early=not prev)
                        if nxt:
                            transpose(g + 1)
                        for m in (MC - 2, MC - 1):
                            down_chunk(g, m, early=False)

                    run(pe, group)

                @block.scalar
                def _(act):
                    def split(g):
                        for half in range(KH):
                            act.wait_ge(t_ready, g * 2 + half + 1)
                            nc.scalar.activation(xnT[0][:, half, :], tr[half][:, :], ACT.Copy)\
                                .then_inc(hi_ready, 1)

                    split(0)

                    def group(g, prev, nxt):
                        for m in range(MC):
                            act.wait_ge(up_ready, g * MC + m + 1)
                            if prev or m >= RING:
                                act.wait_ge(hid_split, g * MC + m - RING + 1)
                            nc.scalar.activation(hid[m % RING][:, :], up[m % RING][:, :], ACT.Gelu,
                                                 bias=b1_folded[:, m:m + 1]).then_inc(gelu_done, 1)
                        if nxt:
                            split(g + 1)

                    run(act, group)

                @block.vector
                def _(dve):
                    def norm_stats(g):
                        for j in range(G):
                            last = nc.vector.bn_stats(stats[:, j, :], acts[:, bass.ds(g * GF + j * F, F)])
                        last.then_inc(stats_ready, 1)
                        wait_apart(dve, stats_ready, g + 1, dve_waits)
                        for j in range(G):
                            last = nc.vector.bn_aggr(moments[:, j, :], stats[:, j, :])
                        last.then_inc(moments_ready, 1)

                    def normalise(g, early):
                        dve.wait_ge(rstd_ready, g + 1)
                        if not early:
                            dve.wait_ge(t_ready, g * 2)
                        for j in range(G):
                            last = nc.vector.tensor_scalar(xn[:, j, :], acts[:, bass.ds(g * GF + j * F, F)],
                                                           moments[:, j, 0:1], rstd[:, j:j + 1],
                                                           ALU.subtract, ALU.mult)
                        last.then_inc(normed, 1)

                    def split(g):
                        for half in range(KH):
                            dve.wait_ge(hi_ready, g * 2 + half + 1)
                            nc.vector.tensor_tensor(xnT[1][:, half, :], tr[half][:, :],
                                                    f32(xnT[0][:, half, :]), ALU.subtract)\
                                .then_inc(lo_ready, 1)

                    def split_hidden(g, m, early):
                        r = m % RING
                        dve.wait_ge(gelu_done, g * MC + m + 1)
                        if not early:
                            dve.wait_ge(down_done, g * MC + m - RING + 1)
                        nc.vector.tensor_copy(hid_hi[r][:, :], hid[r][:, :]).then_inc(hid_hi_ready, 1)
                        dve.wait_ge(hid_hi_ready, g * MC + m + 1)
                        nc.vector.tensor_tensor(hid_lo[r][:, :], hid[r][:, :], f32(hid_hi[r][:, :]),
                                                ALU.subtract).then_inc(hid_split, 1)

                    def add_down(g):
                        dve.wait_ge(b2_added, g + 1)
                        dve.wait_ge(down_done, g * MC + MC)
                        for i in range(2):
                            where = acts[:, bass.ds(g * GF + i * PAIR * F, PAIR * F)]
                            nc.vector.tensor_tensor(where, acc[i][:, :], where, ALU.add).then_inc(x2_added, 1)

                    norm_stats(0)
                    normalise(0, early=True)
                    split(0)

                    def group(g, prev, nxt):
                        for m in range(MC):
                            if prev and m == 0:
                                add_down(g - 1)
                            split_hidden(g, m, early=not prev and m < RING)
                            if nxt and m == 2:
                                norm_stats(g + 1)
                            if nxt and m == 4:
                                normalise(g + 1, early=False)
                        if nxt:
                            split(g + 1)

                    def refill_weights():
                        for i, (hi, lo) in enumerate((wq_s, wk_s, wv_s)):
                            dve.wait_ge(raw_loaded[i], 16)
                            nc.vector.tensor_copy(hi[:, :, :], raw[i][:, :, :]).then_inc(raw_hi_ready, 1)
                            dve.wait_ge(raw_hi_ready, i + 1)
                            nc.vector.tensor_tensor(lo[:, :, :], raw[i][:, :, :], f32(hi[:, :, :]),
                                                    ALU.subtract).then_inc(raw_split, 1)

                    run(dve, group)
                    add_down(GROUPS - 1)
                    refill_weights()

        def hop_phase():
            s = ExitStack()
            with s:
                adj_sb = [sb(s, f"h_adj_sb{i}", [128, G, N], I32) for i in range(2)]
                keep = [sb(s, f"keep{i}", [128, G, N]) for i in range(2)]
                fill = [sb(s, f"fill{i}", [128, G, N]) for i in range(2)]
                xs = [sb(s, f"xs{i}", [128, G, F]) for i in range(2)]
                xsT = tuple(sb(s, f"xsT_{p}", [128, KH, GN], F32R) for p in ("hi", "lo"))
                qT = [sb(s, f"h_qT{i}", [128, KH, GN]) for i in range(2)]
                kT = [sb(s, f"h_kT{i}", [128, KH, GN]) for i in range(2)]
                z0 = [sb(s, f"z0{i}", [128, G, F]) for i in range(2)]
                z0_part = [sb(s, f"z0_part{i}", [128, G, F]) for i in range(2)]
                resid = [sb(s, f"resid{i}", [128, G, F]) for i in range(2)]
                probs = [sb(s, f"h_probs{i}", [128, PAIR, H, N]) for i in range(2)]
                least = [sb(s, f"h_least{i}", [128, PAIR * H]) for i in range(2)]
                sums = [sb(s, f"h_sums{i}", [128, PAIR, KH]) for i in range(2)]
                shares = [sb(s, f"shares{i}", [128, PAIR, KH]) for i in range(2)]
                probsT = [sb(s, f"h_probsT{i}", [128, 4, 4 * N]) for i in range(2)]
                zT = sb(s, "zT", [128, PAIR, KH * N])
                z = sb(s, "z", [128, PAIR, F])
                y = [sb(s, f"y{i}", [128, PAIR, F]) for i in range(2)]
                stats = sb(s, "h_stats", [128, PAIR, 6])
                moments = sb(s, "h_moments", [128, PAIR, 2])
                var_eps = sb(s, "h_var_eps", [128, PAIR])
                rstd = sb(s, "h_rstd", [128, PAIR])
                score_bank, pt_bank, lin = bank[0:2], bank[2:4], bank[4:6]
                fwd_bank, back_bank = bank[6], bank[7]

                dve_waits = sem("h_dve_waits")
                pool_waits = sem("h_pool_waits")
                adj_loaded = [sem(f"h_adj_loaded{i}") for i in range(2)]
                fill_ready = sem("fill_ready")
                mask_ready = sem("mask_ready")
                xs_ready = sem("xs_ready")
                z0_part_ready = sem("z0_part_ready")
                resid_ready = sem("h_resid_ready")
                proj_ready = sem("h_proj_ready")
                hi_ready = sem("xsT_hi_ready")
                lo_ready = sem("xsT_lo_ready")
                proj_copied = sem("h_proj_copied")
                z0_ready = sem("z0_ready")
                scores_ready = sem("h_scores_ready")
                round_kept = sem("round_kept")
                round_masked = sem("h_round_masked")
                exp_done = sem("h_exp_done")
                pt_ready = sem("h_pt_ready")
                pt_copied = sem("h_pt_copied")
                shares_ready = sem("shares_ready")
                normalised = sem("normalised")
                fwd_ready = sem("fwd_ready")
                zT_copied = sem("zT_copied")
                back_ready = sem("back_ready")
                z_ready = sem("z_ready")
                stats_ready = sem("h_stats_ready")
                moments_ready = sem("h_moments_ready")
                var_ready = sem("h_var_ready")
                rstd_ready = sem("h_rstd_ready")
                centred = sem("centred")
                y_ready = sem("y_ready")
                y_free = [sem(f"y_free{i}") for i in range(2)]

                def loaded(g, par):
                    return g * 8 + (8 if par else 16)

                def run(engine, group):
                    group(0, 0, cur=True, prev=False, nxt=True, tail=False)
                    group(1, 1, cur=True, prev=True, nxt=True, tail=False)
                    with engine.Fori(1, GROUPS // 2 - 1) as i:
                        group(i * 2, 0, cur=True, prev=True, nxt=True, tail=True)
                        group(i * 2 + 1, 1, cur=True, prev=True, nxt=True, tail=True)
                    group(GROUPS - 2, 0, cur=True, prev=True, nxt=True, tail=True)
                    group(GROUPS - 1, 1, cur=True, prev=True, nxt=False, tail=True)
                    group(GROUPS, 0, cur=False, prev=True, nxt=False, tail=True)
                    group(GROUPS + 1, 1, cur=False, prev=False, nxt=False, tail=True)

                chunks_at = {1: (0, 1), 2: (2,), 3: (3,), 4: (4,), 5: (5,), 6: (6,)}
                prev_units_at = {1: (4,), 2: (5,), 3: (6, 7)}
                cur_units_at = {5: (0,), 6: (1,), 7: (2, 3)}

                def hop_number(g, pair, hop):
                    return g * 2 * HOPS + pair * HOPS + hop

                block = s.enter_context(nc.Block())

                @block.sync
                def _(sp):
                    def load(g, par):
                        sp.dma_start(adj_sb[par][:, :, :], adj[g, :, :, :]).then_inc(adj_loaded[par], 16)

                    def store(g, pair):
                        sp.wait_ge(y_ready, g * 2 + pair + 1)
                        sp.dma_start(out[g, :, PAIR * pair:PAIR * (pair + 1), :], y[pair][:, :, :])\
                            .then_inc(y_free[pair], 16)

                    load(0, 0)
                    load(1, 1)
                    for pair in range(2):
                        sp.sem_inc(y_free[pair], 16)

                    def group(g, par, more):
                        if more:
                            sp.wait_ge(mask_ready, g + 1)
                            load(g + 2, par)
                        for pair in range(2):
                            store(g, pair)

                    with sp.Fori(0, GROUPS // 2 - 1) as i:
                        group(i * 2, 0, True)
                        group(i * 2 + 1, 1, True)
                    group(GROUPS - 2, 0, False)
                    group(GROUPS - 1, 1, False)
                    for pair in range(2):
                        sp.wait_ge(y_free[pair], 16 * (GROUPS + 1))

                @block.gpsimd
                def _(pool):
                    def mask(g, par, early):
                        if not early:
                            pool.wait_ge(round_masked, (g - 1) * SLOTS)
                        wait_apart(pool, adj_loaded[par], loaded(g, par), pool_waits)
                        nc.gpsimd.tensor_scalar(fill[par][:, :, :], adj_sb[par][:, :, :], 0.0, HOP_MASK,
                                                ALU.is_equal, ALU.mult).then_inc(fill_ready, 1)
                        wait_apart(pool, fill_ready, g + 1, pool_waits)
                        nc.gpsimd.tensor_scalar(keep[par][:, :, :], fill[par][:, :, :], -1.0 / HOP_MASK, 1.0,
                                                ALU.mult, ALU.add).then_inc(mask_ready, 1)

                    def z_parts(g, par, early):
                        if not early:
                            pool.wait_ge(z_ready, (g - 1) * 2 * HOPS)
                        wait_apart(pool, z0_ready, g * 2 + 2, pool_waits)
                        nc.gpsimd.tensor_scalar(z0_part[par][:, :, :], z0[par][:, :, :], ALPHA, None, ALU.mult)\
                            .then_inc(z0_part_ready, 1)

                    def residual(g, par):
                        pool.wait_ge(z0_part_ready, g + 1)
                        pool.wait_ge(xs_ready, g + 1)
                        nc.gpsimd.tensor_tensor(resid[par][:, :, :], xs[par][:, :, :], z0_part[par][:, :, :],
                                                ALU.add).then_inc(resid_ready, 1)

                    def normalise_round(g, slot):
                        n = g * SLOTS + slot
                        pair, r = slot // ROUNDS, slot % ROUNDS
                        pool.wait_ge(shares_ready, n + 1)
                        part = probs[pair][:, :, r:H:4, :]
                        nc.gpsimd.tensor_tensor(
                            part, part, shares[slot % 2][:, :, :].unsqueeze(3)
                            .broadcast_to([128, PAIR, KH, N]), ALU.mult).then_inc(normalised, 1)

                    def root(n):
                        wait_apart(pool, moments_ready, n + 1, pool_waits)
                        nc.gpsimd.tensor_scalar(var_eps[:, :], moments[:, :, 1], EPS, None, ALU.add)\
                            .then_inc(var_ready, 1)
                        pool.wait_ge(var_ready, n + 1)
                        nc.gpsimd.tensor_tensor(rstd[:, :], var_eps[:, :], neg_half[:, 0:PAIR], ALU.pow)\
                            .then_inc(rstd_ready, 1)

                    mask(0, 0, early=True)

                    def group(g, par, cur, prev, nxt, tail):
                        for slot in range(SLOTS):
                            if prev and slot == 0:
                                normalise_round(g - 1, SLOTS - 1)
                            if cur and slot > 0:
                                normalise_round(g, slot - 1)
                            if cur and slot == 1:
                                z_parts(g, par, early=isinstance(g, int) and g < 2)
                            if tail and slot == 2:
                                root((g - 2) * 2 + 1)
                            if cur and slot == 2:
                                residual(g, par)
                            if nxt and slot == 3:
                                mask(g + 1, 1 - par, early=not prev)
                            if prev and slot == 5:
                                root((g - 1) * 2)

                    run(pool, group)

                @block.tensor
                def _(pe):
                    def project(g, par, chunk, first=False):
                        transpose, feature_major, node_major = pe_project(
                            pe, lin, xs[par], xsT, {"q": wq_s, "k": wk_s, "v": wv_s}, proj_ready)
                        if chunk == 0:
                            pe.wait_ge(xs_ready, g + 1)
                            if not first:
                                pe.wait_ge(z0_ready, g * 2 - 1)
                            transpose(0)
                        elif chunk == 1:
                            if not first:
                                pe.wait_ge(z0_ready, g * 2)
                            transpose(1)
                        elif chunk in (2, 3):
                            pe.wait_ge(lo_ready, g * 2 + 2)
                            feature_major("q", chunk - 2)
                        elif chunk in (4, 5):
                            pe.wait_ge(proj_copied, g * 4 + chunk - 3)
                            feature_major("k", chunk - 4)
                        else:
                            pe.wait_ge(proj_copied, g * 4 + chunk - 3)
                            node_major("v", chunk - 6)

                    def scores(g, par, slot, early):
                        if slot == 0:
                            pe.wait_ge(proj_copied, g * 4 + 4)
                        if not early:
                            pe.wait_ge(round_kept, g * SLOTS + slot - 1)
                        score_round(score_bank[slot % 2], qT[par], kT[par], slot // ROUNDS, slot % ROUNDS)\
                            .then_inc(scores_ready, 1)

                    def transpose_probs(g, unit, early):
                        graph, half = unit // 2, unit % 2
                        pair = graph // PAIR
                        if unit % 4 == 0:
                            pe.wait_ge(normalised, g * SLOTS + ROUNDS * pair + ROUNDS)
                        if not early:
                            pe.wait_ge(pt_copied, g * SLOTS + unit - 1)
                        for c in range(4):
                            last = nc.tensor.transpose(pt_bank[unit % 2][:, c * N:(c + 1) * N],
                                                       probs[pair][:, graph % PAIR, 4 * half + c, :], ident[:, :])
                        last.then_inc(pt_ready, 1)

                    def forward(g, par, pair, hop, early):
                        n = hop_number(g, pair, hop)
                        if hop == 0:
                            pe.wait_ge(pt_copied, g * SLOTS + 4 * pair + 4)
                            pe.wait_ge(z0_ready, g * 2 + 2)
                            if not early:
                                pe.wait_ge(zT_copied, n)
                        else:
                            pe.wait_ge(z_ready, n)
                        for j in range(PAIR):
                            for half in range(KH):
                                for c in range(4):
                                    h = 4 * half + c
                                    l = (z0[par][:, PAIR * pair + j, h * D:(h + 1) * D] if hop == 0
                                         else z[:, j, h * D:(h + 1) * D])
                                    last = nc.tensor.matmul(
                                        fwd_bank[D * c:D * (c + 1), (2 * j + half) * N:(2 * j + half + 1) * N],
                                        l, probsT[pair][:, 2 * j + half, c * N:(c + 1) * N],
                                        start=True, stop=True, tile_position=(0, D * c))
                        last.then_inc(fwd_ready, 1)

                    def back(g, pair, hop, early):
                        n = hop_number(g, pair, hop)
                        pe.wait_ge(zT_copied, n + 1)
                        if hop == 0 and not early:
                            pe.wait_ge(z_ready, n)
                        for j in range(PAIR):
                            for half in range(KH):
                                last = nc.tensor.transpose(
                                    back_bank[:, j * F + half * 128:j * F + (half + 1) * 128],
                                    zT[:, j, half * N:(half + 1) * N], ident[:, :])
                        last.then_inc(back_ready, 1)

                    for chunk in range(7):
                        project(0, 0, chunk, first=True)

                    def group(g, par, cur, prev, nxt, tail):
                        first = isinstance(g, int) and g == 1
                        for slot in range(SLOTS):
                            if cur:
                                scores(g, par, slot, early=not prev and slot < 2)
                            if tail and slot == 0:
                                back(g - 2, 1, HOPS - 1, early=False)
                            if prev and slot > 0:
                                back(g - 1, (slot - 1) // HOPS, (slot - 1) % HOPS, early=first and slot == 1)
                            if cur and slot == 0:
                                project(g, par, 7)
                            if nxt:
                                for chunk in chunks_at.get(slot, ()):
                                    project(g + 1, 1 - par, chunk)
                            if prev:
                                for unit in prev_units_at.get(slot, ()):
                                    transpose_probs(g - 1, unit, early=False)
                            if cur:
                                for unit in cur_units_at.get(slot, ()):
                                    transpose_probs(g, unit, early=not prev and unit < 2)
                            if prev:
                                forward(g - 1, 1 - par, slot // HOPS, slot % HOPS, early=first and slot == 0)

                    run(pe, group)

                @block.scalar
                def _(act):
                    def project(g, par, chunk, early):
                        act.wait_ge(proj_ready, g * 8 + chunk + 1)
                        if chunk < 2:
                            nc.scalar.activation(xsT[0][:, chunk, :], lin[chunk][:, :], ACT.Copy)\
                                .then_inc(hi_ready, 1)
                        elif chunk < 4:
                            if not early:
                                act.wait_ge(scores_ready, (g - 1) * SLOTS)
                            h = chunk - 2
                            nc.scalar.activation(qT[par][:, h, :], lin[h][:, :], ACT.Identity, scale=-1.0,
                                                 bias=hop_q_bias[:, h:h + 1]).then_inc(proj_copied, 1)
                        else:
                            h = chunk - 4
                            c = COLS["hop_bk"].start + h
                            nc.scalar.activation(kT[par][:, h, :], lin[h][:, :], ACT.Identity,
                                                 bias=cols[:, c:c + 1]).then_inc(proj_copied, 1)

                    def exponentials(g, slot, early):
                        pair, r = slot // ROUNDS, slot % ROUNDS
                        act.wait_ge(round_masked, g * SLOTS + slot + 1)
                        if not early:
                            act.wait_ge(shares_ready, g * SLOTS + slot - 1)
                        for j in range(PAIR):
                            for half in range(KH):
                                h = r + 4 * half
                                last = nc.scalar.activation(
                                    probs[pair][:, j, h, :], probs[pair][:, j, h, :], ACT.Exp, scale=-1.0,
                                    bias=least[pair][:, j * H + h:j * H + h + 1],
                                    accum_out=sums[slot % 2][:, j, half:half + 1])
                        last.then_inc(exp_done, 1)

                    def copy_probs(g, unit, early):
                        pair = unit // 4
                        act.wait_ge(pt_ready, g * SLOTS + unit + 1)
                        if unit % 4 == 0 and not early:
                            act.wait_ge(fwd_ready, (g - 1) * 2 * HOPS + (pair + 1) * HOPS)
                        nc.scalar.activation(probsT[pair][:, unit % 4, :], pt_bank[unit % 2][:, :], ACT.Copy)\
                            .then_inc(pt_copied, 1)

                    def copy_hop(g, pair, hop, early):
                        n = hop_number(g, pair, hop)
                        act.wait_ge(fwd_ready, n + 1)
                        if not early:
                            act.wait_ge(back_ready, n)
                        nc.scalar.activation(zT[:, :, :].rearrange("p j n -> p (j n)"), fwd_bank[:, :], ACT.Copy,
                                             scale=1.0 - ALPHA)\
                            .then_inc(zT_copied, 1)

                    for chunk in range(6):
                        project(0, 0, chunk, early=True)

                    def group(g, par, cur, prev, nxt, tail):
                        for slot in range(SLOTS):
                            if tail and slot == 0:
                                copy_hop(g - 2, 1, HOPS - 1, early=False)
                            if prev and slot > 0:
                                copy_hop(g - 1, (slot - 1) // HOPS, (slot - 1) % HOPS,
                                         early=isinstance(g, int) and g == 1 and slot == 1)
                            if prev and slot == 0:
                                exponentials(g - 1, SLOTS - 1, early=False)
                            if cur and slot > 0:
                                exponentials(g, slot - 1, early=not prev and slot < 3)
                            if nxt:
                                for chunk in chunks_at.get(slot, ()):
                                    if chunk < 6:
                                        project(g + 1, 1 - par, chunk, early=not prev)
                            if prev:
                                for unit in prev_units_at.get(slot, ()):
                                    copy_probs(g - 1, unit, early=isinstance(g, int) and g == 1)
                            if cur:
                                for unit in cur_units_at.get(slot, ()):
                                    copy_probs(g, unit, early=not prev)

                    run(act, group)

                @block.vector
                def _(dve):
                    def split(g):
                        for half in range(KH):
                            dve.wait_ge(hi_ready, g * 2 + half + 1)
                            nc.vector.tensor_tensor(xsT[1][:, half, :], lin[half][:, :],
                                                    f32(xsT[0][:, half, :]), ALU.subtract)\
                                .then_inc(lo_ready, 1)

                    def values(g, par, p, early):
                        dve.wait_ge(proj_ready, g * 8 + 7 + p)
                        if p == 0 and not early:
                            dve.wait_ge(z0_part_ready, g - 1)
                        nc.vector.tensor_tensor(
                            z0[par][:, PAIR * p:PAIR * (p + 1), :],
                            lin[p][:, :].rearrange("p (j f) -> p j f", j=PAIR),
                            row("hop_bv").unsqueeze(1).broadcast_to([128, PAIR, F]), ALU.add)\
                            .then_inc(z0_ready, 1)

                    def keep_round(g, par, slot, early):
                        pair, r = slot // ROUNDS, slot % ROUNDS
                        if slot == 0:
                            dve.wait_ge(mask_ready, g + 1)
                        if r == 0 and not early:
                            dve.wait_ge(pt_ready, (g - 1) * SLOTS + 4 * pair + 4)
                        dve.wait_ge(scores_ready, g * SLOTS + slot + 1)
                        nc.vector.tensor_tensor(
                            probs[pair][:, :, r:H:4, :],
                            score_bank[slot % 2][:, :].rearrange("p (j h n) -> p j h n", j=PAIR, h=KH),
                            keep[par][:, PAIR * pair:PAIR * (pair + 1), :].unsqueeze(2)
                            .broadcast_to([128, PAIR, KH, N]), ALU.mult).then_inc(round_kept, 1)

                    def mask_round(g, par, slot):
                        pair, r = slot // ROUNDS, slot % ROUNDS
                        wait_apart(dve, round_kept, g * SLOTS + slot + 1, dve_waits)
                        for j in range(PAIR):
                            for h in (r, r + 4):
                                last = nc.vector.tensor_tensor_reduce(
                                    out=probs[pair][:, j, h, :], in0=probs[pair][:, j, h, :],
                                    in1=fill[par][:, PAIR * pair + j, :], scale=1.0, scalar=LEAST_START,
                                    op0=ALU.add, op1=ALU.min,
                                    accum_out=least[pair][:, j * H + h:j * H + h + 1])
                        last.then_inc(round_masked, 1)

                    def invert_sums(g, slot, early):
                        n = g * SLOTS + slot
                        if not early:
                            dve.wait_ge(normalised, n - 1)
                        dve.wait_ge(exp_done, n + 1)
                        nc.vector.reciprocal(shares[slot % 2][:, :, :], sums[slot % 2][:, :, :])\
                            .then_inc(shares_ready, 1)

                    def take_hop(g, par, pair, hop):
                        last_hop = hop == HOPS - 1
                        if last_hop:
                            dve.wait_ge(resid_ready, g + 1)
                            dve.wait_ge(y_free[pair], g * 16 + 16)
                        elif hop == 0:
                            dve.wait_ge(z0_part_ready, g + 1)
                        dve.wait_ge(back_ready, hop_number(g, pair, hop) + 1)
                        to = y[pair] if last_hop else z
                        part = resid[par] if last_hop else z0_part[par]
                        nc.vector.tensor_tensor(to[:, :, :], back_bank[:, :].rearrange("p (j f) -> p j f", j=PAIR),
                                                part[:, PAIR * pair:PAIR * (pair + 1), :], ALU.add)\
                            .then_inc(z_ready, 1)

                    def final_stats(g, pair):
                        n = g * 2 + pair
                        dve.wait_ge(z_ready, (n + 1) * HOPS)
                        for j in range(PAIR):
                            last = nc.vector.bn_stats(stats[:, j, :], y[pair][:, j, :])
                        last.then_inc(stats_ready, 1)
                        wait_apart(dve, stats_ready, n + 1, dve_waits)
                        for j in range(PAIR):
                            last = nc.vector.bn_aggr(moments[:, j, :], stats[:, j, :])
                        last.then_inc(moments_ready, 1)

                    def final_norm(g, pair):
                        n = g * 2 + pair
                        dve.wait_ge(rstd_ready, n + 1)
                        for j in range(PAIR):
                            last = nc.vector.scalar_tensor_tensor(
                                out=y[pair][:, j, :], in0=y[pair][:, j, :], scalar=moments[:, j, 0:1],
                                in1=row("gamma"), op0=ALU.subtract, op1=ALU.mult)
                        last.then_inc(centred, 1)
                        dve.wait_ge(centred, n + 1)
                        for j in range(PAIR):
                            last = nc.vector.scalar_tensor_tensor(
                                out=y[pair][:, j, :], in0=y[pair][:, j, :], scalar=rstd[:, j:j + 1],
                                in1=row("beta"), op0=ALU.mult, op1=ALU.add)
                        last.then_inc(y_ready, 1)

                    def copy_x(g, par, early):
                        if not early:
                            dve.wait_ge(resid_ready, g - 1)
                            dve.wait_ge(proj_ready, g * 8 - 14)
                        nc.vector.tensor_copy(xs[par][:, :, :].rearrange("p j f -> p (j f)"),
                                              acts[:, bass.ds(g * GF, GF)]).then_inc(xs_ready, 1)

                    copy_x(0, 0, early=True)
                    split(0)

                    values(0, 0, 0, early=True)

                    def group(g, par, cur, prev, nxt, tail):
                        early = isinstance(g, int) and g < 2
                        for slot in range(SLOTS):
                            if cur:
                                keep_round(g, par, slot, early=not prev)
                            if tail and slot == 0:
                                take_hop(g - 2, par, 1, HOPS - 1)
                            if prev and slot > 0:
                                take_hop(g - 1, 1 - par, (slot - 1) // HOPS, (slot - 1) % HOPS)
                            if cur:
                                mask_round(g, par, slot)
                            if prev and slot == 0:
                                invert_sums(g - 1, SLOTS - 1, early=False)
                            if cur and slot > 0:
                                invert_sums(g, slot - 1, early=not prev and slot < 3)
                            if nxt and slot == 0:
                                copy_x(g + 1, 1 - par, early=early)
                            if cur and slot == 0:
                                values(g, par, 1, early=early)
                            if nxt and slot == 1:
                                split(g + 1)
                            if tail and slot == 2:
                                final_stats(g - 2, 1)
                            if tail and slot == 3:
                                final_norm(g - 2, 1)
                            if prev and slot == 5:
                                final_stats(g - 1, 0)
                            if nxt and slot == 6:
                                values(g + 1, 1 - par, 0, early=early)
                            if prev and slot == 7:
                                final_norm(g - 1, 0)

                    run(dve, group)

        with mlp_stack:
            with att_stack:
                setup()
                attention_phase()
            mlp_phase()
        hop_phase()


def kernel(x, adj, L0_gnn_ln1_g, L0_gnn_ln1_b, L0_gnn_ln2_g, L0_gnn_ln2_b, L0_gnn_wq, L0_gnn_bq, L0_gnn_wk,
           L0_gnn_bk, L0_gnn_wv, L0_gnn_bv, L0_gnn_wo, L0_gnn_bo, L0_gnn_w1, L0_gnn_b1, L0_gnn_w2, L0_gnn_b2,
           L1_gnn_Wq, L1_gnn_bq, L1_gnn_Wk, L1_gnn_bk, L1_gnn_Wv, L1_gnn_bv, L1_gnn_gamma, L1_gnn_beta):
    import numpy as np
    import concourse.bacc as bacc
    from concourse.bass_utils import run_bass_kernel_spmd

    def by_group(a):
        a = np.asarray(a)
        return np.ascontiguousarray(a.reshape(GROUPS, G, N, a.shape[2]).transpose(0, 2, 1, 3))

    def columns(*vectors):
        return np.ascontiguousarray(np.concatenate([np.asarray(a).reshape(-1, 128) for a in vectors]).T)

    arrays = {
        "x_in": by_group(x),
        "adj_in": by_group(adj),
        "vec_cols": columns(L0_gnn_ln1_g, L0_gnn_ln1_b, L0_gnn_ln2_g, L0_gnn_ln2_b, L0_gnn_bq, L0_gnn_bk,
                            L0_gnn_bv, L0_gnn_b1, L1_gnn_bq, L1_gnn_bk),
        "vec_rows": np.concatenate([np.asarray(a).reshape(1, -1) for a in
                                    (L0_gnn_bo, L0_gnn_b2, L1_gnn_bv, L1_gnn_gamma, L1_gnn_beta)], axis=1),
        "wq": np.asarray(L0_gnn_wq), "wk": np.asarray(L0_gnn_wk), "wv": np.asarray(L0_gnn_wv),
        "wo": np.asarray(L0_gnn_wo), "w1": np.asarray(L0_gnn_w1), "w2": np.asarray(L0_gnn_w2),
        "hwq": np.ascontiguousarray(np.asarray(L1_gnn_Wq).T),
        "hwk": np.ascontiguousarray(np.asarray(L1_gnn_Wk).T),
        "hwv": np.ascontiguousarray(np.asarray(L1_gnn_Wv).T),
    }
    nc = bacc.Bacc("TRN2", target_bir_lowering=False, num_devices=1)
    aps = [nc.dram_tensor(n, a.shape, mybir.dt.from_np(a.dtype), kind="ExternalInput").ap()
           for n, a in arrays.items()]
    out = nc.dram_tensor("out", (GROUPS, N, G, F), F32, kind="ExternalOutput").ap()
    graph_transformer(nc, *aps, out)
    r = run_bass_kernel_spmd(nc, [arrays], core_ids=[0])
    got = r.results[0]["out"]
    return np.ascontiguousarray(got.transpose(0, 2, 1, 3)).reshape(B, N, F)
```

```python
import concourse.bass as bass
from concourse import mybir
from contextlib import ExitStack

F32 = mybir.dt.float32
F32R = mybir.dt.float32r
I32 = mybir.dt.int32
ALU = mybir.AluOpType
ACT = mybir.ActivationFunctionType

B, N, F = 64, 128, 256
H = 8
D = F // H
FF = 4 * F
G = 4
GROUPS = B // G
KH = F // 128
MC = FF // 128
GN = G * N
GF = G * F
PAIR = 2
ROUNDS = 4
SLOTS = 2 * ROUNDS
HOPS = 4
ALPHA = 0.1
EPS = 1e-5
HOP_MASK = 16384.0
FAR = 1e30
LEAST_START = 3e38
QSCALE = 1.0 / float(D) ** 0.5

COLS = {}
for _name, _n in (("ln1_g", KH), ("ln1_b", KH), ("ln2_g", KH), ("ln2_b", KH), ("bq", KH), ("bk", KH),
                  ("bv", KH), ("b1", MC), ("hop_bq", KH), ("hop_bk", KH)):
    COLS[_name] = slice(sum(s.stop - s.start for s in COLS.values()),
                        sum(s.stop - s.start for s in COLS.values()) + _n)
NCOLS = sum(s.stop - s.start for s in COLS.values())
ROWS = ["bo", "b2", "hop_bv", "gamma", "beta"]


def graph_transformer(nc, x, adj, vec_cols, vec_rows, wq, wk, wv, wo, w1, w2, hwq, hwk, hwv, out):
    outer = ExitStack()
    mlp_stack = ExitStack()
    att_stack = ExitStack()

    def sb(stack, name, shape, dt=F32):
        return stack.enter_context(nc.sbuf_tensor(name, shape, dt))

    def sem(name):
        return outer.enter_context(nc.semaphore(name))

    def f32(ap):
        return ap.bitcast(F32)

    def wait_apart(engine, semaphore, value, passed):
        engine.wait_ge(semaphore, value)
        engine.sem_inc(passed, 1)

    with outer:
        bank = [outer.enter_context(nc.psum_tensor(f"bank{i}", [128, 512], F32)) for i in range(8)]
        acts = sb(outer, "acts", [128, GROUPS * GF])
        cols = sb(outer, "cols", [128, NCOLS])
        rows = sb(outer, "rows", [128, len(ROWS), F])
        ident = sb(outer, "ident", [128, 128])
        neg_half = sb(outer, "neg_half", [128, G])
        bo_folded = sb(outer, "bo_folded", [128, F])
        b1_folded = sb(outer, "b1_folded", [128, MC])
        q_bias = sb(outer, "q_bias", [128, KH])
        k_bias = sb(outer, "k_bias", [128, KH])
        hop_q_bias = sb(outer, "hop_q_bias", [128, KH])

        stats = sb(outer, "stats", [128, G, 6])
        moments = sb(outer, "moments", [128, G, 2])
        var_eps = sb(outer, "var_eps", [128, G])
        rstd = sb(outer, "rstd", [128, G])
        xn = sb(outer, "xn", [128, G, F])
        xnT = tuple(sb(outer, f"xnT_{p}", [128, KH, GN], F32R) for p in ("hi", "lo"))

        def split_weight(stack, name, shape):
            return tuple(sb(stack, f"{name}_{part}", shape, F32R) for part in ("hi", "lo"))

        wq_s = split_weight(outer, "wq", [128, KH, F])
        wk_s = split_weight(outer, "wk", [128, KH, F])
        wv_s = split_weight(outer, "wv", [128, KH, F])
        w1_s = split_weight(mlp_stack, "w1", [128, KH, FF])
        w2_s = split_weight(mlp_stack, "w2", [128, MC, F])
        wo_s = split_weight(att_stack, "wo", [128, KH, F])

        def products(weight, act):
            return ((weight[0], act[0]), (weight[1], act[0]), (weight[0], act[1]))

        raw_at = [GROUPS * GF]

        def raw_weight(k, n):
            raw_at[0] -= k * n
            return acts[:, raw_at[0]:raw_at[0] + k * n].rearrange("p (k n) -> p k n", k=k)

        w1_raw, w2_raw = raw_weight(KH, FF), raw_weight(MC, F)
        mlp_loaded = [sem("w1_loaded"), sem("w2_loaded")]

        def row(name):
            return rows[:, ROWS.index(name), :]

        m_dve_waits = sem("m_dve_waits")
        m_pool_waits = sem("m_pool_waits")
        m_stats_ready = sem("m_stats_ready")
        m_moments_ready = sem("m_moments_ready")
        m_var_ready = sem("m_var_ready")
        m_rstd_ready = sem("m_rstd_ready")
        m_normed = sem("m_normed")
        m_t_ready = sem("m_t_ready")
        m_hi_ready = sem("m_hi_ready")
        m_lo_ready = sem("m_lo_ready")
        up_ready = sem("up_ready")
        down_done = sem("down_done")
        b2_added = sem("b2_added")
        x2_added = sem("x2_added")
        RING = 4
        xs_ready = sem("xs_ready")
        h_proj_ready = sem("h_proj_ready")
        h_hi_ready = sem("xsT_hi_ready")
        h_lo_ready = sem("xsT_lo_ready")
        tr = bank[4:6]

        def mlp_norm_stats(dve, g):
            for j in range(G):
                last = nc.vector.bn_stats(stats[:, j, :], acts[:, bass.ds(g * GF + j * F, F)])
            last.then_inc(m_stats_ready, 1)
            wait_apart(dve, m_stats_ready, g + 1, m_dve_waits)
            for j in range(G):
                last = nc.vector.bn_aggr(moments[:, j, :], stats[:, j, :])
            last.then_inc(m_moments_ready, 1)

        def mlp_root(pool, g):
            wait_apart(pool, m_moments_ready, g + 1, m_pool_waits)
            nc.gpsimd.tensor_scalar(var_eps[:, :], moments[:, :, 1], EPS, None, ALU.add)\
                .then_inc(m_var_ready, 1)
            pool.wait_ge(m_var_ready, g + 1)
            nc.gpsimd.tensor_tensor(rstd[:, :], var_eps[:, :], neg_half[:, :], ALU.pow)\
                .then_inc(m_rstd_ready, 1)

        def mlp_normalise(dve, g):
            dve.wait_ge(m_rstd_ready, g + 1)
            for j in range(G):
                last = nc.vector.tensor_scalar(xn[:, j, :], acts[:, bass.ds(g * GF + j * F, F)],
                                               moments[:, j, 0:1], rstd[:, j:j + 1],
                                               ALU.subtract, ALU.mult)
            last.then_inc(m_normed, 1)

        def mlp_transpose(pe, g):
            pe.wait_ge(m_normed, g + 1)
            for half in range(KH):
                for j in range(G):
                    last = nc.tensor.transpose(tr[half][:, j * N:(j + 1) * N],
                                               xn[:, j, half * 128:(half + 1) * 128], ident[:, :])
                last.then_inc(m_t_ready, 1)

        def mlp_up(g, m):
            todo = [(k, w, a) for k in range(KH) for w, a in products(w1_s, xnT)]
            for n, (k, w, a) in enumerate(todo):
                last = nc.tensor.matmul(bank[m % RING][:, :], w[:, k, m * 128:(m + 1) * 128],
                                        a[:, k, :], start=(n == 0), stop=(n == len(todo) - 1))
            last.then_inc(up_ready, 1)

        def mlp_add_down(dve, g):
            dve.wait_ge(b2_added, g + 1)
            dve.wait_ge(down_done, g * MC + MC)
            for i in range(2):
                where = acts[:, bass.ds(g * GF + i * PAIR * F, PAIR * F)]
                nc.vector.tensor_tensor(where, bank[6 + i][:, :], where, ALU.add).then_inc(x2_added, 1)

        def mlp_split_high(act, g):
            for half in range(KH):
                act.wait_ge(m_t_ready, g * 2 + half + 1)
                nc.scalar.activation(xnT[0][:, half, :], tr[half][:, :], ACT.Copy).then_inc(m_hi_ready, 1)

        def split_low(dve, g, hi_ready, lo_ready):
            for half in range(KH):
                dve.wait_ge(hi_ready, g * 2 + half + 1)
                nc.vector.tensor_tensor(xnT[1][:, half, :], tr[half][:, :], f32(xnT[0][:, half, :]),
                                        ALU.subtract).then_inc(lo_ready, 1)

        def pe_project(pe, lin, xn, act_s, weights, proj_ready):
            def transpose(half):
                for j in range(G):
                    last = nc.tensor.transpose(lin[half][:, j * N:(j + 1) * N],
                                               xn[:, j, half * 128:(half + 1) * 128], ident[:, :])
                last.then_inc(proj_ready, 1)

            def feature_major(which, half):
                todo = [(k, w, a) for k in range(KH) for w, a in products(weights[which], act_s)]
                for n, (k, w, a) in enumerate(todo):
                    last = nc.tensor.matmul(lin[half][:, :], w[:, k, half * 128:(half + 1) * 128],
                                            a[:, k, :], start=(n == 0), stop=(n == len(todo) - 1))
                last.then_inc(proj_ready, 1)

            def node_major(which, pair):
                for j in range(PAIR):
                    g = PAIR * pair + j
                    todo = [(k, w, a) for k in range(KH) for w, a in products(weights[which], act_s)]
                    for n, (k, w, a) in enumerate(todo):
                        last = nc.tensor.matmul(lin[pair][:, j * F:(j + 1) * F],
                                                a[:, k, g * N:(g + 1) * N], w[:, k, :],
                                                start=(n == 0), stop=(n == len(todo) - 1))
                last.then_inc(proj_ready, 1)

            return transpose, feature_major, node_major

        def score_round(score_bank, qT, kT, pair, r):
            for j in range(PAIR):
                cols_ = slice((PAIR * pair + j) * N, (PAIR * pair + j + 1) * N)
                for half in range(KH):
                    last = nc.tensor.matmul(
                        score_bank[:, (2 * j + half) * N:(2 * j + half + 1) * N],
                        qT[D * r:D * (r + 1), half, cols_], kT[D * r:D * (r + 1), half, cols_],
                        start=True, stop=True)
            return last

        def attention_phase():
            s = ExitStack()
            with s:
                xin = [sb(s, f"xin{i}", [128, G, F]) for i in range(2)]
                adj_sb = [sb(s, f"adj_sb{i}", [128, G, N], I32) for i in range(2)]
                bias = [sb(s, f"bias{i}", [128, G, N]) for i in range(2)]
                edge = sb(s, "edge", [128, G, N])
                qT = [sb(s, f"qT{i}", [128, KH, GN]) for i in range(2)]
                kT = [sb(s, f"kT{i}", [128, KH, GN]) for i in range(2)]
                v = [sb(s, f"v{i}", [128, G, F]) for i in range(2)]
                probs = [sb(s, f"probs{i}", [128, PAIR, H, N]) for i in range(2)]
                least = [sb(s, f"least{i}", [128, PAIR, H]) for i in range(2)]
                probsT = [sb(s, f"probsT{i}", [128, 4 * N]) for i in range(2)]
                sums = [sb(s, f"sums{i}", [128, PAIR, KH]) for i in range(2)]
                shares = [sb(s, f"a_shares{i}", [128, PAIR, KH]) for i in range(2)]
                attT = tuple([sb(s, f"attT{i}_{p}", [128, PAIR, KH * N], F32R) for i in range(2)]
                             for p in ("hi", "lo"))
                score_bank, pt_bank, lin = bank[0:2], bank[2:4], bank[4:6]
                pv_bank, wo_bank = bank[6], bank[7]

                raws = {name: raw_weight(KH, F) for name in ("wq", "wk", "wv", "wo")}
                splits = {"wq": wq_s, "wk": wk_s, "wv": wv_s, "wo": wo_s}
                cv = sb(s, "cv", [128, KH])
                cv_wide = raw_weight(KH, 128)
                fold_bank, bo_bank = pv_bank, pt_bank[1]
                fold_at = {"wq": 0, "wk": KH, "wv": 2 * KH}
                cols_loaded = sem("cols_loaded")
                rows_loaded = sem("rows_loaded")
                w_loaded = {name: sem(f"{name}_loaded") for name in raws}
                consts_ready = sem("consts_ready")
                ident_zeroed = sem("ident_zeroed")
                w_hi_ready = sem("w_hi_ready")
                w_split = sem("w_split")
                folds_ready = sem("folds_ready")
                col_biases_ready = sem("col_biases_ready")
                cv_ready = sem("cv_ready")
                cv_spread = sem("cv_spread")
                bo_product_ready = sem("bo_product_ready")
                bo_ready = sem("bo_ready")

                x_loaded = [sem(f"x_loaded{i}") for i in range(2)]
                mlp_hi_ready = sem("mlp_hi_ready")
                mlp_split = sem("mlp_split")
                fold_ready = sem("b1_fold_ready")
                b1_ready = sem("b1_ready")
                dve_waits = sem("dve_waits")
                pool_waits = sem("pool_waits")
                adj_loaded = [sem(f"adj_loaded{i}") for i in range(2)]
                bias_parts = sem("bias_parts")
                bias_ready = sem("bias_ready")
                resid_ready = sem("resid_ready")
                stats_ready = sem("stats_ready")
                moments_ready = sem("moments_ready")
                var_ready = sem("var_ready")
                rstd_ready = sem("rstd_ready")
                normed = sem("normed")
                proj_ready = sem("proj_ready")
                hi_ready = sem("xnT_hi_ready")
                lo_ready = sem("xnT_lo_ready")
                proj_copied = sem("proj_copied")
                v_copied = sem("v_copied")
                scores_ready = sem("scores_ready")
                round_masked = sem("round_masked")
                exp_done = sem("exp_done")
                pt_ready = sem("pt_ready")
                pt_copied = sem("pt_copied")
                pv_ready = sem("pv_ready")
                shares_ready = sem("a_shares_ready")
                normalised = sem("a_normalised")
                att_hi_ready = sem("att_hi_ready")
                att_split = sem("att_split")
                wo_ready = sem("wo_ready")
                x1_added = sem("x1_added")

                def loaded(g, par):
                    return g * 8 + (8 if par else 16)

                def run(engine, group):
                    group(0, 0, cur=True, prev=False, nxt=True)
                    group(1, 1, cur=True, prev=True, nxt=True)
                    with engine.Fori(1, GROUPS // 2 - 1) as i:
                        group(i * 2, 0, cur=True, prev=True, nxt=True)
                        group(i * 2 + 1, 1, cur=True, prev=True, nxt=True)
                    group(GROUPS - 2, 0, cur=True, prev=True, nxt=True)
                    group(GROUPS - 1, 1, cur=True, prev=True, nxt=False)
                    group(GROUPS, 0, cur=False, prev=True, nxt=False)

                def two_more(g):
                    return not (isinstance(g, int) and g >= GROUPS - 2)

                chunks_at = {2: (0, 1), 3: (2,), 4: (3,), 5: (4, 5), 7: (6,)}
                cur_units_at = {6: (0, 1), 7: (2, 3)}
                prev_units_at = {1: (4,), 2: (5,), 3: (6, 7)}
                prev_weighed_at = {0: (2, 3), 2: (4,), 3: (5,), 4: (6, 7)}

                block = s.enter_context(nc.Block())

                @block.sync
                def _(sp):
                    def load(g, par):
                        sp.dma_start(xin[par][:, :, :], x[g, :, :, :]).then_inc(x_loaded[par], 16)
                        sp.dma_start(adj_sb[par][:, :, :], adj[g, :, :, :]).then_inc(adj_loaded[par], 16)

                    load(0, 0)
                    sp.wait_ge(w_loaded["wv"], 16)
                    load(1, 1)
                    with sp.Fori(0, GROUPS // 2 - 1) as i:
                        for par in range(2):
                            g = i * 2 + par
                            sp.wait_ge(bias_ready, g + 1)
                            sp.wait_ge(resid_ready, g + 1)
                            sp.wait_ge(normed, g + 1)
                            load(g + 2, par)

                @block.gpsimd
                def _(pool):
                    nc.gpsimd.memset(ident[:, :], 0.0).then_inc(ident_zeroed, 1)
                    pool.wait_ge(ident_zeroed, 1)
                    nc.gpsimd.affine_select(out=ident[:, :], in_=ident[:, :], compare_op=ALU.not_equal,
                                            fill=1.0, base=0, pattern=[[-1, 128]], channel_multiplier=1)\
                        .then_inc(consts_ready, 1)
                    nc.gpsimd.memset(neg_half[:, :], -0.5).then_inc(consts_ready, 1)
                    pool.wait_ge(consts_ready, 2)

                    def root(g):
                        wait_apart(pool, moments_ready, g + 1, pool_waits)
                        nc.gpsimd.tensor_scalar(var_eps[:, :], moments[:, :, 1], EPS, None, ALU.add)\
                            .then_inc(var_ready, 1)
                        pool.wait_ge(var_ready, g + 1)
                        nc.gpsimd.tensor_tensor(rstd[:, :], var_eps[:, :], neg_half[:, :], ALU.pow)\
                            .then_inc(rstd_ready, 1)

                    def mask(g, par, early, step):
                        if step == 0:
                            wait_apart(pool, adj_loaded[par], loaded(g, par), pool_waits)
                            nc.gpsimd.tensor_scalar(edge[:, :, :], adj_sb[par][:, :, :], 0.0, -ALPHA,
                                                    ALU.max, ALU.mult).then_inc(bias_parts, 1)
                        elif step == 1:
                            if not early:
                                wait_apart(pool, round_masked, (g - 1) * SLOTS, pool_waits)
                            nc.gpsimd.tensor_scalar(bias[par][:, :, :], adj_sb[par][:, :, :], 0.0, None,
                                                    ALU.max).then_inc(bias_parts, 1)
                        elif step == 2:
                            pool.wait_ge(bias_parts, g * 4 + 2)
                            nc.gpsimd.tensor_tensor(edge[:, :, :], edge[:, :, :], bias[par][:, :, :], ALU.mult)\
                                .then_inc(bias_parts, 1)
                        elif step == 3:
                            wait_apart(pool, bias_parts, g * 4 + 3, pool_waits)
                            nc.gpsimd.tensor_scalar(bias[par][:, :, :], adj_sb[par][:, :, :], 0.0, FAR,
                                                    ALU.is_le, ALU.mult).then_inc(bias_parts, 1)
                        else:
                            pool.wait_ge(bias_parts, g * 4 + 4)
                            nc.gpsimd.tensor_tensor(bias[par][:, :, :], bias[par][:, :, :], edge[:, :, :],
                                                    ALU.add).then_inc(bias_ready, 1)
                            pool.wait_ge(bias_ready, g + 1)

                    def normalise_round(g, slot):
                        pair, r = slot // ROUNDS, slot % ROUNDS
                        pool.wait_ge(shares_ready, g * SLOTS + slot + 1)
                        part = probs[pair][:, :, r:H:4, :]
                        nc.gpsimd.tensor_tensor(
                            part, part, shares[slot % 2][:, :, :].unsqueeze(3)
                            .broadcast_to([128, PAIR, KH, N]), ALU.mult).then_inc(normalised, 1)

                    root(0)
                    for step in range(5):
                        mask(0, 0, early=True, step=step)

                    def group(g, par, cur, prev, nxt):
                        for slot in range(SLOTS):
                            if cur and not prev and slot == 0:
                                root(1)
                            if prev and slot == 0:
                                normalise_round(g - 1, SLOTS - 1)
                            if cur and slot > 0:
                                normalise_round(g, slot - 1)
                            if nxt and slot in (0, 2, 3, 5, 6):
                                mask(g + 1, 1 - par, early=not prev, step=(0, 2, 3, 5, 6).index(slot))
                            if cur and slot == 7 and two_more(g):
                                root(g + 2)
                            if nxt and slot == 7 and not two_more(g):
                                mlp_root(pool, 0)

                    run(pool, group)

                @block.tensor
                def _(pe):
                    transpose, feature_major, node_major = pe_project(
                        pe, lin, xn, xnT, {"q": wq_s, "k": wk_s, "v": wv_s}, proj_ready)

                    def project(g, chunk, first=False):
                        if chunk == 0:
                            pe.wait_ge(normed, g + 1)
                            if not first:
                                pe.wait_ge(v_copied, g * 2 - 1)
                            transpose(0)
                        elif chunk == 1:
                            if not first:
                                pe.wait_ge(v_copied, g * 2)
                            transpose(1)
                        elif chunk in (2, 3):
                            pe.wait_ge(lo_ready, g * 2 + 2)
                            feature_major("q", chunk - 2)
                        elif chunk in (4, 5):
                            pe.wait_ge(proj_copied, g * 4 + chunk - 3)
                            feature_major("k", chunk - 4)
                        else:
                            pe.wait_ge(proj_copied, g * 4 + chunk - 3)
                            node_major("v", chunk - 6)

                    def scores(g, par, slot, early):
                        if slot == 0:
                            pe.wait_ge(proj_copied, g * 4 + 4)
                        if not early:
                            pe.wait_ge(round_masked, g * SLOTS + slot - 1)
                        score_round(score_bank[slot % 2], qT[par], kT[par], slot // ROUNDS, slot % ROUNDS)\
                            .then_inc(scores_ready, 1)

                    def transpose_probs(g, unit, early):
                        graph, half = unit // 2, unit % 2
                        pair = graph // PAIR
                        if unit % 4 == 0:
                            pe.wait_ge(normalised, g * SLOTS + ROUNDS * pair + ROUNDS)
                        if not early:
                            pe.wait_ge(pt_copied, g * SLOTS + unit - 1)
                        for c in range(4):
                            last = nc.tensor.transpose(pt_bank[unit % 2][:, c * N:(c + 1) * N],
                                                       probs[pair][:, graph % PAIR, 4 * half + c, :], ident[:, :])
                        last.then_inc(pt_ready, 1)

                    def weigh(g, par, unit, early):
                        graph, half = unit // 2, unit % 2
                        if unit == 0:
                            pe.wait_ge(v_copied, g * 2 + 2)
                        pe.wait_ge(pt_copied, g * SLOTS + unit + 1)
                        if half == 0 and not early:
                            pe.wait_ge(att_split, g * G + graph)
                        for c in range(4):
                            h = 4 * half + c
                            last = nc.tensor.matmul(
                                pv_bank[D * c:D * (c + 1), half * N:(half + 1) * N],
                                v[par][:, graph, h * D:(h + 1) * D], probsT[unit % 2][:, c * N:(c + 1) * N],
                                start=True, stop=True, tile_position=(0, D * c))
                        last.then_inc(pv_ready, 1)

                    def fold_mlp_shift():
                        pe.wait_ge(mlp_loaded[0], 16)
                        for m in range(MC):
                            for k in range(KH):
                                b = COLS["ln2_b"].start + k
                                last = nc.tensor.matmul(wo_bank[:, m:m + 1], w1_raw[:, k, m * 128:(m + 1) * 128],
                                                        cols[:, b:b + 1], start=(k == 0), stop=(k == KH - 1))
                        last.then_inc(fold_ready, 1)

                    def output(g, pair, early):
                        pe.wait_ge(att_split, g * G + PAIR * (pair + 1))
                        if early:
                            pe.wait_ge(b1_ready, 1)
                        else:
                            pe.wait_ge(x1_added, g * 2 + pair)
                        for j in range(PAIR):
                            todo = [(k, w, a) for k in range(KH)
                                    for w, a in products(wo_s, (attT[0][pair], attT[1][pair]))]
                            for n, (k, w, a) in enumerate(todo):
                                last = nc.tensor.matmul(wo_bank[:, j * F:(j + 1) * F],
                                                        a[:, j, k * N:(k + 1) * N], w[:, k, :],
                                                        start=(n == 0), stop=(n == len(todo) - 1))
                        last.then_inc(wo_ready, 1)

                    def fold_norm_shift(names):
                        pe.wait_ge(cols_loaded, 16)
                        for name in names:
                            pe.wait_ge(w_loaded[name], 16)
                            for m in range(KH):
                                c = fold_at[name] + m
                                for k in range(KH):
                                    b = COLS["ln1_b"].start + k
                                    last = nc.tensor.matmul(
                                        fold_bank[:, c:c + 1], raws[name][:, k, m * 128:(m + 1) * 128],
                                        cols[:, b:b + 1], start=(k == 0), stop=(k == KH - 1))
                            last.then_inc(folds_ready, 1)

                    def fold_value_shift():
                        pe.wait_ge(cv_spread, 1)
                        pe.wait_ge(w_loaded["wo"], 16)
                        for k in range(KH):
                            last = nc.tensor.matmul(bo_bank[:, 0:F], cv_wide[:, k, :], raws["wo"][:, k, :],
                                                    start=(k == 0), stop=(k == KH - 1))
                        last.then_inc(bo_product_ready, 1)

                    fold_norm_shift(("wq",))
                    pe.wait_ge(consts_ready, 2)
                    for chunk in range(7):
                        if chunk == 2:
                            fold_norm_shift(("wk", "wv"))
                        if chunk in (2, 4, 6):
                            pe.wait_ge(w_split, KH * (chunk // 2))
                        project(0, chunk, first=True)
                    fold_value_shift()

                    def group(g, par, cur, prev, nxt):
                        for slot in range(SLOTS):
                            if cur:
                                scores(g, par, slot, early=not prev and slot < 2)
                            if prev and slot in (2, 3):
                                for unit in prev_weighed_at[slot]:
                                    weigh(g - 1, 1 - par, unit, early=False)
                            if cur and slot == 7:
                                for unit in (0, 1):
                                    weigh(g, par, unit, early=not prev)
                            if cur and slot == 0:
                                project(g, 7)
                            if prev and slot == 3:
                                transpose_probs(g - 1, 6, early=False)
                            if nxt:
                                for chunk in chunks_at.get(slot, ()):
                                    project(g + 1, chunk)
                            if cur and not nxt and slot == 2:
                                pe.wait_ge(v_copied, GROUPS * 2)
                                mlp_transpose(pe, 0)
                            if prev:
                                for unit in prev_units_at.get(slot, ()):
                                    if unit != 6:
                                        transpose_probs(g - 1, unit, early=False)
                            if cur:
                                for unit in cur_units_at.get(slot, ()):
                                    transpose_probs(g, unit, early=not prev and unit < 2)
                            if not cur and slot in (0, 1):
                                if slot == 0:
                                    pe.wait_ge(mlp_split, KH + MC)
                                    pe.wait_ge(m_lo_ready, 2)
                                    pe.wait_ge(round_masked, GROUPS * SLOTS)
                                mlp_up(0, slot)
                            if prev and slot in (0, 4):
                                for unit in prev_weighed_at[slot]:
                                    weigh(g - 1, 1 - par, unit, early=False)
                            if cur and not prev and slot == 1:
                                fold_mlp_shift()
                            if prev and slot == 1:
                                output(g - 1, 0, early=isinstance(g, int) and g == 1)
                            if prev and slot == 6:
                                output(g - 1, 1, early=False)

                    run(pe, group)

                @block.scalar
                def _(act):
                    act.dma_start(cols[:, :], vec_cols).then_inc(cols_loaded, 16)
                    for name, w in (("wq", wq), ("wk", wk), ("wv", wv), ("wo", wo)):
                        act.dma_start(raws[name], w.rearrange("(k p) n -> p k n", p=128))\
                            .then_inc(w_loaded[name], 16)
                    act.dma_start(rows[:, :, :].rearrange("p r n -> p (r n)"),
                                  vec_rows.broadcast_to([128, len(ROWS) * F])).then_inc(rows_loaded, 16)
                    for raw, w, loaded_ in zip((w1_raw, w2_raw), (w1, w2), mlp_loaded):
                        act.dma_start(raw, w.rearrange("(k p) n -> p k n", p=128)).then_inc(loaded_, 16)

                    def project(g, par, chunk, early):
                        act.wait_ge(proj_ready, g * 8 + chunk + 1)
                        if chunk < 2:
                            nc.scalar.activation(xnT[0][:, chunk, :], lin[chunk][:, :], ACT.Copy)\
                                .then_inc(hi_ready, 1)
                        elif chunk < 4:
                            if not early:
                                act.wait_ge(scores_ready, (g - 1) * SLOTS)
                            h = chunk - 2
                            nc.scalar.activation(qT[par][:, h, :], lin[h][:, :], ACT.Identity,
                                                 scale=-QSCALE, bias=q_bias[:, h:h + 1])\
                                .then_inc(proj_copied, 1)
                        else:
                            h = chunk - 4
                            nc.scalar.activation(kT[par][:, h, :], lin[h][:, :], ACT.Identity,
                                                 bias=k_bias[:, h:h + 1]).then_inc(proj_copied, 1)

                    def exponentials(g, slot, early):
                        pair, r = slot // ROUNDS, slot % ROUNDS
                        act.wait_ge(round_masked, g * SLOTS + slot + 1)
                        if not early:
                            act.wait_ge(shares_ready, g * SLOTS + slot - 1)
                        for j in range(PAIR):
                            for half in range(KH):
                                h = r + 4 * half
                                last = nc.scalar.activation(probs[pair][:, j, h, :], probs[pair][:, j, h, :],
                                                            ACT.Exp, scale=-1.0,
                                                            bias=least[pair][:, j, h:h + 1],
                                                            accum_out=sums[slot % 2][:, j, half:half + 1])
                        last.then_inc(exp_done, 1)

                    def copy_probs(g, unit, early):
                        act.wait_ge(pt_ready, g * SLOTS + unit + 1)
                        if not early:
                            act.wait_ge(pv_ready, g * SLOTS + unit - 1)
                        nc.scalar.activation(probsT[unit % 2][:, :], pt_bank[unit % 2][:, :], ACT.Copy)\
                            .then_inc(pt_copied, 1)

                    for chunk in range(6):
                        if chunk == 2:
                            act.wait_ge(col_biases_ready, 2)
                        project(0, 0, chunk, early=True)

                    def group(g, par, cur, prev, nxt):
                        for slot in range(SLOTS):
                            if prev and slot == 0:
                                exponentials(g - 1, SLOTS - 1, early=False)
                            if cur and slot > 0:
                                exponentials(g, slot - 1, early=not prev and slot < 3)
                            if nxt:
                                for chunk in chunks_at.get(slot, ()):
                                    if chunk < 6:
                                        project(g + 1, 1 - par, chunk, early=not prev)
                            if cur and not nxt and slot == 2:
                                act.wait_ge(proj_ready, GROUPS * 8)
                                mlp_split_high(act, 0)
                            if prev:
                                for unit in prev_units_at.get(slot, ()):
                                    copy_probs(g - 1, unit, early=False)
                            if cur:
                                for unit in cur_units_at.get(slot, ()):
                                    copy_probs(g, unit, early=not prev and unit < 2)

                    run(act, group)

                @block.vector
                def _(dve):
                    def norm_stats(g, par):
                        dve.wait_ge(x_loaded[par], loaded(g, par))
                        for j in range(G):
                            last = nc.vector.bn_stats(stats[:, j, :], xin[par][:, j, :])
                        last.then_inc(stats_ready, 1)
                        wait_apart(dve, stats_ready, g + 1, dve_waits)
                        for j in range(G):
                            last = nc.vector.bn_aggr(moments[:, j, :], stats[:, j, :])
                        last.then_inc(moments_ready, 1)

                    def normalise(g, par, early):
                        dve.wait_ge(rstd_ready, g + 1)
                        if not early:
                            dve.wait_ge(proj_ready, g * 8 - 6)
                        for j in range(G):
                            last = nc.vector.tensor_scalar(xn[:, j, :], xin[par][:, j, :],
                                                           moments[:, j, 0:1], rstd[:, j:j + 1],
                                                           ALU.subtract, ALU.mult)
                        last.then_inc(normed, 1)

                    def mask_round(g, par, slot, early):
                        pair, r = slot // ROUNDS, slot % ROUNDS
                        if slot == 0:
                            dve.wait_ge(bias_ready, g + 1)
                        if r == 0 and not early:
                            dve.wait_ge(pt_ready, (g - 1) * SLOTS + 4 * pair + 4)
                        wait_apart(dve, scores_ready, g * SLOTS + slot + 1, dve_waits)
                        for j in range(PAIR):
                            for half in range(KH):
                                h = r + 4 * half
                                last = nc.vector.tensor_tensor_reduce(
                                    out=probs[pair][:, j, h, :],
                                    in0=score_bank[slot % 2][:, (2 * j + half) * N:(2 * j + half + 1) * N],
                                    in1=bias[par][:, PAIR * pair + j, :], scale=1.0, scalar=LEAST_START,
                                    op0=ALU.add, op1=ALU.min, accum_out=least[pair][:, j, h:h + 1])
                        last.then_inc(round_masked, 1)

                    def values(g, par, p, early):
                        dve.wait_ge(proj_ready, g * 8 + 7 + p)
                        if p == 0 and not early:
                            dve.wait_ge(pv_ready, (g - 1) * SLOTS)
                        nc.vector.tensor_copy(
                            v[par][:, PAIR * p:PAIR * (p + 1), :].rearrange("p j f -> p (j f)"),
                            lin[p][:, :]).then_inc(v_copied, 1)

                    def residual(g, par):
                        nc.vector.tensor_tensor(
                            acts[:, bass.ds(g * GF, GF)].rearrange("p (j f) -> p j f", j=G),
                            xin[par][:, :, :], bo_folded[:, :].unsqueeze(1).broadcast_to([128, G, F]),
                            ALU.add).then_inc(resid_ready, 1)

                    def invert_sums(g, slot, early):
                        n = g * SLOTS + slot
                        if not early:
                            dve.wait_ge(normalised, n - 1)
                        dve.wait_ge(exp_done, n + 1)
                        nc.vector.reciprocal(shares[slot % 2][:, :, :], sums[slot % 2][:, :, :])\
                            .then_inc(shares_ready, 1)

                    def split_mlp_weights(parts):
                        for n in parts:
                            raw, (hi, lo), k = (w1_raw, w1_s, n) if n < KH else (w2_raw, w2_s, n - KH)
                            dve.wait_ge(mlp_loaded[0 if n < KH else 1], 16)
                            c = COLS["ln2_g"].start + k
                            gain = cols[:, c:c + 1] if n < KH else 1.0
                            nc.vector.tensor_scalar(hi[:, k, :], raw[:, k, :], gain, None, ALU.mult)\
                                .then_inc(mlp_hi_ready, 1)
                            dve.wait_ge(mlp_hi_ready, n + 1)
                            nc.vector.scalar_tensor_tensor(
                                out=lo[:, k, :], in0=raw[:, k, :], scalar=gain, in1=f32(hi[:, k, :]),
                                op0=ALU.mult, op1=ALU.subtract).then_inc(mlp_split, 1)

                    def take_attention(g, graph, early):
                        pair, j = graph // PAIR, graph % PAIR
                        n = g * G + graph
                        dve.wait_ge(pv_ready, n * 2 + 2)
                        if j == 0 and not early:
                            dve.wait_ge(wo_ready, g * 2 + pair - 1)
                        nc.vector.tensor_copy(attT[0][pair][:, j, :], pv_bank[:, 0:KH * N])\
                            .then_inc(att_hi_ready, 1)
                        dve.wait_ge(att_hi_ready, n + 1)
                        nc.vector.tensor_tensor(attT[1][pair][:, j, :], pv_bank[:, 0:KH * N],
                                                f32(attT[0][pair][:, j, :]), ALU.subtract)\
                            .then_inc(att_split, 1)

                    def add_output(g, pair):
                        dve.wait_ge(wo_ready, g * 2 + pair + 1)
                        if pair == 0:
                            dve.wait_ge(resid_ready, g + 1)
                        where = acts[:, bass.ds(g * GF + pair * PAIR * F, PAIR * F)]
                        nc.vector.tensor_tensor(where, wo_bank[:, :], where, ALU.add).then_inc(x1_added, 1)

                    def split_weight_parts(name):
                        done = KH * list(raws).index(name)
                        dve.wait_ge(w_loaded[name], 16)
                        hi, lo = splits[name]
                        for k in range(KH):
                            c = COLS["ln1_g"].start + k
                            gain = 1.0 if name == "wo" else cols[:, c:c + 1]
                            nc.vector.tensor_scalar(hi[:, k, :], raws[name][:, k, :], gain, None, ALU.mult)\
                                .then_inc(w_hi_ready, 1)
                        for k in range(KH):
                            c = COLS["ln1_g"].start + k
                            gain = 1.0 if name == "wo" else cols[:, c:c + 1]
                            dve.wait_ge(w_hi_ready, done + k + 1)
                            nc.vector.scalar_tensor_tensor(
                                out=lo[:, k, :], in0=raws[name][:, k, :], scalar=gain,
                                in1=f32(hi[:, k, :]), op0=ALU.mult, op1=ALU.subtract).then_inc(w_split, 1)

                    def fold_biases():
                        dve.wait_ge(folds_ready, 3)
                        nc.vector.tensor_tensor(k_bias[:, :], fold_bank[:, fold_at["wk"]:fold_at["wk"] + KH],
                                                cols[:, COLS["bk"]], ALU.add)
                        nc.vector.tensor_tensor(q_bias[:, :], fold_bank[:, fold_at["wq"]:fold_at["wq"] + KH],
                                                cols[:, COLS["bq"]], ALU.add).then_inc(col_biases_ready, 1)
                        nc.vector.tensor_tensor(cv[:, :], fold_bank[:, fold_at["wv"]:fold_at["wv"] + KH],
                                                cols[:, COLS["bv"]], ALU.add).then_inc(cv_ready, 1)
                        dve.wait_ge(col_biases_ready, 1)
                        nc.vector.tensor_scalar(q_bias[:, :], q_bias[:, :], -QSCALE, None, ALU.mult)\
                            .then_inc(col_biases_ready, 1)
                        dve.wait_ge(cv_ready, 1)
                        nc.vector.tensor_copy(cv_wide[:, :, :], cv[:, :].unsqueeze(2).broadcast_to([128, KH, 128]))\
                            .then_inc(cv_spread, 1)
                        nc.vector.tensor_scalar(hop_q_bias[:, :], cols[:, COLS["hop_bq"]], -1.0, None, ALU.mult)

                    norm_stats(0, 0)
                    dve.wait_ge(cols_loaded, 16)
                    split_weight_parts("wq")
                    normalise(0, 0, early=True)
                    split_weight_parts("wk")
                    split_low(dve, 0, hi_ready, lo_ready)
                    fold_biases()
                    split_weight_parts("wv")
                    split_weight_parts("wo")
                    dve.wait_ge(bo_product_ready, 1)
                    dve.wait_ge(rows_loaded, 16)
                    nc.vector.tensor_tensor(bo_folded[:, :], bo_bank[:, 0:F], row("bo"), ALU.add)\
                        .then_inc(bo_ready, 1)
                    values(0, 0, 0, early=True)
                    dve.wait_ge(bo_ready, 1)

                    def group(g, par, cur, prev, nxt):
                        for slot in range(SLOTS):
                            if prev and slot in (0, 1, 4, 5):
                                take_attention(g - 1, (0, 1, 4, 5).index(slot),
                                               early=isinstance(g, int) and g == 1)
                            if cur:
                                mask_round(g, par, slot, early=not prev)
                            if prev and slot == 0:
                                invert_sums(g - 1, SLOTS - 1, early=False)
                            if cur and slot > 0:
                                invert_sums(g, slot - 1, early=not prev and slot < 3)
                            if cur and not prev and slot == 0:
                                norm_stats(1, 1)
                            if nxt and slot == 1:
                                normalise(g + 1, 1 - par, early=False)
                            if cur and slot == 6 and two_more(g):
                                norm_stats(g + 2, par)
                            if nxt and slot == 6 and not two_more(g):
                                mlp_norm_stats(dve, 0)
                            if cur and not nxt and slot == 1:
                                dve.wait_ge(proj_ready, GROUPS * 8 - 6)
                                mlp_normalise(dve, 0)
                            if cur and slot == 0:
                                values(g, par, 1, early=isinstance(g, int) and g < 2)
                            if prev and slot in (2, 7):
                                add_output(g - 1, slot // 4)
                            if nxt and slot == 2:
                                split_low(dve, g + 1, hi_ready, lo_ready)
                            if cur and not nxt and slot == 2:
                                split_low(dve, 0, m_hi_ready, m_lo_ready)
                            if cur and slot == 3:
                                residual(g, par)
                            if nxt and slot == 7:
                                values(g + 1, 1 - par, 0, early=isinstance(g, int) and g < 1)
                            if cur and not prev and slot in (1, 2, 4, 5, 6):
                                split_mlp_weights({1: (0,), 2: (1,), 4: (2, 3, 4), 5: (5, 6), 6: (7, 8, 9)}[slot])
                            if cur and not prev and slot == 3:
                                dve.wait_ge(fold_ready, 1)
                                nc.vector.tensor_tensor(b1_folded[:, :], wo_bank[:, 0:MC], cols[:, COLS["b1"]],
                                                        ALU.add).then_inc(b1_ready, 1)

                    run(dve, group)

        def mlp_phase():
            s = ExitStack()
            with s:
                hid = [sb(s, f"hid{i}", [128, GN]) for i in range(RING)]
                hid_hi = [sb(s, f"hid_hi{i}", [128, GN], F32R) for i in range(RING)]
                hid_lo = [sb(s, f"hid_lo{i}", [128, GN], F32R) for i in range(RING)]
                raw = [sb(s, f"raw{i}", [128, KH, F]) for i in range(3)]
                acc = bank[6:8]

                raw_loaded = [sem(f"raw_loaded{i}") for i in range(3)]
                raw_hi_ready = sem("raw_hi_ready")
                raw_split = sem("raw_split")

                gelu_done = sem("gelu_done")
                hid_hi_ready = sem("hid_hi_ready")
                hid_split = sem("hid_split")

                def run(engine, group):
                    group(0, prev=False, nxt=True)
                    with engine.Fori(1, GROUPS - 1) as g:
                        group(g, prev=True, nxt=True)
                    group(GROUPS - 1, prev=True, nxt=False)

                def group_acts(g):
                    return acts[:, bass.ds(g * GF, GF)]

                block = s.enter_context(nc.Block())

                @block.sync
                def _(sp):
                    for i, w in enumerate((hwq, hwk, hwv)):
                        sp.dma_start(raw[i][:, :, :], w.rearrange("(k p) n -> p k n", p=128))\
                            .then_inc(raw_loaded[i], 16)

                @block.gpsimd
                def _(pool):
                    def group(g, prev, nxt):
                        pool.wait_ge(m_normed, g + 1)
                        where = group_acts(g).rearrange("p (j f) -> p j f", j=G)
                        nc.gpsimd.tensor_tensor(where, where, row("b2").unsqueeze(1).broadcast_to([128, G, F]),
                                                ALU.add).then_inc(b2_added, 1)
                        if nxt:
                            mlp_root(pool, g + 1)

                    run(pool, group)

                @block.tensor
                def _(pe):
                    hop_transpose = pe_project(pe, tr, xn, xnT, None, h_proj_ready)[0]

                    def up_chunk(g, m, early):
                        if m == 0:
                            pe.wait_ge(m_lo_ready, g * 2 + 2)
                        if not early:
                            pe.wait_ge(gelu_done, g * MC + m - RING + 1)
                        mlp_up(g, m)

                    def down_chunk(g, m, early):
                        pe.wait_ge(hid_split, g * MC + m + 1)
                        if m == 0 and not early:
                            pe.wait_ge(x2_added, g * 2)
                        r = m % RING
                        for j in range(G):
                            for n, (w, a) in enumerate(products(w2_s, (hid_hi[r], hid_lo[r]))):
                                last = nc.tensor.matmul(
                                    acc[j // 2][:, (j % 2) * F:(j % 2 + 1) * F], a[:, j * N:(j + 1) * N],
                                    w[:, m, :], start=(m == 0 and n == 0 and j % 2 == 0),
                                    stop=(m == MC - 1 and n == 2), skip_group_check=True)
                        last.then_inc(down_done, 1)

                    def group(g, prev, nxt):
                        for m in range(MC):
                            if prev or m >= 2:
                                up_chunk(g, m, early=not prev and m < RING)
                            if m >= 2:
                                down_chunk(g, m - 2, early=not prev)
                        if nxt:
                            mlp_transpose(pe, g + 1)
                        else:
                            pe.wait_ge(xs_ready, 1)
                            for half in range(KH):
                                hop_transpose(half)
                        for m in (MC - 2, MC - 1):
                            down_chunk(g, m, early=False)

                    run(pe, group)

                @block.scalar
                def _(act):
                    def group(g, prev, nxt):
                        for m in range(MC):
                            act.wait_ge(up_ready, g * MC + m + 1)
                            if prev or m >= RING:
                                act.wait_ge(hid_split, g * MC + m - RING + 1)
                            nc.scalar.activation(hid[m % RING][:, :], bank[m % RING][:, :], ACT.Gelu,
                                                 bias=b1_folded[:, m:m + 1]).then_inc(gelu_done, 1)
                        if nxt:
                            mlp_split_high(act, g + 1)
                        else:
                            for half in range(KH):
                                act.wait_ge(h_proj_ready, half + 1)
                                nc.scalar.activation(xnT[0][:, half, :], tr[half][:, :], ACT.Copy)\
                                    .then_inc(h_hi_ready, 1)

                    run(act, group)

                @block.vector
                def _(dve):
                    def split_hidden(g, m, early):
                        r = m % RING
                        dve.wait_ge(gelu_done, g * MC + m + 1)
                        if not early:
                            dve.wait_ge(down_done, g * MC + m - RING + 1)
                        nc.vector.tensor_copy(hid_hi[r][:, :], hid[r][:, :]).then_inc(hid_hi_ready, 1)
                        dve.wait_ge(hid_hi_ready, g * MC + m + 1)
                        nc.vector.tensor_tensor(hid_lo[r][:, :], hid[r][:, :], f32(hid_hi[r][:, :]),
                                                ALU.subtract).then_inc(hid_split, 1)

                    def group(g, prev, nxt):
                        for m in range(MC):
                            if prev and m == 0:
                                mlp_add_down(dve, g - 1)
                            split_hidden(g, m, early=not prev and m < RING)
                            if not prev and m >= MC - 3:
                                refill_weight(m - (MC - 3))
                            if nxt and m == 2:
                                mlp_norm_stats(dve, g + 1)
                            if nxt and m == 4:
                                dve.wait_ge(m_t_ready, g * 2 + 2)
                                mlp_normalise(dve, g + 1)
                            if not nxt and m == 4:
                                dve.wait_ge(m_t_ready, GROUPS * 2)
                                nc.vector.tensor_copy(xn[:, :, :].rearrange("p j f -> p (j f)"), acts[:, 0:GF])\
                                    .then_inc(xs_ready, 1)
                        if nxt:
                            split_low(dve, g + 1, m_hi_ready, m_lo_ready)
                        else:
                            split_low(dve, 0, h_hi_ready, h_lo_ready)

                    def refill_weight(i):
                        hi, lo = (wq_s, wk_s, wv_s)[i]
                        dve.wait_ge(raw_loaded[i], 16)
                        nc.vector.tensor_copy(hi[:, :, :], raw[i][:, :, :]).then_inc(raw_hi_ready, 1)
                        dve.wait_ge(raw_hi_ready, i + 1)
                        nc.vector.tensor_tensor(lo[:, :, :], raw[i][:, :, :], f32(hi[:, :, :]),
                                                ALU.subtract).then_inc(raw_split, 1)

                    run(dve, group)

        def hop_phase():
            s = ExitStack()
            with s:
                adj_sb = [sb(s, f"h_adj_sb{i}", [128, G, N], I32) for i in range(2)]
                keep = [sb(s, f"keep{i}", [128, G, N]) for i in range(2)]
                fill = [sb(s, f"fill{i}", [128, G, N]) for i in range(2)]
                xs = [xn, sb(s, "xs1", [128, G, F])]
                xsT = xnT
                qT = [sb(s, f"h_qT{i}", [128, KH, GN]) for i in range(2)]
                kT = [sb(s, f"h_kT{i}", [128, KH, GN]) for i in range(2)]
                z0 = [sb(s, f"z0{i}", [128, G, F]) for i in range(2)]
                z0_part = [sb(s, f"z0_part{i}", [128, G, F]) for i in range(2)]
                resid = [sb(s, f"resid{i}", [128, G, F]) for i in range(2)]
                probs = [sb(s, f"h_probs{i}", [128, PAIR, H, N]) for i in range(2)]
                least = [sb(s, f"h_least{i}", [128, PAIR * H]) for i in range(2)]
                sums = [sb(s, f"h_sums{i}", [128, PAIR, KH]) for i in range(2)]
                shares = [sb(s, f"shares{i}", [128, PAIR, KH]) for i in range(2)]
                probsT = [sb(s, f"h_probsT{i}", [128, 4, 4 * N]) for i in range(2)]
                zT = sb(s, "zT", [128, PAIR, KH * N])
                z = sb(s, "z", [128, PAIR, F])
                y = [sb(s, f"y{i}", [128, PAIR, F]) for i in range(2)]
                score_bank, pt_bank, lin = bank[0:2], bank[2:4], bank[4:6]
                fwd_bank, back_bank = bank[6], bank[7]

                dve_waits = sem("h_dve_waits")
                pool_waits = sem("h_pool_waits")
                adj_loaded = [sem(f"h_adj_loaded{i}") for i in range(2)]
                fill_ready = sem("fill_ready")
                mask_ready = sem("mask_ready")
                z0_part_ready = sem("z0_part_ready")
                resid_ready = sem("h_resid_ready")
                proj_ready, hi_ready, lo_ready = h_proj_ready, h_hi_ready, h_lo_ready
                proj_copied = sem("h_proj_copied")
                z0_ready = sem("z0_ready")
                scores_ready = sem("h_scores_ready")
                round_kept = sem("round_kept")
                round_masked = sem("h_round_masked")
                exp_done = sem("h_exp_done")
                pt_ready = sem("h_pt_ready")
                pt_copied = sem("h_pt_copied")
                shares_ready = sem("shares_ready")
                normalised = sem("normalised")
                fwd_ready = sem("fwd_ready")
                zT_copied = sem("zT_copied")
                back_ready = sem("back_ready")
                z_ready = sem("z_ready")
                stats_ready = sem("h_stats_ready")
                moments_ready = sem("h_moments_ready")
                var_ready = sem("h_var_ready")
                rstd_ready = sem("h_rstd_ready")
                centred = sem("centred")
                y_ready = sem("y_ready")
                lane_zT = qT[0][:, 0, :].rearrange("p (j n) -> p j n", j=PAIR)
                lane_z = qT[0][:, 1, :].rearrange("p (j f) -> p j f", j=PAIR)
                lane_fwd, lane_back_bank = score_bank
                lane_fwd_ready = sem("lane_fwd_ready")
                lane_zT_copied = sem("lane_zT_copied")
                lane_back_ready = sem("lane_back_ready")
                lane_z_ready = sem("lane_z_ready")
                last = GROUPS - 1
                y_free = [sem(f"y_free{i}") for i in range(2)]

                def loaded(g, par):
                    return g * 8 + (8 if par else 16)

                def run(engine, group, drain):
                    group(0, 0, cur=True, prev=False, nxt=True, tail=False)
                    group(1, 1, cur=True, prev=True, nxt=True, tail=False)
                    with engine.Fori(1, GROUPS // 2 - 1) as i:
                        group(i * 2, 0, cur=True, prev=True, nxt=True, tail=True)
                        group(i * 2 + 1, 1, cur=True, prev=True, nxt=True, tail=True)
                    group(GROUPS - 2, 0, cur=True, prev=True, nxt=True, tail=True)
                    group(GROUPS - 1, 1, cur=True, prev=True, nxt=False, tail=True)
                    drain()

                chunks_at = {1: (0, 1), 2: (2,), 3: (3,), 4: (4,), 5: (5,), 6: (6,)}
                prev_units_at = {1: (4,), 2: (5,), 3: (6, 7)}
                cur_units_at = {6: (0, 1), 7: (2, 3)}

                def hop_number(g, pair, hop):
                    return g * 2 * HOPS + pair * HOPS + hop

                block = s.enter_context(nc.Block())

                @block.sync
                def _(sp):
                    def load(g, par):
                        sp.dma_start(adj_sb[par][:, :, :], adj[g, :, :, :]).then_inc(adj_loaded[par], 16)

                    def store(g, pair):
                        sp.wait_ge(y_ready, g * 2 + pair + 1)
                        sp.dma_start(out[g, :, PAIR * pair:PAIR * (pair + 1), :], y[pair][:, :, :])\
                            .then_inc(y_free[pair], 16)

                    load(0, 0)
                    load(1, 1)
                    for pair in range(2):
                        sp.sem_inc(y_free[pair], 16)

                    def group(g, par, more):
                        if more:
                            sp.wait_ge(mask_ready, g + 1)
                            load(g + 2, par)
                        for pair in range(2):
                            store(g, pair)

                    with sp.Fori(0, GROUPS // 2 - 1) as i:
                        group(i * 2, 0, True)
                        group(i * 2 + 1, 1, True)
                    group(GROUPS - 2, 0, False)
                    group(GROUPS - 1, 1, False)
                    for pair in range(2):
                        sp.wait_ge(y_free[pair], 16 * (GROUPS + 1))

                @block.gpsimd
                def _(pool):
                    def mask(g, par, early):
                        if not early:
                            pool.wait_ge(round_masked, (g - 1) * SLOTS)
                        wait_apart(pool, adj_loaded[par], loaded(g, par), pool_waits)
                        nc.gpsimd.tensor_scalar(fill[par][:, :, :], adj_sb[par][:, :, :], 0.0, HOP_MASK,
                                                ALU.is_equal, ALU.mult).then_inc(fill_ready, 1)
                        wait_apart(pool, fill_ready, g + 1, pool_waits)
                        nc.gpsimd.tensor_scalar(keep[par][:, :, :], fill[par][:, :, :], -1.0 / HOP_MASK, 1.0,
                                                ALU.mult, ALU.add).then_inc(mask_ready, 1)

                    def z_parts(g, par, early):
                        if not early:
                            pool.wait_ge(z_ready, (g - 1) * 2 * HOPS)
                        wait_apart(pool, z0_ready, g * 2 + 2, pool_waits)
                        nc.gpsimd.tensor_scalar(z0_part[par][:, :, :], z0[par][:, :, :], ALPHA, None, ALU.mult)\
                            .then_inc(z0_part_ready, 1)

                    def residual(g, par):
                        pool.wait_ge(z0_part_ready, g + 1)
                        pool.wait_ge(xs_ready, g + 1)
                        nc.gpsimd.tensor_tensor(resid[par][:, :, :], xs[par][:, :, :], z0_part[par][:, :, :],
                                                ALU.add).then_inc(resid_ready, 1)

                    def normalise_round(g, slot):
                        n = g * SLOTS + slot
                        pair, r = slot // ROUNDS, slot % ROUNDS
                        pool.wait_ge(shares_ready, n + 1)
                        part = probs[pair][:, :, r:H:4, :]
                        nc.gpsimd.tensor_tensor(
                            part, part, shares[slot % 2][:, :, :].unsqueeze(3)
                            .broadcast_to([128, PAIR, KH, N]), ALU.mult).then_inc(normalised, 1)

                    def root(n):
                        wait_apart(pool, moments_ready, n + 1, pool_waits)
                        nc.gpsimd.tensor_scalar(var_eps[:, 0:PAIR], moments[:, 0:PAIR, 1], EPS, None, ALU.add)\
                            .then_inc(var_ready, 1)
                        pool.wait_ge(var_ready, n + 1)
                        nc.gpsimd.tensor_tensor(rstd[:, 0:PAIR], var_eps[:, 0:PAIR], neg_half[:, 0:PAIR], ALU.pow)\
                            .then_inc(rstd_ready, 1)

                    mask(0, 0, early=True)

                    def group(g, par, cur, prev, nxt, tail):
                        for slot in range(SLOTS):
                            if prev and slot == 0:
                                normalise_round(g - 1, SLOTS - 1)
                            if cur and slot > 0:
                                normalise_round(g, slot - 1)
                            if cur and slot == 1:
                                z_parts(g, par, early=isinstance(g, int) and g < 2)
                            if tail and slot == 2:
                                root((g - 2) * 2 + 1)
                            if cur and slot == 2:
                                residual(g, par)
                            if nxt and slot == 5:
                                mask(g + 1, 1 - par, early=not prev)
                            if prev and slot == 5:
                                root((g - 1) * 2)

                    def drain():
                        normalise_round(last, SLOTS - 1)
                        for n in (last * 2 - 1, last * 2, last * 2 + 1):
                            root(n)

                    run(pool, group, drain)

                @block.tensor
                def _(pe):
                    def project(g, par, chunk, first=False):
                        transpose, feature_major, node_major = pe_project(
                            pe, lin, xs[par], xsT, {"q": wq_s, "k": wk_s, "v": wv_s}, proj_ready)
                        if chunk == 0:
                            pe.wait_ge(xs_ready, g + 1)
                            if not first:
                                pe.wait_ge(z0_ready, g * 2 - 1)
                            transpose(0)
                        elif chunk == 1:
                            if not first:
                                pe.wait_ge(z0_ready, g * 2)
                            transpose(1)
                        elif chunk in (2, 3):
                            pe.wait_ge(lo_ready, g * 2 + 2)
                            feature_major("q", chunk - 2)
                        elif chunk in (4, 5):
                            pe.wait_ge(proj_copied, g * 4 + chunk - 3)
                            feature_major("k", chunk - 4)
                        else:
                            pe.wait_ge(proj_copied, g * 4 + chunk - 3)
                            node_major("v", chunk - 6)

                    def scores(g, par, slot, early):
                        if slot == 0:
                            pe.wait_ge(proj_copied, g * 4 + 4)
                        if not early:
                            pe.wait_ge(round_kept, g * SLOTS + slot - 1)
                        score_round(score_bank[slot % 2], qT[par], kT[par], slot // ROUNDS, slot % ROUNDS)\
                            .then_inc(scores_ready, 1)

                    def transpose_probs(g, unit, early):
                        graph, half = unit // 2, unit % 2
                        pair = graph // PAIR
                        if unit % 4 == 0:
                            pe.wait_ge(normalised, g * SLOTS + ROUNDS * pair + ROUNDS)
                        if not early:
                            pe.wait_ge(pt_copied, g * SLOTS + unit - 1)
                        for c in range(4):
                            last = nc.tensor.transpose(pt_bank[unit % 2][:, c * N:(c + 1) * N],
                                                       probs[pair][:, graph % PAIR, 4 * half + c, :], ident[:, :])
                        last.then_inc(pt_ready, 1)

                    def forward_products(to, z_, pair):
                        for j in range(PAIR):
                            for half in range(KH):
                                for c in range(4):
                                    h = 4 * half + c
                                    product = nc.tensor.matmul(
                                        to[D * c:D * (c + 1), (2 * j + half) * N:(2 * j + half + 1) * N],
                                        z_[:, j, h * D:(h + 1) * D],
                                        probsT[pair][:, 2 * j + half, c * N:(c + 1) * N],
                                        start=True, stop=True, tile_position=(0, D * c))
                        return product

                    def back_transposes(to, zT_):
                        for j in range(PAIR):
                            for half in range(KH):
                                transpose = nc.tensor.transpose(
                                    to[:, j * F + half * 128:j * F + (half + 1) * 128],
                                    zT_[:, j, half * N:(half + 1) * N], ident[:, :])
                        return transpose

                    def forward(g, par, pair, hop, early):
                        n = hop_number(g, pair, hop)
                        if hop == 0:
                            pe.wait_ge(pt_copied, g * SLOTS + 4 * pair + 4)
                            pe.wait_ge(z0_ready, g * 2 + 2)
                            if early:
                                pe.wait_ge(x2_added, GROUPS * 2)
                            else:
                                pe.wait_ge(zT_copied, n)
                        else:
                            pe.wait_ge(z_ready, n)
                        forward_products(fwd_bank, z if hop else z0[par][:, PAIR * pair:PAIR * (pair + 1), :],
                                         pair).then_inc(fwd_ready, 1)

                    def back(g, pair, hop, early):
                        n = hop_number(g, pair, hop)
                        pe.wait_ge(zT_copied, n + 1)
                        if hop == 0 and not early:
                            pe.wait_ge(z_ready, n)
                        back_transposes(back_bank, zT).then_inc(back_ready, 1)

                    for chunk in range(2, 7):
                        project(0, 0, chunk, first=True)

                    def group(g, par, cur, prev, nxt, tail):
                        first = isinstance(g, int) and g == 1
                        for slot in range(SLOTS):
                            if cur:
                                scores(g, par, slot, early=not prev and slot < 2)
                            if tail and slot == 0:
                                back(g - 2, 1, HOPS - 1, early=False)
                            if prev and slot > 0:
                                back(g - 1, (slot - 1) // HOPS, (slot - 1) % HOPS, early=first and slot == 1)
                            if cur and slot == 0:
                                project(g, par, 7)
                            if nxt:
                                for chunk in chunks_at.get(slot, ()):
                                    project(g + 1, 1 - par, chunk)
                            if prev:
                                for unit in prev_units_at.get(slot, ()):
                                    transpose_probs(g - 1, unit, early=False)
                            if cur:
                                for unit in cur_units_at.get(slot, ()):
                                    transpose_probs(g, unit, early=not prev and unit < 2)
                            if prev:
                                forward(g - 1, 1 - par, slot // HOPS, slot % HOPS, early=first and slot == 0)

                    def lane_forward(hop):
                        if hop == 0:
                            pe.wait_ge(pt_copied, GROUPS * SLOTS)
                            pe.wait_ge(round_kept, GROUPS * SLOTS)
                        else:
                            pe.wait_ge(lane_z_ready, hop)
                        forward_products(lane_fwd, lane_z if hop else z0[1][:, PAIR:2 * PAIR, :], 1)\
                            .then_inc(lane_fwd_ready, 1)

                    def lane_back(hop):
                        pe.wait_ge(lane_zT_copied, hop + 1)
                        back_transposes(lane_back_bank, lane_zT).then_inc(lane_back_ready, 1)

                    def drain():
                        back(last - 1, 1, HOPS - 1, early=False)
                        forward(last, 1, 0, 0, early=False)
                        back(last, 0, 0, early=False)
                        forward(last, 1, 0, 1, early=False)
                        transpose_probs(last, 4, early=False)
                        transpose_probs(last, 5, early=False)
                        back(last, 0, 1, early=False)
                        transpose_probs(last, 6, early=False)
                        transpose_probs(last, 7, early=False)
                        forward(last, 1, 0, 2, early=False)
                        lane_forward(0)
                        back(last, 0, 2, early=False)
                        forward(last, 1, 0, 3, early=False)
                        lane_back(0)
                        lane_forward(1)
                        back(last, 0, 3, early=False)
                        lane_back(1)
                        for hop in range(2, HOPS):
                            lane_forward(hop)
                            lane_back(hop)

                    run(pe, group, drain)

                @block.scalar
                def _(act):
                    def project(g, par, chunk, early):
                        act.wait_ge(proj_ready, g * 8 + chunk + 1)
                        if chunk < 2:
                            nc.scalar.activation(xsT[0][:, chunk, :], lin[chunk][:, :], ACT.Copy)\
                                .then_inc(hi_ready, 1)
                        elif chunk < 4:
                            if not early:
                                act.wait_ge(scores_ready, (g - 1) * SLOTS)
                            h = chunk - 2
                            nc.scalar.activation(qT[par][:, h, :], lin[h][:, :], ACT.Identity, scale=-1.0,
                                                 bias=hop_q_bias[:, h:h + 1]).then_inc(proj_copied, 1)
                        else:
                            h = chunk - 4
                            c = COLS["hop_bk"].start + h
                            nc.scalar.activation(kT[par][:, h, :], lin[h][:, :], ACT.Identity,
                                                 bias=cols[:, c:c + 1]).then_inc(proj_copied, 1)

                    def exponentials(g, slot, early):
                        pair, r = slot // ROUNDS, slot % ROUNDS
                        act.wait_ge(round_masked, g * SLOTS + slot + 1)
                        if not early:
                            act.wait_ge(shares_ready, g * SLOTS + slot - 1)
                        for j in range(PAIR):
                            for half in range(KH):
                                h = r + 4 * half
                                last = nc.scalar.activation(
                                    probs[pair][:, j, h, :], probs[pair][:, j, h, :], ACT.Exp, scale=-1.0,
                                    bias=least[pair][:, j * H + h:j * H + h + 1],
                                    accum_out=sums[slot % 2][:, j, half:half + 1])
                        last.then_inc(exp_done, 1)

                    def copy_probs(g, unit, early):
                        pair = unit // 4
                        act.wait_ge(pt_ready, g * SLOTS + unit + 1)
                        if unit % 4 == 0 and not early:
                            act.wait_ge(fwd_ready, (g - 1) * 2 * HOPS + (pair + 1) * HOPS)
                        nc.scalar.activation(probsT[pair][:, unit % 4, :], pt_bank[unit % 2][:, :], ACT.Copy)\
                            .then_inc(pt_copied, 1)

                    def copy_hop(g, pair, hop, early):
                        n = hop_number(g, pair, hop)
                        act.wait_ge(fwd_ready, n + 1)
                        if not early:
                            act.wait_ge(back_ready, n)
                        nc.scalar.activation(zT[:, :, :].rearrange("p j n -> p (j n)"), fwd_bank[:, :], ACT.Copy,
                                             scale=1.0 - ALPHA)\
                            .then_inc(zT_copied, 1)

                    for chunk in range(2, 6):
                        project(0, 0, chunk, early=True)

                    def group(g, par, cur, prev, nxt, tail):
                        for slot in range(SLOTS):
                            if tail and slot == 0:
                                copy_hop(g - 2, 1, HOPS - 1, early=False)
                            if prev and slot > 0:
                                copy_hop(g - 1, (slot - 1) // HOPS, (slot - 1) % HOPS,
                                         early=isinstance(g, int) and g == 1 and slot == 1)
                            if prev and slot == 0:
                                exponentials(g - 1, SLOTS - 1, early=False)
                            if cur and slot > 0:
                                exponentials(g, slot - 1, early=not prev and slot < 3)
                            if nxt:
                                for chunk in chunks_at.get(slot, ()):
                                    if chunk < 6:
                                        project(g + 1, 1 - par, chunk, early=not prev)
                            if prev:
                                for unit in prev_units_at.get(slot, ()):
                                    copy_probs(g - 1, unit, early=isinstance(g, int) and g == 1)
                            if cur:
                                for unit in cur_units_at.get(slot, ()):
                                    copy_probs(g, unit, early=not prev)

                    def lane_copy_hop(hop):
                        act.wait_ge(lane_fwd_ready, hop + 1)
                        if hop:
                            act.wait_ge(lane_back_ready, hop)
                        nc.scalar.activation(qT[0][:, 0, :], lane_fwd[:, :], ACT.Copy, scale=1.0 - ALPHA)\
                            .then_inc(lane_zT_copied, 1)

                    def drain():
                        copy_hop(last - 1, 1, HOPS - 1, early=False)
                        exponentials(last, SLOTS - 1, early=False)
                        copy_hop(last, 0, 0, early=False)
                        copy_hop(last, 0, 1, early=False)
                        for unit in range(4, 8):
                            copy_probs(last, unit, early=False)
                        copy_hop(last, 0, 2, early=False)
                        lane_copy_hop(0)
                        copy_hop(last, 0, 3, early=False)
                        for hop in range(1, HOPS):
                            lane_copy_hop(hop)

                    run(act, group, drain)

                @block.vector
                def _(dve):
                    def values(g, par, p, early):
                        dve.wait_ge(proj_ready, g * 8 + 7 + p)
                        if p == 0 and not early:
                            dve.wait_ge(z0_part_ready, g - 1)
                        nc.vector.tensor_tensor(
                            z0[par][:, PAIR * p:PAIR * (p + 1), :],
                            lin[p][:, :].rearrange("p (j f) -> p j f", j=PAIR),
                            row("hop_bv").unsqueeze(1).broadcast_to([128, PAIR, F]), ALU.add)\
                            .then_inc(z0_ready, 1)

                    def keep_round(g, par, slot, early):
                        pair, r = slot // ROUNDS, slot % ROUNDS
                        if slot == 0:
                            dve.wait_ge(mask_ready, g + 1)
                        if r == 0 and not early:
                            dve.wait_ge(pt_ready, (g - 1) * SLOTS + 4 * pair + 4)
                        dve.wait_ge(scores_ready, g * SLOTS + slot + 1)
                        nc.vector.tensor_tensor(
                            probs[pair][:, :, r:H:4, :],
                            score_bank[slot % 2][:, :].rearrange("p (j h n) -> p j h n", j=PAIR, h=KH),
                            keep[par][:, PAIR * pair:PAIR * (pair + 1), :].unsqueeze(2)
                            .broadcast_to([128, PAIR, KH, N]), ALU.mult).then_inc(round_kept, 1)

                    def mask_round(g, par, slot):
                        pair, r = slot // ROUNDS, slot % ROUNDS
                        wait_apart(dve, round_kept, g * SLOTS + slot + 1, dve_waits)
                        for j in range(PAIR):
                            for h in (r, r + 4):
                                last = nc.vector.tensor_tensor_reduce(
                                    out=probs[pair][:, j, h, :], in0=probs[pair][:, j, h, :],
                                    in1=fill[par][:, PAIR * pair + j, :], scale=1.0, scalar=LEAST_START,
                                    op0=ALU.add, op1=ALU.min,
                                    accum_out=least[pair][:, j * H + h:j * H + h + 1])
                        last.then_inc(round_masked, 1)

                    def invert_sums(g, slot, early):
                        n = g * SLOTS + slot
                        if not early:
                            dve.wait_ge(normalised, n - 1)
                        dve.wait_ge(exp_done, n + 1)
                        nc.vector.reciprocal(shares[slot % 2][:, :, :], sums[slot % 2][:, :, :])\
                            .then_inc(shares_ready, 1)

                    def take_hop(g, par, pair, hop):
                        last_hop = hop == HOPS - 1
                        if last_hop:
                            dve.wait_ge(resid_ready, g + 1)
                            dve.wait_ge(y_free[pair], g * 16 + 16)
                        elif hop == 0:
                            dve.wait_ge(z0_part_ready, g + 1)
                        dve.wait_ge(back_ready, hop_number(g, pair, hop) + 1)
                        to = y[pair] if last_hop else z
                        part = resid[par] if last_hop else z0_part[par]
                        nc.vector.tensor_tensor(to[:, :, :], back_bank[:, :].rearrange("p (j f) -> p j f", j=PAIR),
                                                part[:, PAIR * pair:PAIR * (pair + 1), :], ALU.add)\
                            .then_inc(z_ready, 1)

                    def final_stats(g, pair, in_lane=False):
                        n = g * 2 + pair
                        if in_lane:
                            dve.wait_ge(lane_z_ready, HOPS)
                        else:
                            dve.wait_ge(z_ready, (n + 1) * HOPS)
                        for j in range(PAIR):
                            last = nc.vector.bn_stats(stats[:, j, :], y[pair][:, j, :])
                        last.then_inc(stats_ready, 1)
                        wait_apart(dve, stats_ready, n + 1, dve_waits)
                        for j in range(PAIR):
                            last = nc.vector.bn_aggr(moments[:, j, :], stats[:, j, :])
                        last.then_inc(moments_ready, 1)

                    def final_centre(g, pair):
                        n = g * 2 + pair
                        dve.wait_ge(rstd_ready, n + 1)
                        for j in range(PAIR):
                            last = nc.vector.scalar_tensor_tensor(
                                out=y[pair][:, j, :], in0=y[pair][:, j, :], scalar=moments[:, j, 0:1],
                                in1=row("gamma"), op0=ALU.subtract, op1=ALU.mult)
                        last.then_inc(centred, 1)

                    def final_scale(g, pair):
                        n = g * 2 + pair
                        dve.wait_ge(centred, n + 1)
                        for j in range(PAIR):
                            last = nc.vector.scalar_tensor_tensor(
                                out=y[pair][:, j, :], in0=y[pair][:, j, :], scalar=rstd[:, j:j + 1],
                                in1=row("beta"), op0=ALU.mult, op1=ALU.add)
                        last.then_inc(y_ready, 1)

                    def final_norm(g, pair):
                        final_centre(g, pair)
                        final_scale(g, pair)

                    def copy_x(g, par, early):
                        if not early:
                            dve.wait_ge(resid_ready, g - 1)
                            dve.wait_ge(proj_ready, g * 8 - 14)
                        nc.vector.tensor_copy(xs[par][:, :, :].rearrange("p j f -> p (j f)"),
                                              acts[:, bass.ds(g * GF, GF)]).then_inc(xs_ready, 1)


                    copy_x(1, 1, early=True)
                    mlp_add_down(dve, GROUPS - 1)
                    values(0, 0, 0, early=True)

                    def group(g, par, cur, prev, nxt, tail):
                        early = isinstance(g, int) and g < 2
                        for slot in range(SLOTS):
                            if cur:
                                keep_round(g, par, slot, early=not prev)
                            if tail and slot == 0:
                                take_hop(g - 2, par, 1, HOPS - 1)
                            if prev and slot > 0:
                                take_hop(g - 1, 1 - par, (slot - 1) // HOPS, (slot - 1) % HOPS)
                            if cur:
                                mask_round(g, par, slot)
                            if prev and slot == 0:
                                invert_sums(g - 1, SLOTS - 1, early=False)
                            if cur and slot > 0:
                                invert_sums(g, slot - 1, early=not prev and slot < 3)
                            if nxt and prev and slot == 0:
                                copy_x(g + 1, 1 - par, early=early)
                            if cur and slot == 0:
                                values(g, par, 1, early=early)
                            if nxt and slot == 1:
                                split_low(dve, g + 1, hi_ready, lo_ready)
                            if tail and slot == 2:
                                final_stats(g - 2, 1)
                            if tail and slot == 3:
                                final_centre(g - 2, 1)
                            if tail and slot == 4:
                                final_scale(g - 2, 1)
                            if prev and slot == 5:
                                final_stats(g - 1, 0)
                            if nxt and slot == 6:
                                values(g + 1, 1 - par, 0, early=early)
                            if prev and slot == 7:
                                final_norm(g - 1, 0)

                    def lane_take_hop(hop):
                        last_hop = hop == HOPS - 1
                        if last_hop:
                            dve.wait_ge(y_free[1], last * 16 + 16)
                        dve.wait_ge(lane_back_ready, hop + 1)
                        part = resid[1] if last_hop else z0_part[1]
                        nc.vector.tensor_tensor(y[1][:, :, :] if last_hop else lane_z,
                                                lane_back_bank[:, :].rearrange("p (j f) -> p j f", j=PAIR),
                                                part[:, PAIR:2 * PAIR, :], ALU.add).then_inc(lane_z_ready, 1)

                    def drain():
                        take_hop(last - 1, 0, 1, HOPS - 1)
                        invert_sums(last, SLOTS - 1, early=False)
                        take_hop(last, 1, 0, 0)
                        final_stats(last - 1, 1)
                        take_hop(last, 1, 0, 1)
                        final_norm(last - 1, 1)
                        take_hop(last, 1, 0, 2)
                        lane_take_hop(0)
                        take_hop(last, 1, 0, 3)
                        lane_take_hop(1)
                        final_stats(last, 0)
                        lane_take_hop(2)
                        final_norm(last, 0)
                        lane_take_hop(3)
                        final_stats(last, 1, in_lane=True)
                        final_norm(last, 1)

                    run(dve, group, drain)

        with mlp_stack:
            with att_stack:
                attention_phase()
            mlp_phase()
        hop_phase()


def kernel(x, adj, L0_gnn_ln1_g, L0_gnn_ln1_b, L0_gnn_ln2_g, L0_gnn_ln2_b, L0_gnn_wq, L0_gnn_bq, L0_gnn_wk,
           L0_gnn_bk, L0_gnn_wv, L0_gnn_bv, L0_gnn_wo, L0_gnn_bo, L0_gnn_w1, L0_gnn_b1, L0_gnn_w2, L0_gnn_b2,
           L1_gnn_Wq, L1_gnn_bq, L1_gnn_Wk, L1_gnn_bk, L1_gnn_Wv, L1_gnn_bv, L1_gnn_gamma, L1_gnn_beta):
    import numpy as np
    import concourse.bacc as bacc
    from concourse.bass_utils import run_bass_kernel_spmd

    def by_group(a):
        a = np.asarray(a)
        return np.ascontiguousarray(a.reshape(GROUPS, G, N, a.shape[2]).transpose(0, 2, 1, 3))

    def columns(*vectors):
        return np.ascontiguousarray(np.concatenate([np.asarray(a).reshape(-1, 128) for a in vectors]).T)

    arrays = {
        "x_in": by_group(x),
        "adj_in": by_group(adj),
        "vec_cols": columns(L0_gnn_ln1_g, L0_gnn_ln1_b, L0_gnn_ln2_g, L0_gnn_ln2_b, L0_gnn_bq, L0_gnn_bk,
                            L0_gnn_bv, L0_gnn_b1, L1_gnn_bq, L1_gnn_bk),
        "vec_rows": np.concatenate([np.asarray(a).reshape(1, -1) for a in
                                    (L0_gnn_bo, L0_gnn_b2, L1_gnn_bv, L1_gnn_gamma, L1_gnn_beta)], axis=1),
        "wq": np.asarray(L0_gnn_wq), "wk": np.asarray(L0_gnn_wk), "wv": np.asarray(L0_gnn_wv),
        "wo": np.asarray(L0_gnn_wo), "w1": np.asarray(L0_gnn_w1), "w2": np.asarray(L0_gnn_w2),
        "hwq": np.ascontiguousarray(np.asarray(L1_gnn_Wq).T),
        "hwk": np.ascontiguousarray(np.asarray(L1_gnn_Wk).T),
        "hwv": np.ascontiguousarray(np.asarray(L1_gnn_Wv).T),
    }
    nc = bacc.Bacc("TRN2", target_bir_lowering=False, num_devices=1)
    aps = [nc.dram_tensor(n, a.shape, mybir.dt.from_np(a.dtype), kind="ExternalInput").ap()
           for n, a in arrays.items()]
    out = nc.dram_tensor("out", (GROUPS, N, G, F), F32, kind="ExternalOutput").ap()
    graph_transformer(nc, *aps, out)
    r = run_bass_kernel_spmd(nc, [arrays], core_ids=[0])
    got = r.results[0]["out"]
    return np.ascontiguousarray(got.transpose(0, 2, 1, 3)).reshape(B, N, F)
```
